# Optimizing a Trainium2 kernel written in Bass

```python
import numpy as np
import jax
import jax.numpy as jnp

def _softmax(x, axis=-1):
    return jax.nn.softmax(x, axis=axis)

def _gelu(x):
    return jax.nn.gelu(x, approximate=True)

def _silu(x):
    return jax.nn.silu(x)

def _sigmoid(x):
    return jax.nn.sigmoid(x)

def _layernorm(x, axis=-1, eps=1e-05):
    m = jnp.mean(x, axis=axis, keepdims=True)
    v = jnp.var(x, axis=axis, keepdims=True)
    return (x - m) / jnp.sqrt(v + eps)

def _scatter_add(tgt, idx, src, axis=0):
    return tgt.at[idx].add(src)

def _segment_sum(src, seg, n):
    return jax.ops.segment_sum(src, seg, n)
kernel_name = 'mk_lm_tower_d2_tok_ids256_r4_c89d5e'

def setup_inputs(seed: int=0):
    np.random.seed(seed)
    _w = jnp.asarray

    def _rec_inputs():
        import jax
        import jax.numpy as jnp
        _rk = jax.random.key(seed)
        x = jax.random.randint(jax.random.fold_in(_rk, 1), (128, 128), 0, 24991, jnp.int32)
        return x
    x = _rec_inputs()

    def _L0_tok_setup():
        import jax, jax.numpy as jnp
        import numpy as np
        VOCAB = 25000
        DIM_SRC = 75
        DIM_PROJ = 64
        key = jax.random.key(seed)
        ks = jax.random.split(key, 8)
        B, S = (32, 128)
        batch = jax.random.randint(ks[0], (B, S), 0, VOCAB, dtype=jnp.int64)
        embed_table = jax.random.normal(ks[1], (VOCAB, 2 * DIM_SRC), dtype=jnp.float32)
        W1 = jax.random.normal(ks[2], (DIM_SRC, DIM_PROJ), dtype=jnp.float32) * 0.05
        b1 = jax.random.normal(ks[3], (DIM_PROJ,), dtype=jnp.float32) * 0.05
        W2 = jax.random.normal(ks[4], (DIM_SRC, DIM_PROJ), dtype=jnp.float32) * 0.05
        b2 = jax.random.normal(ks[5], (DIM_PROJ,), dtype=jnp.float32) * 0.05
        Wa = jax.random.normal(ks[6], (DIM_PROJ, 1), dtype=jnp.float32) * 0.05
        ba = jax.random.normal(ks[7], (1,), dtype=jnp.float32) * 0.05
        return {'batch': batch, 'embed_table': embed_table, 'W1': W1, 'b1': b1, 'W2': W2, 'b2': b2, 'Wa': Wa, 'ba': ba}
    _L0_tok_all = _L0_tok_setup()
    _L0_tok_in = {k: v for k, v in _L0_tok_all.items() if k in ('embed_table', 'W1', 'b1', 'W2', 'b2', 'Wa', 'ba')}
    del _L0_tok_all

    def _L0_attn_setup():
        import jax, jax.numpy as jnp
        import numpy as np
        import math
        B, S, D = (4, 1024, 64)
        key = jax.random.key(seed)
        ks = jax.random.split(key, 9)
        s = 1.0 / math.sqrt(D)
        return {'src': jax.random.normal(ks[0], (B, S, D), dtype=jnp.float32), 'Wq': jax.random.normal(ks[1], (D, D), dtype=jnp.float32) * s, 'bq': jax.random.normal(ks[2], (D,), dtype=jnp.float32) * s, 'Wk': jax.random.normal(ks[3], (D, D), dtype=jnp.float32) * s, 'bk': jax.random.normal(ks[4], (D,), dtype=jnp.float32) * s, 'Wv': jax.random.normal(ks[5], (D, D), dtype=jnp.float32) * s, 'bv': jax.random.normal(ks[6], (D,), dtype=jnp.float32) * s, 'Wo': jax.random.normal(ks[7], (D, D), dtype=jnp.float32) * s, 'bo': jax.random.normal(ks[8], (D,), dtype=jnp.float32) * s}
    _L0_attn_all = _L0_attn_setup()
    _L0_attn_in = {k: v for k, v in _L0_attn_all.items() if k in ('Wq', 'bq', 'Wk', 'bk', 'Wv', 'bv', 'Wo', 'bo')}
    del _L0_attn_all

    def _L0_ffn_setup():
        import jax, jax.numpy as jnp
        import numpy as np
        B, T, C = (64, 96, 64)
        NH, NKV = (4, 2)
        HD = C // NH
        NREP = NH // NKV
        NE, TOPK = (8, 2)
        HID = int(8 / 3 * C)
        EPS_RMS = 1e-06

        def _rope_tables(t_len):
            inv_freq = 1.0 / 10000.0 ** (np.arange(0, HD, 2, dtype=np.float32) / HD)
            t = np.arange(t_len, dtype=np.float32)
            freqs = np.outer(t, inv_freq)
            emb = np.concatenate([freqs, freqs], axis=-1)
            return (jnp.asarray(np.cos(emb)), jnp.asarray(np.sin(emb)))

        def _rotate_half(x):
            h = x.shape[-1] // 2
            return jnp.concatenate([-x[..., h:], x[..., :h]], axis=-1)

        def _rmsnorm(v, w):
            return v * jax.lax.rsqrt(jnp.mean(v * v, axis=-1, keepdims=True) + EPS_RMS) * w
        key = jax.random.key(seed)
        ks = jax.random.split(key, 10)
        s = lambda k, shape: jax.random.normal(k, shape, jnp.float32) * 0.02
        return {'x': jax.random.normal(ks[0], (B, T, C), jnp.float32), 'ln1_w': jnp.ones((C,), jnp.float32), 'ln2_w': jnp.ones((C,), jnp.float32), 'wq': s(ks[1], (NH * HD, C)), 'wk': s(ks[2], (NKV * HD, C)), 'wv': s(ks[3], (NKV * HD, C)), 'wo': s(ks[4], (C, C)), 'router_w': s(ks[5], (NE, C)), 'w1': s(ks[6], (NE, HID, C)), 'w2': s(ks[7], (NE, C, HID)), 'w3': s(ks[8], (NE, HID, C))}
    _L0_ffn_all = _L0_ffn_setup()
    _L0_ffn_in = {k: v for k, v in _L0_ffn_all.items() if k in ('ln1_w', 'ln2_w', 'wq', 'wk', 'wv', 'wo', 'router_w', 'w1', 'w2', 'w3')}
    del _L0_ffn_all

    def _L1_attn_setup():
        import jax, jax.numpy as jnp
        import numpy as np
        B, S, D, H, K = (8, 256, 64, 8, 5)
        DK = D // H

        def _layernorm(x, w, b, eps=1e-12):
            m = x.mean(-1, keepdims=True)
            v = ((x - m) ** 2).mean(-1, keepdims=True)
            return w * (x - m) / jnp.sqrt(v + eps) + b

        def _forward(x, conv_w, conv_b, sqrt_beta, ln_w, ln_b, q_w, q_b, k_w, k_b, v_w, v_b, out_w, out_b, gammas):
            b, s, d = x.shape
            h = gammas.shape[0]
            dk = d // h
            xc = x.transpose(0, 2, 1)
            low = jax.lax.conv_general_dilated(xc, conv_w, window_strides=(1,), padding=[(K - 1, 0)], dimension_numbers=('NCH', 'OIH', 'NCH'))
            low = low.transpose(0, 2, 1) + conv_b
            high = x - low
            hid = _layernorm(low + sqrt_beta ** 2 * high + x, ln_w, ln_b)

            def proj(w, bb):
                return (hid @ w.T + bb).reshape(b, s, h, dk).transpose(0, 2, 1, 3)
            q, k, v = (proj(q_w, q_b), proj(k_w, k_b), proj(v_w, v_b))
            scores = jnp.einsum('bhqd,bhkd->bhqk', q, k) / jnp.sqrt(jnp.float32(dk))
            mask = jnp.tril(jnp.ones((s, s), bool))
            p_ = jax.nn.softmax(jnp.where(mask, scores, -1e+32), axis=-1) * mask
            distcum = jnp.cumsum(p_, axis=-1)
            disttotal = p_.sum(-1, keepdims=True)
            idx = jnp.arange(s)
            pos = jnp.abs(idx[:, None] - idx[None, :]).astype(jnp.float32)
            dist = jax.lax.stop_gradient(jnp.sqrt(jnp.clip((disttotal - distcum) * pos, 0.0)))
            gamma = -jax.nn.softplus(gammas)[None]
            total_effect = jnp.clip(jnp.exp(dist * gamma), 1e-05, 100000.0)
            scores = jnp.where(mask, scores * total_effect, -1e+32)
            p = jax.nn.softmax(scores, axis=-1)
            p = p.at[:, :, 0, :].set(0.0)
            out = jnp.einsum('bhqk,bhkd->bhqd', p, v)
            out = out.transpose(0, 2, 1, 3).reshape(b, s, d)
            return out @ out_w.T + out_b
        key = jax.random.key(seed)
        ks = jax.random.split(key, 8)
        s = 0.05
        return dict(x=jax.random.normal(ks[0], (B, S, D), jnp.float32), conv_w=jax.random.normal(ks[1], (D, D, K), jnp.float32) * s, conv_b=jnp.zeros((D,), jnp.float32), sqrt_beta=jax.random.normal(ks[2], (1, 1, D), jnp.float32), ln_w=jnp.ones((D,), jnp.float32), ln_b=jnp.zeros((D,), jnp.float32), q_w=jax.random.normal(ks[3], (D, D), jnp.float32) * s, q_b=jnp.zeros((D,), jnp.float32), k_w=jax.random.normal(ks[4], (D, D), jnp.float32) * s, k_b=jnp.zeros((D,), jnp.float32), v_w=jax.random.normal(ks[5], (D, D), jnp.float32) * s, v_b=jnp.zeros((D,), jnp.float32), out_w=jax.random.normal(ks[6], (D, D), jnp.float32) * s, out_b=jnp.zeros((D,), jnp.float32), gammas=jax.random.normal(ks[7], (H, 1, 1), jnp.float32) * 0.1)
    _L1_attn_all = _L1_attn_setup()
    _L1_attn_in = {k: v for k, v in _L1_attn_all.items() if k in ('conv_w', 'conv_b', 'sqrt_beta', 'ln_w', 'ln_b', 'q_w', 'q_b', 'k_w', 'k_b', 'v_w', 'v_b', 'out_w', 'out_b', 'gammas')}
    del _L1_attn_all

    def _L1_ffn_setup():
        import jax, jax.numpy as jnp
        import numpy as np
        B, S, D = (8, 1024, 64)
        H = 4 * D
        CAPACITY = 0.5
        key = jax.random.key(seed)
        ks = jax.random.split(key, 6)
        x = jax.random.normal(ks[0], (B, S, D), dtype=jnp.float32)
        attention_mask = jnp.zeros((B, 1, 1, S), dtype=jnp.float32)
        wr = jax.random.normal(ks[1], (D, 1), dtype=jnp.float32) * 0.02
        br = jnp.zeros((1,), dtype=jnp.float32)
        w1 = jax.random.normal(ks[2], (D, H), dtype=jnp.float32) * 0.02
        b1 = jnp.zeros((H,), dtype=jnp.float32)
        w2 = jax.random.normal(ks[3], (H, D), dtype=jnp.float32) * 0.02
        b2 = jnp.zeros((D,), dtype=jnp.float32)
        return {'x': x, 'attention_mask': attention_mask, 'wr': wr, 'br': br, 'w1': w1, 'b1': b1, 'w2': w2, 'b2': b2}
    _L1_ffn_all = _L1_ffn_setup()
    _L1_ffn_in = {k: v for k, v in _L1_ffn_all.items() if k in ('attention_mask', 'wr', 'br', 'w1', 'b1', 'w2', 'b2')}
    del _L1_ffn_all
    return {'x': x, 'L0_tok_embed_table': _L0_tok_in['embed_table'], 'L0_tok_W1': _L0_tok_in['W1'], 'L0_tok_b1': _L0_tok_in['b1'], 'L0_tok_W2': _L0_tok_in['W2'], 'L0_tok_b2': _L0_tok_in['b2'], 'L0_tok_Wa': _L0_tok_in['Wa'], 'L0_tok_ba': _L0_tok_in['ba'], 'L0_attn_Wq': _L0_attn_in['Wq'], 'L0_attn_bq': _L0_attn_in['bq'], 'L0_attn_Wk': _L0_attn_in['Wk'], 'L0_attn_bk': _L0_attn_in['bk'], 'L0_attn_Wv': _L0_attn_in['Wv'], 'L0_attn_bv': _L0_attn_in['bv'], 'L0_attn_Wo': _L0_attn_in['Wo'], 'L0_attn_bo': _L0_attn_in['bo'], 'L0_ffn_ln1_w': _L0_ffn_in['ln1_w'], 'L0_ffn_ln2_w': _L0_ffn_in['ln2_w'], 'L0_ffn_wq': _L0_ffn_in['wq'], 'L0_ffn_wk': _L0_ffn_in['wk'], 'L0_ffn_wv': _L0_ffn_in['wv'], 'L0_ffn_wo': _L0_ffn_in['wo'], 'L0_ffn_router_w': _L0_ffn_in['router_w'], 'L0_ffn_w1': _L0_ffn_in['w1'], 'L0_ffn_w2': _L0_ffn_in['w2'], 'L0_ffn_w3': _L0_ffn_in['w3'], 'L1_attn_conv_w': _L1_attn_in['conv_w'], 'L1_attn_conv_b': _L1_attn_in['conv_b'], 'L1_attn_sqrt_beta': _L1_attn_in['sqrt_beta'], 'L1_attn_ln_w': _L1_attn_in['ln_w'], 'L1_attn_ln_b': _L1_attn_in['ln_b'], 'L1_attn_q_w': _L1_attn_in['q_w'], 'L1_attn_q_b': _L1_attn_in['q_b'], 'L1_attn_k_w': _L1_attn_in['k_w'], 'L1_attn_k_b': _L1_attn_in['k_b'], 'L1_attn_v_w': _L1_attn_in['v_w'], 'L1_attn_v_b': _L1_attn_in['v_b'], 'L1_attn_out_w': _L1_attn_in['out_w'], 'L1_attn_out_b': _L1_attn_in['out_b'], 'L1_attn_gammas': _L1_attn_in['gammas'], 'L1_ffn_attention_mask': _L1_ffn_in['attention_mask'], 'L1_ffn_wr': _L1_ffn_in['wr'], 'L1_ffn_br': _L1_ffn_in['br'], 'L1_ffn_w1': _L1_ffn_in['w1'], 'L1_ffn_b1': _L1_ffn_in['b1'], 'L1_ffn_w2': _L1_ffn_in['w2'], 'L1_ffn_b2': _L1_ffn_in['b2']}

def reference(x, L0_tok_embed_table, L0_tok_W1, L0_tok_b1, L0_tok_W2, L0_tok_b2, L0_tok_Wa, L0_tok_ba, L0_attn_Wq, L0_attn_bq, L0_attn_Wk, L0_attn_bk, L0_attn_Wv, L0_attn_bv, L0_attn_Wo, L0_attn_bo, L0_ffn_ln1_w, L0_ffn_ln2_w, L0_ffn_wq, L0_ffn_wk, L0_ffn_wv, L0_ffn_wo, L0_ffn_router_w, L0_ffn_w1, L0_ffn_w2, L0_ffn_w3, L1_attn_conv_w, L1_attn_conv_b, L1_attn_sqrt_beta, L1_attn_ln_w, L1_attn_ln_b, L1_attn_q_w, L1_attn_q_b, L1_attn_k_w, L1_attn_k_b, L1_attn_v_w, L1_attn_v_b, L1_attn_out_w, L1_attn_out_b, L1_attn_gammas, L1_ffn_attention_mask, L1_ffn_wr, L1_ffn_br, L1_ffn_w1, L1_ffn_b1, L1_ffn_w2, L1_ffn_b2):
    import jax
    import jax.numpy as jnp

    def _L0_tok_ref(batch, embed_table, W1, b1, W2, b2, Wa, ba):
        import jax, jax.numpy as jnp
        import numpy as np
        VOCAB = 25000
        DIM_SRC = 75
        DIM_PROJ = 64
        concat = embed_table[batch]
        e1 = concat[..., :DIM_SRC]
        e2 = concat[..., DIM_SRC:]
        p1 = jnp.einsum('bsd,dp->bsp', e1, W1) + b1
        p2 = jnp.einsum('bsd,dp->bsp', e2, W2) + b2
        proj = jnp.stack([p1, p2], axis=2)
        attn = jax.nn.sigmoid(jnp.einsum('bsvp,po->bsvo', proj, Wa) + ba)
        out = jnp.sum(proj * attn, axis=2)
        return out

    def _L0_attn_ref(src, Wq, bq, Wk, bk, Wv, bv, Wo, bo):
        import jax, jax.numpy as jnp
        import numpy as np
        import math
        B, S, D = (4, 1024, 64)
        q = src @ Wq.T + bq
        k = src @ Wk.T + bk
        v = src @ Wv.T + bv
        row_mask = (q[:, :, 0] != 0) & (k[:, :, 0] != 0)
        mask = row_mask[:, :, None]
        scale = 1.0 / math.sqrt(D)
        scores = jnp.einsum('bid,bjd->bij', q, k) * scale
        scores = jnp.where(mask, scores, jnp.float32(-1000000000.0))
        prob = jax.nn.softmax(scores, axis=-1)
        prob = jnp.where(mask, prob, 0.0)
        out = jnp.einsum('bij,bjd->bid', prob, v)
        return out @ Wo.T + bo

    def _L0_ffn_ref(x, ln1_w, ln2_w, wq, wk, wv, wo, router_w, w1, w2, w3):
        import jax, jax.numpy as jnp
        import numpy as np
        B, T, C = (64, 96, 64)
        NH, NKV = (4, 2)
        HD = C // NH
        NREP = NH // NKV
        NE, TOPK = (8, 2)
        HID = int(8 / 3 * C)
        EPS_RMS = 1e-06

        def _rope_tables(t_len):
            inv_freq = 1.0 / 10000.0 ** (np.arange(0, HD, 2, dtype=np.float32) / HD)
            t = np.arange(t_len, dtype=np.float32)
            freqs = np.outer(t, inv_freq)
            emb = np.concatenate([freqs, freqs], axis=-1)
            return (jnp.asarray(np.cos(emb)), jnp.asarray(np.sin(emb)))

        def _rotate_half(x):
            h = x.shape[-1] // 2
            return jnp.concatenate([-x[..., h:], x[..., :h]], axis=-1)

        def _rmsnorm(v, w):
            return v * jax.lax.rsqrt(jnp.mean(v * v, axis=-1, keepdims=True) + EPS_RMS) * w
        Bx, Tx, Cx = x.shape
        h = _rmsnorm(x, ln1_w)
        q = (h @ wq.T).reshape(Bx, Tx, NH, HD).transpose(0, 2, 1, 3)
        k = (h @ wk.T).reshape(Bx, Tx, NKV, HD).transpose(0, 2, 1, 3)
        v = (h @ wv.T).reshape(Bx, Tx, NKV, HD).transpose(0, 2, 1, 3)
        cos, sin = _rope_tables(Tx)
        cos, sin = (cos[None, None], sin[None, None])
        q = q * cos + _rotate_half(q) * sin
        k = k * cos + _rotate_half(k) * sin
        k = jnp.repeat(k, NREP, axis=1)
        v = jnp.repeat(v, NREP, axis=1)
        scores = jnp.einsum('bhtd,bhsd->bhts', q, k) / jnp.sqrt(jnp.float32(HD))
        causal = jnp.tril(jnp.ones((Tx, Tx), dtype=bool))
        scores = jnp.where(causal[None, None], scores, jnp.float32(-1e+30))
        att = jax.nn.softmax(scores, axis=-1)
        y = jnp.einsum('bhts,bhsd->bhtd', att, v).transpose(0, 2, 1, 3).reshape(Bx, Tx, Cx)
        x = x + y @ wo.T
        flat = _rmsnorm(x, ln2_w).reshape(-1, Cx)
        probs = jax.nn.softmax(flat @ router_w.T, axis=-1)
        tp, ti = jax.lax.top_k(probs, TOPK)
        tp = tp / (jnp.sum(tp, axis=-1, keepdims=True) + 1e-09)
        weights = jnp.sum(tp[..., None] * jax.nn.one_hot(ti, NE, dtype=flat.dtype), axis=1)
        out = jnp.zeros_like(flat)
        for e in range(NE):
            hh = jax.nn.silu(flat @ w1[e].T) * (flat @ w3[e].T)
            out = out + weights[:, e:e + 1] * (hh @ w2[e].T)
        return x + out.reshape(Bx, Tx, Cx)

    def _L1_attn_ref(x, conv_w, conv_b, sqrt_beta, ln_w, ln_b, q_w, q_b, k_w, k_b, v_w, v_b, out_w, out_b, gammas):
        import jax, jax.numpy as jnp
        import numpy as np
        B, S, D, H, K = (8, 256, 64, 8, 5)
        DK = D // H

        def _layernorm(x, w, b, eps=1e-12):
            m = x.mean(-1, keepdims=True)
            v = ((x - m) ** 2).mean(-1, keepdims=True)
            return w * (x - m) / jnp.sqrt(v + eps) + b

        def _forward(x, conv_w, conv_b, sqrt_beta, ln_w, ln_b, q_w, q_b, k_w, k_b, v_w, v_b, out_w, out_b, gammas):
            b, s, d = x.shape
            h = gammas.shape[0]
            dk = d // h
            xc = x.transpose(0, 2, 1)
            low = jax.lax.conv_general_dilated(xc, conv_w, window_strides=(1,), padding=[(K - 1, 0)], dimension_numbers=('NCH', 'OIH', 'NCH'))
            low = low.transpose(0, 2, 1) + conv_b
            high = x - low
            hid = _layernorm(low + sqrt_beta ** 2 * high + x, ln_w, ln_b)

            def proj(w, bb):
                return (hid @ w.T + bb).reshape(b, s, h, dk).transpose(0, 2, 1, 3)
            q, k, v = (proj(q_w, q_b), proj(k_w, k_b), proj(v_w, v_b))
            scores = jnp.einsum('bhqd,bhkd->bhqk', q, k) / jnp.sqrt(jnp.float32(dk))
            mask = jnp.tril(jnp.ones((s, s), bool))
            p_ = jax.nn.softmax(jnp.where(mask, scores, -1e+32), axis=-1) * mask
            distcum = jnp.cumsum(p_, axis=-1)
            disttotal = p_.sum(-1, keepdims=True)
            idx = jnp.arange(s)
            pos = jnp.abs(idx[:, None] - idx[None, :]).astype(jnp.float32)
            dist = jax.lax.stop_gradient(jnp.sqrt(jnp.clip((disttotal - distcum) * pos, 0.0)))
            gamma = -jax.nn.softplus(gammas)[None]
            total_effect = jnp.clip(jnp.exp(dist * gamma), 1e-05, 100000.0)
            scores = jnp.where(mask, scores * total_effect, -1e+32)
            p = jax.nn.softmax(scores, axis=-1)
            p = p.at[:, :, 0, :].set(0.0)
            out = jnp.einsum('bhqk,bhkd->bhqd', p, v)
            out = out.transpose(0, 2, 1, 3).reshape(b, s, d)
            return out @ out_w.T + out_b
        return _forward(x, conv_w, conv_b, sqrt_beta, ln_w, ln_b, q_w, q_b, k_w, k_b, v_w, v_b, out_w, out_b, gammas)

    def _L1_ffn_ref(x, attention_mask, wr, br, w1, b1, w2, b2):
        import jax, jax.numpy as jnp
        import numpy as np
        B, S, D = (8, 1024, 64)
        H = 4 * D
        CAPACITY = 0.5
        b, s, d = x.shape
        weights = (jnp.einsum('bsd,do->bso', x, wr) + br)[..., 0]
        k = max(1, int(CAPACITY * s))
        kk = k - 1 if k > 1 else 1
        _, idx = jax.lax.top_k(weights, k)
        sel_idx = idx[:, :kk]
        sel = jnp.take_along_axis(x, sel_idx[:, :, None], axis=1)
        h = jax.nn.gelu(jnp.einsum('bkd,dh->bkh', sel, w1) + b1)
        y = jnp.einsum('bkh,hd->bkd', h, w2) + b2
        w_sel = jnp.take_along_axis(weights, sel_idx, axis=1)
        y = y * w_sel[..., None]
        batch_idx = jnp.arange(b)[:, None]
        processed = jnp.zeros_like(x).at[batch_idx, sel_idx].set(y)
        return processed + x
    h = _L0_tok_ref(x, L0_tok_embed_table, L0_tok_W1, L0_tok_b1, L0_tok_W2, L0_tok_b2, L0_tok_Wa, L0_tok_ba)
    h = h + _L0_attn_ref(_layernorm(h, axis=-1), L0_attn_Wq, L0_attn_bq, L0_attn_Wk, L0_attn_bk, L0_attn_Wv, L0_attn_bv, L0_attn_Wo, L0_attn_bo)
    h = h + _L0_ffn_ref(_layernorm(h, axis=-1), L0_ffn_ln1_w, L0_ffn_ln2_w, L0_ffn_wq, L0_ffn_wk, L0_ffn_wv, L0_ffn_wo, L0_ffn_router_w, L0_ffn_w1, L0_ffn_w2, L0_ffn_w3)
    h = h + _L1_attn_ref(_layernorm(h, axis=-1), L1_attn_conv_w, L1_attn_conv_b, L1_attn_sqrt_beta, L1_attn_ln_w, L1_attn_ln_b, L1_attn_q_w, L1_attn_q_b, L1_attn_k_w, L1_attn_k_b, L1_attn_v_w, L1_attn_v_b, L1_attn_out_w, L1_attn_out_b, L1_attn_gammas)
    h = h + _L1_ffn_ref(_layernorm(h, axis=-1), L1_ffn_attention_mask, L1_ffn_wr, L1_ffn_br, L1_ffn_w1, L1_ffn_b1, L1_ffn_w2, L1_ffn_b2)
    return h

_drawn_inputs = setup_inputs


def setup_inputs(seed=0):
    import zlib

    import numpy as np

    out = dict(_drawn_inputs(seed))
    spreads = {'L0_ffn_ln1_w': (1.0, 0.6),
     'L0_ffn_ln2_w': (1.0, 0.6),
     'L1_attn_conv_b': (0.0, 0.8),
     'L1_attn_ln_w': (1.0, 0.6),
     'L1_attn_ln_b': (0.0, 0.8),
     'L1_attn_q_b': (0.0, 2.0),
     'L1_attn_k_b': (0.0, 2.0),
     'L1_attn_v_b': (0.0, 1.022),
     'L1_attn_out_b': (0.0, 0.311),
     'L1_ffn_b1': (0.0, 0.8),
     'L1_ffn_b2': (0.0, 0.8)}
    factors = {'L0_attn_bk': 64.0,
     'L0_ffn_wq': 8.0,
     'L0_ffn_wk': 8.0,
     'L0_ffn_wv': 5.868,
     'L0_ffn_wo': 6.844,
     'L0_ffn_router_w': 8.0,
     'L0_ffn_w1': 8.0,
     'L0_ffn_w2': 8.0,
     'L0_ffn_w3': 8.0,
     'L1_attn_q_w': 8.0,
     'L1_attn_k_w': 8.0,
     'L1_attn_gammas': 55.418,
     'L1_ffn_wr': 8.0,
     'L1_ffn_w1': 8.0,
     'L1_ffn_w2': 8.0}
    for name, (base, spread) in spreads.items():
        noise = np.random.default_rng([zlib.crc32(name.encode()), seed]).standard_normal(out[name].shape)
        drawn = base * np.exp(spread * noise) if base else spread * noise
        out[name] = jnp.asarray(drawn.astype(out[name].dtype))
    for name, factor in factors.items():
        out[name] = (out[name] * factor).astype(out[name].dtype)
    return out
```

```python
from contextlib import ExitStack

import concourse.bass as bass
import numpy as np
from concourse import mybir

ALU = mybir.AluOpType
ACT = mybir.ActivationFunctionType
AX = mybir.AxisListType.X
F32 = mybir.dt.float32
BF16 = mybir.dt.bfloat16
I32 = mybir.dt.int32

P = 128
D = 64
GB = 4
W = GB * P


class Signals:

    def __init__(self, mem, phase, slots, **owned):
        self.slots, self.sems = slots, {}
        self.names = {engine: text.split() for engine, text in owned.items()}
        for listed in self.names.values():
            for name in listed:
                name, _, count = name.partition("*")
                made = [mem.sem(f"{phase}_{name}{k}") for k in range(int(count or 1))]
                self.sems[name] = made if count else made[0]

    def __getitem__(self, name):
        return self.sems[name]

    def start(self, eng, engine):
        for name in self.names[engine]:
            made = self.sems[name.partition("*")[0]]
            for sem in made if "*" in name else [made]:
                eng.sem_inc(sem, self.slots)

    def now(self, n):
        return n + (self.slots + 1)

    def ago(self, n, k):
        return n + (self.slots + 1 - k)

    def before(self, n):
        return n + self.slots

    def past(self, n):
        return n + 1


def grouped(ap, width):
    return ap.rearrange("p (g w) -> p g w", w=width)


def over(ap, width):
    return ap[:, :, None].to_broadcast([ap.shape[0], ap.shape[1], width])


class Mem:

    def __init__(self, nc, ctx):
        self.nc, self.ctx, self.sems = nc, ctx, []

    def sb(self, name, shape, dt=F32):
        return self.ctx.enter_context(self.nc.sbuf_tensor(name, shape, dt))

    def ps(self, name, shape, dt=F32):
        return self.ctx.enter_context(self.nc.psum_tensor(name, shape, dt))

    def sem(self, name):
        self.sems.append(self.ctx.enter_context(self.nc.semaphore(name)))
        return self.sems[-1]

    def clear_semaphores(self):
        numbers = sorted(s.num for s in self.sems)
        with self.nc.Block() as block:
            @block.gpsimd
            def _(pool):
                first = last = numbers[0]
                for n in numbers[1:] + [None]:
                    if n is None or n != last + 1:
                        pool.sem_clear(range(first, last + 1))
                        first = n
                    last = n




def phase_embed_attend(nc, dram, H, ident, gathered, NB):
    E_DIM = dram["table"].shape[1] // 2
    KE = E_DIM + 1
    KX = D + 1
    NG = NB // GB
    SLOTS = 2
    assert NG % SLOTS == 0
    with ExitStack() as ctx:
        m = Mem(nc, ctx)
        tok = m.sb("tok", [P, NB], I32)
        idx = [m.sb(f"idx{u}", [P, GB], I32) for u in range(SLOTS)]
        nothing = m.sb("nothing", [P, 2], I32)
        rows = [m.sb(f"rows{u}", [P, GB, 2 * E_DIM]) for u in range(SLOTS)]
        rowsT = [m.sb(f"rowsT{u}", [P, 2, W]) for u in range(SLOTS)]
        tokw = m.sb("tokw", [KE, 2, KX])
        tokwT = m.sb("tokwT", [D, 2, KE])
        wa = m.sb("wa", [D, 1])
        nba = m.sb("nba", [P, 1])
        qa = m.sb("qa", [D, KX])
        ka = m.sb("ka", [D, KX])
        va = m.sb("va", [D, KX])
        woT = m.sb("woT", [D, D])
        bo = m.sb("bo", [P, D])
        qk = m.sb("qk", [KX, KX])
        vo = m.sb("vo", [KX, D + 3])
        gate = [m.sb(f"gate{u}", [P, 2, GB]) for u in range(SLOTS)]
        part = [m.sb(f"part{u}", [P, 2, GB, D]) for u in range(SLOTS)]
        h0 = [m.sb(f"h0{u}", [P, GB, D]) for u in range(SLOTS)]
        st = [m.sb(f"st{u}", [P, GB, 6]) for u in range(SLOTS)]
        mv = [m.sb(f"mv{u}", [P, GB, 2]) for u in range(SLOTS)]
        rstd = [m.sb(f"rstd{u}", [P, GB]) for u in range(SLOTS)]
        xn = [m.sb(f"xn{u}", [P, GB, D]) for u in range(SLOTS)]
        xT = [m.sb(f"xT{u}", [KX, W]) for u in range(SLOTS)]
        yT = [m.sb(f"yT{u}", [KX, W]) for u in range(SLOTS)]
        v = [m.sb(f"v{u}", [P, GB, D + 3]) for u in range(SLOTS)]
        mx = [m.sb(f"mx{u}", [P, GB]) for u in range(SLOTS)]
        pr = [m.sb(f"pr{u}", [P, W]) for u in range(SLOTS)]
        pT = [m.sb(f"pT{u}", [P, W]) for u in range(SLOTS)]
        live = [m.sb(f"live{u}", [P, GB, 2]) for u in range(SLOTS)]
        rs = [m.sb(f"rs{u}", [P, GB]) for u in range(SLOTS)]
        att = [m.sb(f"att{u}", [P, GB, D]) for u in range(SLOTS)]
        bank = [[m.ps(f"bk{u}{k}", [P, 512]) for k in range(4)] for u in range(SLOTS)]

        passed = m.sem("a_passed")
        loaded = m.sem("a_loaded")
        assert len(gathered) == SLOTS
        preset = m.sem("a_preset")
        folded = m.sem("a_folded")
        folded_sb = m.sem("a_folded_sb")
        S = Signals(m, "a", SLOTS,
                    gpsimd="idx_staged settled bias_added",
                    tensor="rows_turned projected x_turned y_made v_made scored p_turned attended",
                    scalar="rows0_kept gate_exp0 gate_exp log_var rstd_made xT_kept v_kept p_exp pT_kept",
                    vector="rows1_kept gate_plus gated part0 part1 h0_made stats moments centred yT_kept "
                           "max_made shifted live_made live_row inv_sum inv_live att_made h_made")
        LOADS = 11

        with nc.Block() as block:
            @block.sync
            def _(sp):
                sp.dma_start(tok[:], dram["tokens"]).then_inc(loaded, 16)
                sp.dma_start(tokw[:, :, 0:D], dram["tok_w"].rearrange("v k n -> k v n")).then_inc(loaded, 16)
                sp.dma_start(tokwT[:], dram["tok_wT"].rearrange("v k n -> k v n")).then_inc(loaded, 16)
                sp.dma_start(wa[:], dram["tok_wa"]).then_inc(loaded, 16)
                sp.dma_start(nba[:], dram["tok_ba"]).then_inc(loaded, 16)
                sp.dma_start(qa[:], dram["a0_q"]).then_inc(loaded, 16)
                sp.dma_start(ka[:], dram["a0_k"]).then_inc(loaded, 16)
                sp.dma_start(va[:], dram["a0_v"]).then_inc(loaded, 16)
                sp.dma_start(woT[:], dram["a0_woT"]).then_inc(loaded, 16)
                sp.dma_start(bo[:], dram["a0_bo"]).then_inc(loaded, 16)
                sp.dma_start(vo[:, D + 1:D + 3], dram["a0_first"]).then_inc(loaded, 16)

            @block.gpsimd
            def _(pool):
                S.start(pool, "gpsimd")
                pool.wait_ge(loaded, 16 * LOADS)
                pool.wait_ge(preset, 2 * SLOTS + 3)
                with pool.Fori(0, NG // SLOTS) as i:
                    for u in range(SLOTS):
                        n = i * SLOTS + u
                        pool.wait_ge(S["rows_turned"], S.past(n))
                        pool.tensor_tensor(idx[u][:], tok[:, bass.ds(n * GB, GB)], nothing[:, 0:1].to_broadcast([P, GB]),
                                           ALU.add).then_inc(S["idx_staged"], 1)
                        pool.wait_ge(S["idx_staged"], S.now(n))
                        pool.tensor_tensor(nothing[:, 1:2], nothing[:, 0:1], nothing[:, 0:1], ALU.add)\
                            .then_inc(S["settled"], 1)
                        for b in range(GB):
                            pool.indirect_dma_start(rows[u][:, b, :], None, dram["table"],
                                                    bass.IndirectOffsetOnAxis(ap=idx[u][:, b:b + 1], axis=0))\
                                .then_inc(gathered[u], 16)
                    for u in range(SLOTS):
                        n = i * SLOTS + u
                        pool.wait_ge(S["centred"], S.now(n))
                        pool.tensor_tensor(H[:, bass.ds(n * GB, GB), :], h0[u][:],
                                           bo[:, None, :].to_broadcast([P, GB, D]), ALU.add)\
                            .then_inc(S["bias_added"], 1)

            @block.tensor
            def _(pe):
                S.start(pe, "tensor")
                pe.wait_ge(loaded, 16 * LOADS)
                for k in range(2):
                    nc.tensor.matmul(bank[0][0][0:KE, k:k + 1], tokwT[:, k, :], wa[:], start=True, stop=True)
                nc.tensor.matmul(bank[0][1][0:KX, 0:KX], qa[:], ka[:], start=True, stop=True)
                nc.tensor.matmul(bank[0][2][0:KX, 0:D], va[:], woT[:], start=True, stop=True).then_inc(folded, 1)
                pe.wait_ge(folded_sb, 4)
                pe.wait_ge(preset, 2 * SLOTS + 3)
                with pe.Fori(0, NG // SLOTS) as i:
                    for u in range(SLOTS):
                        n, bk = i * SLOTS + u, bank[u]
                        pe.wait_ge(gathered[u], (i + 1) * (16 * GB))
                        pe.wait_ge(S["pT_kept"], S.past(n))
                        pe.wait_ge(S["att_made"], S.past(n))
                        for k in range(2):
                            for b in range(GB):
                                last = nc.tensor.transpose(bk[k][0:E_DIM, b * P:(b + 1) * P],
                                                           rows[u][:, b, k * E_DIM:(k + 1) * E_DIM], ident[:])
                        last.then_inc(S["rows_turned"], 1)
                    for u in range(SLOTS):
                        n, bk = i * SLOTS + u, bank[u]
                        pe.wait_ge(S["rows0_kept"], S.now(n))
                        pe.wait_ge(S["rows1_kept"], S.now(n))
                        pe.wait_ge(S["v_kept"], S.past(n))
                        pe.wait_ge(S["shifted"], S.past(n))
                        for k in range(2):
                            for b in range(GB):
                                last = nc.tensor.matmul(bk[2 + k][:, b * KX:(b + 1) * KX],
                                                        rowsT[u][0:KE, k, b * P:(b + 1) * P], tokw[:, k, :],
                                                        start=True, stop=True)
                        last.then_inc(S["projected"], 1)
                    for u in range(SLOTS):
                        n, bk = i * SLOTS + u, bank[u]
                        pe.wait_ge(S["centred"], S.now(n))
                        pe.sem_inc(passed, 1)
                        for b in range(GB):
                            last = nc.tensor.transpose(bk[0][0:D, b * P:(b + 1) * P], xn[u][:, b, :], ident[:])
                        last.then_inc(S["x_turned"], 1)
                    for u in range(SLOTS):
                        n, bk = i * SLOTS + u, bank[u]
                        pe.wait_ge(S["xT_kept"], S.now(n))
                        nc.tensor.matmul(bk[1][0:KX, :], qk[:], xT[u][:], start=True, stop=True)\
                            .then_inc(S["y_made"], 1)
                        for b in range(GB):
                            last = nc.tensor.matmul(bk[2][:, b * (D + 3):(b + 1) * (D + 3)],
                                                    xT[u][:, b * P:(b + 1) * P], vo[:], start=True, stop=True)
                        last.then_inc(S["v_made"], 1)
                    for u in range(SLOTS):
                        n, bk = i * SLOTS + u, bank[u]
                        pe.wait_ge(S["yT_kept"], S.now(n))
                        for b in range(GB):
                            last = nc.tensor.matmul(bk[3][:, b * P:(b + 1) * P], yT[u][:, b * P:(b + 1) * P],
                                                    xT[u][:, b * P:(b + 1) * P], start=True, stop=True)
                        last.then_inc(S["scored"], 1)
                    for u in range(SLOTS):
                        n, bk = i * SLOTS + u, bank[u]
                        pe.wait_ge(S["p_exp"], S.now(n))
                        for b in range(GB):
                            last = nc.tensor.transpose(bk[0][:, b * P:(b + 1) * P], pr[u][:, b * P:(b + 1) * P],
                                                       ident[:])
                        last.then_inc(S["p_turned"], 1)
                    for u in range(SLOTS):
                        n, bk = i * SLOTS + u, bank[u]
                        pe.wait_ge(S["pT_kept"], S.now(n))
                        pe.wait_ge(S["v_kept"], S.now(n))
                        for b in range(GB):
                            last = nc.tensor.matmul(bk[1][:, b * KX:(b + 1) * KX], pT[u][:, b * P:(b + 1) * P],
                                                    v[u][:, b, 0:KX], start=True, stop=True)
                        last.then_inc(S["attended"], 1)

            @block.scalar
            def _(act):
                S.start(act, "scalar")
                act.preload_act_table_set("natural_log_exp_and_others")
                act.wait_ge(loaded, 16 * LOADS)
                act.wait_ge(folded, 1)
                nc.scalar.activation(tokw[:, :, D], bank[0][0][0:KE, 0:2], ACT.Copy).then_inc(folded_sb, 1)
                nc.scalar.activation(qk[:], bank[0][1][0:KX, 0:KX], ACT.Copy, scale=D ** -0.5)\
                    .then_inc(folded_sb, 1)
                nc.scalar.activation(vo[:, 0:D], bank[0][2][0:KX, 0:D], ACT.Copy).then_inc(folded_sb, 1)
                nc.scalar.activation(nba[:], nba[:], ACT.Copy, scale=-1.0).then_inc(folded_sb, 1)
                act.wait_ge(folded_sb, 4)
                act.wait_ge(preset, 2 * SLOTS + 3)
                with act.Fori(0, NG // SLOTS) as i:
                    for u in range(SLOTS):
                        n, bk = i * SLOTS + u, bank[u]
                        act.wait_ge(S["rows_turned"], S.now(n))
                        act.wait_ge(S["projected"], S.past(n))
                        nc.scalar.activation(rowsT[u][0:E_DIM, 0, :], bk[0][0:E_DIM, :], ACT.Copy)\
                            .then_inc(S["rows0_kept"], 1)
                    for u in range(SLOTS):
                        n, bk = i * SLOTS + u, bank[u]
                        act.wait_ge(S["projected"], S.now(n))
                        act.wait_ge(S["part1"], S.past(n))
                        for k in range(2):
                            logit = grouped(bk[2 + k][:, 0:GB * KX], KX)[:, :, D]
                            nc.scalar.activation(gate[u][:, k, :], logit, ACT.Exp, bias=nba[:, 0:1], scale=-1.0)\
                                .then_inc(S["gate_exp"] if k else S["gate_exp0"], 1)
                    for u in range(SLOTS):
                        n = i * SLOTS + u
                        act.wait_ge(S["moments"], S.now(n))
                        act.wait_ge(S["centred"], S.past(n))
                        nc.scalar.activation(rstd[u][:], mv[u][:, :, 1], ACT.Ln, bias=1e-5).then_inc(S["log_var"], 1)
                    for u in range(SLOTS):
                        n = i * SLOTS + u
                        act.wait_ge(S["log_var"], S.now(n))
                        nc.scalar.activation(rstd[u][:], rstd[u][:], ACT.Exp, scale=-0.5).then_inc(S["rstd_made"], 1)
                    for u in range(SLOTS):
                        n, bk = i * SLOTS + u, bank[u]
                        act.wait_ge(S["x_turned"], S.now(n))
                        act.wait_ge(S["scored"], S.past(n))
                        nc.scalar.activation(xT[u][0:D, :], bk[0][0:D, :], ACT.Copy).then_inc(S["xT_kept"], 1)
                    for u in range(SLOTS):
                        n, bk = i * SLOTS + u, bank[u]
                        act.wait_ge(S["v_made"], S.now(n))
                        act.wait_ge(S["attended"], S.past(n))
                        act.wait_ge(S["live_made"], S.past(n))
                        nc.scalar.activation(v[u][:], grouped(bk[2][:, 0:GB * (D + 3)], D + 3), ACT.Copy)\
                            .then_inc(S["v_kept"], 1)
                    for u in range(SLOTS):
                        n = i * SLOTS + u
                        act.wait_ge(S["shifted"], S.now(n))
                        nc.scalar.activation(pr[u][:], pr[u][:], ACT.Exp).then_inc(S["p_exp"], 1)
                    for u in range(SLOTS):
                        n, bk = i * SLOTS + u, bank[u]
                        act.wait_ge(S["p_turned"], S.now(n))
                        act.wait_ge(S["attended"], S.past(n))
                        nc.scalar.activation(pT[u][:], bk[0][:], ACT.Copy).then_inc(S["pT_kept"], 1)

            @block.vector
            def _(dve):
                S.start(dve, "vector")
                nc.vector.memset(nothing[:], 0).then_inc(preset, 1)
                for u in range(SLOTS):
                    nc.vector.memset(rowsT[u][64:P, :, :], 1.0).then_inc(preset, 1)
                    nc.vector.memset(xT[u][D:KX, :], 1.0).then_inc(preset, 1)
                nc.vector.memset(vo[0:D, D:D + 1], 0.0).then_inc(preset, 1)
                nc.vector.memset(vo[D:KX, D:D + 1], 1.0).then_inc(preset, 1)
                dve.wait_ge(preset, 2 * SLOTS + 3)
                with dve.Fori(0, NG // SLOTS) as i:
                    for u in range(SLOTS):
                        n, bk = i * SLOTS + u, bank[u]
                        dve.wait_ge(S["rows_turned"], S.now(n))
                        dve.wait_ge(S["projected"], S.past(n))
                        nc.vector.tensor_copy(rowsT[u][0:E_DIM, 1, :], bk[1][0:E_DIM, :]).then_inc(S["rows1_kept"], 1)
                    for u in range(SLOTS):
                        n = i * SLOTS + u
                        dve.wait_ge(S["gate_exp"], S.now(n))
                        dve.wait_ge(S["h_made"], S.past(n))
                        nc.vector.tensor_scalar(gate[u][:], gate[u][:], 1.0, None, ALU.add).then_inc(S["gate_plus"], 1)
                    for u in range(SLOTS):
                        n = i * SLOTS + u
                        dve.wait_ge(S["gate_plus"], S.now(n))
                        nc.vector.reciprocal(gate[u][:], gate[u][:]).then_inc(S["gated"], 1)
                    for u in range(SLOTS):
                        n, bk = i * SLOTS + u, bank[u]
                        dve.wait_ge(S["gated"], S.now(n))
                        for k in range(2):
                            nc.vector.tensor_tensor(part[u][:, k], grouped(bk[2 + k][:, 0:GB * KX], KX)[:, :, 0:D],
                                                    over(gate[u][:, k, :], D), ALU.mult)\
                                .then_inc(S["part1"] if k else S["part0"], 1)
                    for u in range(SLOTS):
                        n = i * SLOTS + u
                        dve.wait_ge(S["part1"], S.now(n))
                        dve.wait_ge(S["bias_added"], S.past(n))
                        nc.vector.tensor_tensor(h0[u][:], part[u][:, 0], part[u][:, 1], ALU.add)\
                            .then_inc(S["h0_made"], 1)
                    for u in range(SLOTS):
                        n = i * SLOTS + u
                        dve.wait_ge(S["h0_made"], S.now(n))
                        for b in range(GB):
                            last = nc.vector.bn_stats(st[u][:, b, :], h0[u][:, b, :])
                        last.then_inc(S["stats"], 1)
                    for u in range(SLOTS):
                        n = i * SLOTS + u
                        dve.wait_ge(S["stats"], S.now(n))
                        dve.wait_ge(S["rstd_made"], S.past(n))
                        dve.sem_inc(passed, 1)
                        for b in range(GB):
                            last = nc.vector.bn_aggr(mv[u][:, b, :], st[u][:, b, :])
                        last.then_inc(S["moments"], 1)
                    for u in range(SLOTS):
                        n = i * SLOTS + u
                        dve.wait_ge(S["rstd_made"], S.now(n))
                        dve.wait_ge(S["x_turned"], S.past(n))
                        for b in range(GB):
                            last = nc.vector.tensor_scalar(xn[u][:, b, :], h0[u][:, b, :], mv[u][:, b, 0:1],
                                                           rstd[u][:, b:b + 1], ALU.subtract, ALU.mult)
                        last.then_inc(S["centred"], 1)
                    for u in range(SLOTS):
                        n, bk = i * SLOTS + u, bank[u]
                        dve.wait_ge(S["y_made"], S.now(n))
                        dve.wait_ge(S["scored"], S.past(n))
                        nc.vector.tensor_copy(yT[u][:], bk[1][0:KX, :]).then_inc(S["yT_kept"], 1)
                    for u in range(SLOTS):
                        n, bk = i * SLOTS + u, bank[u]
                        dve.wait_ge(S["scored"], S.now(n))
                        nc.vector.tensor_reduce(mx[u][:], grouped(bk[3][:], P), AX, ALU.max).then_inc(S["max_made"], 1)
                    for u in range(SLOTS):
                        n, bk = i * SLOTS + u, bank[u]
                        dve.wait_ge(S["max_made"], S.now(n))
                        dve.wait_ge(S["p_turned"], S.past(n))
                        nc.vector.tensor_tensor(grouped(pr[u][:], P), grouped(bk[3][:], P), over(mx[u][:], P),
                                                ALU.subtract).then_inc(S["shifted"], 1)
                    for u in range(SLOTS):
                        n = i * SLOTS + u
                        dve.wait_ge(S["v_kept"], S.now(n))
                        nc.vector.tensor_scalar(live[u][:], v[u][:, :, D + 1:D + 3], 0.0, None, ALU.not_equal)\
                            .then_inc(S["live_made"], 1)
                    for u in range(SLOTS):
                        n, bk = i * SLOTS + u, bank[u]
                        dve.wait_ge(S["attended"], S.now(n))
                        nc.vector.reciprocal(rs[u][:], grouped(bk[1][:, 0:GB * KX], KX)[:, :, D])\
                            .then_inc(S["inv_sum"], 1)
                    for u in range(SLOTS):
                        n = i * SLOTS + u
                        dve.wait_ge(S["inv_sum"], S.now(n))
                        dve.wait_ge(S["live_made"], S.now(n))
                        nc.vector.tensor_tensor(rs[u][:], rs[u][:], live[u][:, :, 0], ALU.mult).then_inc(S["live_row"], 1)
                    for u in range(SLOTS):
                        n = i * SLOTS + u
                        dve.wait_ge(S["live_row"], S.now(n))
                        nc.vector.tensor_tensor(rs[u][:], rs[u][:], live[u][:, :, 1], ALU.mult).then_inc(S["inv_live"], 1)
                    for u in range(SLOTS):
                        n, bk = i * SLOTS + u, bank[u]
                        dve.wait_ge(S["inv_live"], S.now(n))
                        nc.vector.tensor_tensor(att[u][:], grouped(bk[1][:, 0:GB * KX], KX)[:, :, 0:D],
                                                over(rs[u][:], D), ALU.mult).then_inc(S["att_made"], 1)
                    for u in range(SLOTS):
                        n = i * SLOTS + u
                        dve.wait_ge(S["att_made"], S.now(n))
                        dve.wait_ge(S["bias_added"], S.now(n))
                        hs = H[:, bass.ds(n * GB, GB), :]
                        nc.vector.tensor_tensor(hs, hs, att[u][:], ALU.add).then_inc(S["h_made"], 1)
        m.clear_semaphores()


def phase_block_attention(nc, dram, H, flatT, logits, ident, NB):
    NH, HD, NKV = 4, 16, 2
    NE = dram["router"].shape[1]
    KV = HD + 1
    NG = NB // GB
    SLOTS = 2
    with ExitStack() as ctx:
        m = Mem(nc, ctx)
        wq = m.sb("f_wq", [D, P])
        wk = m.sb("f_wk", [D, P])
        wkp = m.sb("f_wkp", [D, P])
        wv = m.sb("f_wv", [D, NKV * HD])
        wo = m.sb("f_wo", [D, D])
        ln1 = m.sb("f_ln1", [D, 1])
        ln2 = m.sb("f_ln2", [D, 1])
        router = m.sb("f_router", [D, NE])
        rope_q = m.sb("rope_q", [P, P])
        cos_k = m.sb("cos_k", [P, P])
        sin_k = m.sb("sin_k", [P, P])
        hide_f = m.sb("hide_f", [P, P])
        hide = m.sb("hide", [P, P], BF16)
        ident_b = m.sb("ident_b", [P, P], BF16)

        def slots(name, shape):
            return [m.sb(f"{name}{u}", shape) for u in range(SLOTS)]

        st, mv = slots("b_st", [P, GB, 6]), slots("b_mv", [P, GB, 2])
        rstd, msq, rms = slots("b_rstd", [P, GB]), slots("b_msq", [P, GB]), slots("b_rms", [P, GB])
        x, xn, xT = slots("b_x", [P, GB, D]), slots("b_xn", [P, GB, D]), slots("b_xT", [D, W])
        q, k0, k1 = slots("b_q", [P, W]), slots("b_k0", [P, W]), slots("b_k1", [P, W])
        v = slots("b_v", [P, GB, NKV, KV])
        mx = slots("b_mx", [P, NH, GB])
        pr, pT = slots("b_pr", [P, NH, W]), slots("b_pT", [P, NH, W])
        inv = slots("b_inv", [P, GB * NH])
        y, yT = slots("b_y", [P, GB, D]), slots("b_yT", [D, W])
        x2, sq, ss = slots("b_x2", [P, GB, D]), slots("b_sq", [P, GB, D]), slots("b_ss", [P, GB])
        fl, flT = slots("b_fl", [P, GB, 2, D]), slots("b_flT", [P, W])
        bank = [[m.ps(f"b_bk{u}{k}", [P, 512]) for k in range(4)] for u in range(SLOTS)]

        passed = m.sem("b_passed")
        loaded = m.sem("b_loaded")
        ready = m.sem("b_ready")
        S = Signals(m, "b", SLOTS,
                    gpsimd="xn_made k_made h_made flat_made flatT_kept",
                    tensor="x_turned q_made k0_made k1_made v_made scored*4 p_turned*4 attended y_turned "
                           "out_made flat_turned routed",
                    scalar="log_var rstd_made log_msq rms_made xT_kept v_kept p_exp*4 pT_kept*2 yT_kept "
                           "log_ss rms2_made flT_kept logits_kept",
                    vector="stats moments rstd_sq msq_made centred q_kept k0_kept k1_kept max_made*4 shifted*4 "
                           "pT_copied*2 inv_sum y_made x2_made squared summed")
        LOADS, READY = 12, 12

        with nc.Block() as block:
            @block.sync
            def _(sp):
                for dst, name in ((wq, "f_wq"), (wk, "f_wk"), (wkp, "f_wkp"), (wv, "f_wv"), (wo, "f_wo"),
                                  (ln1, "f_ln1"), (ln2, "f_ln2"), (router, "router"), (rope_q, "rope_q"),
                                  (cos_k, "cos_k"), (sin_k, "sin_k"), (hide_f, "hide")):
                    sp.dma_start(dst[:], dram[name]).then_inc(loaded, 16)

            @block.gpsimd
            def _(pool):
                S.start(pool, "gpsimd")
                pool.wait_ge(ready, READY)
                with pool.Fori(0, NG // SLOTS) as i:
                    for u in range(SLOTS):
                        n = i * SLOTS + u
                        pool.wait_ge(S["rms_made"], S.now(n))
                        pool.wait_ge(S["centred"], S.now(n))
                        pool.wait_ge(S["x_turned"], S.past(n))
                        pool.tensor_tensor(xn[u][:], x[u][:], over(rms[u][:], D), ALU.mult).then_inc(S["xn_made"], 1)
                    for u in range(SLOTS):
                        n = i * SLOTS + u
                        pool.wait_ge(S["k0_kept"], S.now(n))
                        pool.wait_ge(S["k1_kept"], S.now(n))
                        pool.tensor_tensor(k0[u][:], k0[u][:], k1[u][:], ALU.add).then_inc(S["k_made"], 1)
                    for u in range(SLOTS):
                        n = i * SLOTS + u
                        pool.wait_ge(S["x2_made"], S.now(n))
                        hs = H[:, bass.ds(n * GB, GB), :]
                        pool.tensor_tensor(hs, hs, x2[u][:], ALU.add).then_inc(S["h_made"], 1)
                    for u in range(SLOTS):
                        n = i * SLOTS + u
                        pool.wait_ge(S["rms2_made"], S.now(n))
                        pool.wait_ge(S["flat_turned"], S.past(n))
                        for half in range(2):
                            last = pool.tensor_tensor(fl[u][:, :, half, :], x2[u][:], over(ss[u][:], D), ALU.mult)
                        last.then_inc(S["flat_made"], 1)
                    for u in range(SLOTS):
                        n = i * SLOTS + u
                        pool.wait_ge(S["flT_kept"], S.now(n))
                        pool.sem_inc(passed, 1)
                        pool.tensor_copy(flatT[:, bass.ds(n * W, W)], flT[u][:]).then_inc(S["flatT_kept"], 1)

            @block.tensor
            def _(pe):
                S.start(pe, "tensor")
                pe.wait_ge(ready, READY)
                with pe.Fori(0, NG // SLOTS) as i:
                    for u in range(SLOTS):
                        n, bk = i * SLOTS + u, bank[u]
                        pe.wait_ge(S["xn_made"], S.now(n))
                        pe.wait_ge(S["logits_kept"], S.past(n))
                        pe.sem_inc(passed, 1)
                        for b in range(GB):
                            last = nc.tensor.transpose(bk[0][0:D, b * P:(b + 1) * P], xn[u][:, b, :], ident[:])
                        last.then_inc(S["x_turned"], 1)
                    for u in range(SLOTS):
                        n, bk = i * SLOTS + u, bank[u]
                        pe.wait_ge(S["xT_kept"], S.now(n))
                        pe.wait_ge(S["yT_kept"], S.past(n))
                        pe.wait_ge(S["x2_made"], S.past(n))
                        pe.wait_ge(S["flT_kept"], S.past(n))
                        nc.tensor.matmul(bk[1][:], wq[:], xT[u][:], start=True, stop=True).then_inc(S["q_made"], 1)
                        nc.tensor.matmul(bk[2][:], wk[:], xT[u][:], start=True, stop=True).then_inc(S["k0_made"], 1)
                        nc.tensor.matmul(bk[3][:], wkp[:], xT[u][:], start=True, stop=True).then_inc(S["k1_made"], 1)
                        for b in range(GB):
                            last = nc.tensor.matmul(bk[0][:, b * NKV * HD:(b + 1) * NKV * HD],
                                                    xT[u][:, b * P:(b + 1) * P], wv[:], start=True, stop=True)
                        last.then_inc(S["v_made"], 1)
                    for u in range(SLOTS):
                        n, bk = i * SLOTS + u, bank[u]
                        pe.wait_ge(S["q_kept"], S.now(n))
                        pe.wait_ge(S["k_made"], S.now(n))
                        pe.wait_ge(S["v_kept"], S.now(n))
                        for h in range(NH):
                            nc.tensor.matmul(bk[h][:], ident_b[:], hide[:, None, :].to_broadcast([P, GB, P]),
                                             start=True, stop=False)
                            r = slice(32 * h, 32 * h + 32)
                            for b in range(GB):
                                c = slice(b * P, (b + 1) * P)
                                last = nc.tensor.matmul(bk[h][:, c], q[u][r, c], k0[u][r, c], start=False,
                                                        stop=(b == GB - 1))
                            last.then_inc(S["scored"][h], 1)
                    for u in range(SLOTS):
                        n, bk = i * SLOTS + u, bank[u]
                        for h in range(NH):
                            pe.wait_ge(S["p_exp"][h], S.now(n))
                            for b in range(GB):
                                c = slice(b * P, (b + 1) * P)
                                last = nc.tensor.transpose(bk[h][:, c], pr[u][:, h, c], ident[:])
                            last.then_inc(S["p_turned"][h], 1)
                    for u in range(SLOTS):
                        n, bk = i * SLOTS + u, bank[u]
                        for h in range(2):
                            pe.wait_ge(S["pT_kept"][h], S.now(n))
                            pe.wait_ge(S["pT_copied"][h], S.now(n))
                        for b in range(GB):
                            for h in range(NH):
                                o = (b * NH + h) * KV
                                last = nc.tensor.matmul(bk[0][:, o:o + KV], pT[u][:, h, b * P:(b + 1) * P],
                                                        v[u][:, b, h * NKV // NH, :], start=True, stop=True)
                        last.then_inc(S["attended"], 1)
                    for u in range(SLOTS):
                        n, bk = i * SLOTS + u, bank[u]
                        pe.wait_ge(S["y_made"], S.now(n))
                        pe.sem_inc(passed, 1)
                        for b in range(GB):
                            last = nc.tensor.transpose(bk[1][0:D, b * P:(b + 1) * P], y[u][:, b, :], ident[:])
                        last.then_inc(S["y_turned"], 1)
                    for u in range(SLOTS):
                        n, bk = i * SLOTS + u, bank[u]
                        pe.wait_ge(S["yT_kept"], S.now(n))
                        for b in range(GB):
                            last = nc.tensor.matmul(bk[2][:, b * D:(b + 1) * D], yT[u][:, b * P:(b + 1) * P], wo[:],
                                                    start=True, stop=True)
                        last.then_inc(S["out_made"], 1)
                    for u in range(SLOTS):
                        n, bk = i * SLOTS + u, bank[u]
                        pe.wait_ge(S["flat_made"], S.now(n))
                        pe.sem_inc(passed, 1)
                        for b in range(GB):
                            last = nc.tensor.transpose(bk[3][:, b * P:(b + 1) * P],
                                                       fl[u][:, b].rearrange("p k d -> p (k d)"), ident[:])
                        last.then_inc(S["flat_turned"], 1)
                    for u in range(SLOTS):
                        n, bk = i * SLOTS + u, bank[u]
                        pe.wait_ge(S["flT_kept"], S.now(n))
                        for b in range(GB):
                            last = nc.tensor.matmul(bk[0][:, b * NE:(b + 1) * NE], flT[u][0:D, b * P:(b + 1) * P],
                                                    router[:], start=True, stop=True)
                        last.then_inc(S["routed"], 1)

            @block.scalar
            def _(act):
                S.start(act, "scalar")
                act.preload_act_table_set("natural_log_exp_and_others")
                act.wait_ge(ready, READY)
                with act.Fori(0, NG // SLOTS) as i:
                    for u in range(SLOTS):
                        n = i * SLOTS + u
                        act.wait_ge(S["moments"], S.now(n))
                        act.wait_ge(S["centred"], S.past(n))
                        nc.scalar.activation(rstd[u][:], mv[u][:, :, 1], ACT.Ln, bias=1e-5).then_inc(S["log_var"], 1)
                    for u in range(SLOTS):
                        n = i * SLOTS + u
                        act.wait_ge(S["log_var"], S.now(n))
                        nc.scalar.activation(rstd[u][:], rstd[u][:], ACT.Exp, scale=-0.5).then_inc(S["rstd_made"], 1)
                    for u in range(SLOTS):
                        n = i * SLOTS + u
                        act.wait_ge(S["msq_made"], S.now(n))
                        act.wait_ge(S["xn_made"], S.past(n))
                        nc.scalar.activation(rms[u][:], msq[u][:], ACT.Ln, bias=1e-6).then_inc(S["log_msq"], 1)
                    for u in range(SLOTS):
                        n = i * SLOTS + u
                        act.wait_ge(S["log_msq"], S.now(n))
                        nc.scalar.activation(rms[u][:], rms[u][:], ACT.Exp, scale=-0.5).then_inc(S["rms_made"], 1)
                    for u in range(SLOTS):
                        n, bk = i * SLOTS + u, bank[u]
                        act.wait_ge(S["x_turned"], S.now(n))
                        act.wait_ge(S["v_made"], S.past(n))
                        nc.scalar.activation(xT[u][:], bk[0][0:D, :], ACT.Copy).then_inc(S["xT_kept"], 1)
                    for u in range(SLOTS):
                        n, bk = i * SLOTS + u, bank[u]
                        act.wait_ge(S["v_made"], S.now(n))
                        act.wait_ge(S["attended"], S.past(n))
                        nc.scalar.activation(v[u][:].rearrange("p b k e -> p (b k) e")[:, :, 0:HD],
                                             grouped(bk[0][:, 0:GB * NKV * HD], HD), ACT.Copy).then_inc(S["v_kept"], 1)
                    for u in range(SLOTS):
                        n, bk = i * SLOTS + u, bank[u]
                        for h in range(NH):
                            act.wait_ge(S["shifted"][h], S.now(n))
                            nc.scalar.activation(pr[u][:, h, :], pr[u][:, h, :], ACT.Exp).then_inc(S["p_exp"][h], 1)
                    for u in range(SLOTS):
                        n, bk = i * SLOTS + u, bank[u]
                        act.wait_ge(S["attended"], S.past(n))
                        for h in range(2):
                            act.wait_ge(S["p_turned"][h], S.now(n))
                            nc.scalar.activation(pT[u][:, h, :], bk[h][:], ACT.Copy).then_inc(S["pT_kept"][h], 1)
                    for u in range(SLOTS):
                        n, bk = i * SLOTS + u, bank[u]
                        act.wait_ge(S["y_turned"], S.now(n))
                        act.wait_ge(S["out_made"], S.past(n))
                        nc.scalar.activation(yT[u][:], bk[1][0:D, :], ACT.Copy).then_inc(S["yT_kept"], 1)
                    for u in range(SLOTS):
                        n = i * SLOTS + u
                        act.wait_ge(S["summed"], S.now(n))
                        nc.scalar.activation(ss[u][:], ss[u][:], ACT.Ln, scale=1.0 / D, bias=1e-6)\
                            .then_inc(S["log_ss"], 1)
                    for u in range(SLOTS):
                        n = i * SLOTS + u
                        act.wait_ge(S["log_ss"], S.now(n))
                        nc.scalar.activation(ss[u][:], ss[u][:], ACT.Exp, scale=-0.5).then_inc(S["rms2_made"], 1)
                    for u in range(SLOTS):
                        n, bk = i * SLOTS + u, bank[u]
                        act.wait_ge(S["flat_turned"], S.now(n))
                        act.wait_ge(S["routed"], S.past(n))
                        act.wait_ge(S["flatT_kept"], S.past(n))
                        nc.scalar.activation(flT[u][:], bk[3][:], ACT.Copy).then_inc(S["flT_kept"], 1)
                    for u in range(SLOTS):
                        n, bk = i * SLOTS + u, bank[u]
                        act.wait_ge(S["routed"], S.now(n))
                        nc.scalar.activation(logits[:, bass.ds(n * GB, GB), :], grouped(bk[0][:, 0:GB * NE], NE),
                                             ACT.Copy).then_inc(S["logits_kept"], 1)

            @block.vector
            def _(dve):
                S.start(dve, "vector")
                dve.wait_ge(loaded, 16 * LOADS)
                for w, g in ((wq, ln1), (wk, ln1), (wkp, ln1), (wv, ln1), (router, ln2)):
                    nc.vector.tensor_scalar(w[:], w[:], g[:, 0:1], None, ALU.mult).then_inc(ready, 1)
                nc.vector.tensor_copy(hide[:], hide_f[:]).then_inc(ready, 1)
                nc.vector.tensor_copy(ident_b[:], ident[:]).then_inc(ready, 1)
                for u in range(SLOTS):
                    nc.vector.memset(v[u][:, :, :, HD:KV], 1.0).then_inc(ready, 1)
                nc.vector.memset(inv[0][:], 0.0).then_inc(ready, 1)
                nc.vector.memset(inv[1][:], 0.0).then_inc(ready, 1)
                nc.vector.memset(ss[0][:], 0.0).then_inc(ready, 1)
                dve.wait_ge(ready, READY)
                with dve.Fori(0, NG // SLOTS) as i:
                    for u in range(SLOTS):
                        n = i * SLOTS + u
                        dve.wait_ge(S["x2_made"], S.past(n))
                        for b in range(GB):
                            last = nc.vector.bn_stats(
                                st[u][:, b, :], H[:, bass.ds(n * GB + b, 1), :].rearrange("p b d -> p (b d)"))
                        last.then_inc(S["stats"], 1)
                    for u in range(SLOTS):
                        n = i * SLOTS + u
                        dve.wait_ge(S["stats"], S.now(n))
                        dve.sem_inc(passed, 1)
                        for b in range(GB):
                            last = nc.vector.bn_aggr(mv[u][:, b, :], st[u][:, b, :])
                        last.then_inc(S["moments"], 1)
                    for u in range(SLOTS):
                        n = i * SLOTS + u
                        dve.wait_ge(S["rstd_made"], S.now(n))
                        nc.vector.tensor_tensor(msq[u][:], rstd[u][:], rstd[u][:], ALU.mult).then_inc(S["rstd_sq"], 1)
                    for u in range(SLOTS):
                        n = i * SLOTS + u
                        dve.wait_ge(S["rstd_sq"], S.now(n))
                        nc.vector.tensor_tensor(msq[u][:], msq[u][:], mv[u][:, :, 1], ALU.mult)\
                            .then_inc(S["msq_made"], 1)
                    for u in range(SLOTS):
                        n = i * SLOTS + u
                        dve.wait_ge(S["xn_made"], S.past(n))
                        for b in range(GB):
                            last = nc.vector.tensor_scalar(
                                x[u][:, b, :], H[:, bass.ds(n * GB + b, 1), :].rearrange("p b d -> p (b d)"),
                                mv[u][:, b, 0:1], rstd[u][:, b:b + 1], ALU.subtract, ALU.mult)
                        last.then_inc(S["centred"], 1)
                    for u in range(SLOTS):
                        n, bk = i * SLOTS + u, bank[u]
                        for dst, src, table, made, kept in ((q, 1, rope_q, S["q_made"], S["q_kept"]),
                                                            (k0, 2, cos_k, S["k0_made"], S["k0_kept"]),
                                                            (k1, 3, sin_k, S["k1_made"], S["k1_kept"])):
                            dve.wait_ge(made, S.now(n))
                            dve.wait_ge(S["scored"][NH - 1], S.past(n))
                            nc.vector.tensor_tensor(grouped(dst[u][:], P), grouped(bk[src][:], P),
                                                    table[:, None, :].to_broadcast([P, GB, P]), ALU.mult)\
                                .then_inc(kept, 1)
                    for u in range(SLOTS):
                        n, bk = i * SLOTS + u, bank[u]
                        for h in range(NH):
                            dve.wait_ge(S["scored"][h], S.now(n))
                            nc.vector.tensor_reduce(mx[u][:, h, :], grouped(bk[h][:], P), AX, ALU.max)\
                                .then_inc(S["max_made"][h], 1)
                    for u in range(SLOTS):
                        n, bk = i * SLOTS + u, bank[u]
                        for h in range(NH):
                            dve.wait_ge(S["max_made"][h], S.now(n))
                            dve.wait_ge(S["p_turned"][h], S.past(n))
                            nc.vector.tensor_tensor(grouped(pr[u][:, h, :], P), grouped(bk[h][:], P),
                                                    over(mx[u][:, h, :], P), ALU.subtract)\
                                .then_inc(S["shifted"][h], 1)
                    for u in range(SLOTS):
                        n, bk = i * SLOTS + u, bank[u]
                        for h in range(2):
                            dve.wait_ge(S["p_turned"][2 + h], S.now(n))
                            dve.wait_ge(S["attended"], S.past(n))
                            nc.vector.tensor_copy(pT[u][:, 2 + h, :], bk[2 + h][:]).then_inc(S["pT_copied"][h], 1)
                    for u in range(SLOTS):
                        n, bk = i * SLOTS + u, bank[u]
                        dve.wait_ge(S["attended"], S.now(n))
                        nc.vector.reciprocal(inv[u][:], grouped(bk[0][:, 0:GB * NH * KV], KV)[:, :, HD])\
                            .then_inc(S["inv_sum"], 1)
                    for u in range(SLOTS):
                        n, bk = i * SLOTS + u, bank[u]
                        dve.wait_ge(S["inv_sum"], S.now(n))
                        dve.wait_ge(S["y_turned"], S.past(n))
                        nc.vector.tensor_tensor(grouped(y[u][:].rearrange("p b d -> p (b d)"), HD),
                                                grouped(bk[0][:, 0:GB * NH * KV], KV)[:, :, 0:HD],
                                                over(inv[u][:], HD), ALU.mult).then_inc(S["y_made"], 1)
                    for u in range(SLOTS):
                        n, bk = i * SLOTS + u, bank[u]
                        dve.wait_ge(S["out_made"], S.now(n))
                        dve.wait_ge(S["h_made"], S.past(n))
                        dve.wait_ge(S["flat_made"], S.past(n))
                        nc.vector.tensor_tensor(x2[u][:], grouped(bk[2][:, 0:GB * D], D), x[u][:], ALU.add)\
                            .then_inc(S["x2_made"], 1)
                    for u in range(SLOTS):
                        n = i * SLOTS + u
                        dve.wait_ge(S["x2_made"], S.now(n))
                        nc.vector.tensor_tensor(sq[u][:], x2[u][:], x2[u][:], ALU.mult).then_inc(S["squared"], 1)
                    for u in range(SLOTS):
                        n = i * SLOTS + u
                        dve.wait_ge(S["squared"], S.now(n))
                        nc.vector.tensor_reduce(ss[u][:], sq[u][:], AX, ALU.add).then_inc(S["summed"], 1)
        m.clear_semaphores()


def phase_experts(nc, dram, H, flatT, logits, ident, NB):
    NE = dram["router"].shape[1]
    NCH = dram["e_w1"].shape[1] // P
    PARTS = 3
    NG = NB // GB
    SLOTS = 2
    PER = SLOTS * NCH
    with ExitStack() as ctx:
        m = Mem(nc, ctx)
        w1 = m.sb("e_w1", [P, NCH * P])
        w3 = m.sb("e_w3", [P, NCH * P])
        w1_parts = [m.sb(f"e_w1_{name}", [P, NCH * P], BF16) for name in ("hh", "mm", "lh")]
        w3_parts = [m.sb(f"e_w3_{name}", [P, NCH * P], BF16) for name in ("hh", "mm", "lh")]
        x_hm = [m.sb(f"x_hm{u}", [P, W], BF16) for u in range(SLOTS)]
        x_hl = [m.sb(f"x_hl{u}", [P, W], BF16) for u in range(SLOTS)]
        x_rest = m.sb("x_rest", [P, W])
        w2 = m.sb("e_w2", [P, NCH, D])
        ln2 = m.sb("e_ln2", [P, 1])
        owner_f = m.sb("owner_f", [PARTS * NE, NCH * P])
        owner = m.sb("owner", [PARTS * NE, NCH * P], BF16)
        rank = m.sb("rank", [P, NE])
        wts = m.sb("wts", [P, NB + GB, PARTS, NE])
        ex = m.sb("ex", [P, NB, NE])
        tie = m.sb("tie", [P, NB, NE])
        pick = m.sb("pick", [P, NB, NE])
        both = m.sb("both", [P, NB, NE])
        low = m.sb("low", [P, NB, NE], BF16)
        top = m.sb("top", [P, NB])
        total = m.sb("total", [P, NB])
        wnow = [m.sb(f"wnow{u}", [P, GB, PARTS * NE]) for u in range(SLOTS)]
        wT = [m.sb(f"wT{u}", [PARTS * NE, W], BF16) for u in range(SLOTS)]
        act1 = [m.sb(f"act1{u}", [P, W]) for u in range(SLOTS)]
        prod = [m.sb(f"prod{u}", [P, W]) for u in range(SLOTS)]
        hid = [m.sb(f"hid{u}", [P, W]) for u in range(SLOTS)]
        b1 = [m.ps(f"c_h1{u}", [P, 512]) for u in range(SLOTS)]
        b3 = [m.ps(f"c_h3{u}", [P, 512]) for u in range(SLOTS)]
        bw = [m.ps(f"c_wb{u}", [P, 512]) for u in range(SLOTS)]
        bo = m.ps("c_out", [P, 512])
        bt = m.ps("c_turn", [P, 512])

        passed = m.sem("c_passed")
        loaded = m.sem("c_loaded")
        ready = m.sem("c_ready")
        shifted = m.sem("c_shifted")
        exped = m.sem("c_exped")
        route = m.sem("c_route")
        split = m.sem("c_split")
        parted = m.sem("c_parted")
        S = Signals(m, "c", SLOTS, tensor="h1_made h3_made wb_made summed", scalar="activated",
                    vector="multiplied weighted")
        G = Signals(m, "cg", SLOTS, tensor="w_turned", scalar="w_staged wT_kept high_kept mid_kept high2_kept",
                    vector="h_made", gpsimd="rest_made low_made")
        LOADS = 6
        READY = 7
        LAG = 2
        TURNS = NG // SLOTS
        assert NG % SLOTS == 0 and TURNS > 1
        ROUTE = 18 + 2 * PARTS

        with nc.Block() as block:
            @block.sync
            def _(sp):
                for dst, name in ((w1, "e_w1"), (w3, "e_w3"), (ln2, "e_ln2"), (owner_f, "owner"), (rank, "rank")):
                    sp.dma_start(dst[:], dram[name]).then_inc(loaded, 16)
                sp.dma_start(w2[:], dram["e_w2"].rearrange("(c p) n -> p c n", p=P)).then_inc(loaded, 16)

            def pipeline(eng, body, prepare):
                for k in range(NCH):
                    prepare(0, 0, k)
                for k in range(PER):
                    body(0, k, 0, PER)
                    prepare(k // NCH + 1, (k // NCH + 1) % SLOTS, k % NCH)
                with eng.Fori(1, TURNS) as i:
                    for k in range(PER):
                        body(i, k, -PER, PER)
                        prepare(i * SLOTS + k // NCH + 1, (k // NCH + 1) % SLOTS, k % NCH)
                for k in range(LAG + 1):
                    body(TURNS, k, -PER, 0)

            @block.gpsimd
            def _(pool):
                G.start(pool, "gpsimd")
                nc.gpsimd.memset(flatT[:, NB * P:NB * P + W], 0.0).then_inc(ready, 1)
                pool.wait_ge(ready, READY)

                def prepare(n, s, k):
                    if k == 1:
                        pool.wait_ge(G["high_kept"], G.now(n))
                        pool.wait_ge(G["low_made"], G.before(n))
                        pool.tensor_tensor(x_rest[D:P, :], flatT[D:P, bass.ds(n * W, W)], x_hm[s][D:P, :],
                                           ALU.subtract).then_inc(G["rest_made"], 1)
                    if k == 3:
                        pool.wait_ge(G["mid_kept"], G.now(n))
                        pool.tensor_tensor(x_hl[s][D:P, :], x_rest[D:P, :], x_hm[s][D:P, :], ALU.subtract)\
                            .then_inc(G["low_made"], 1)

                pipeline(pool, lambda i, k, lo, hi: None, prepare)

            @block.tensor
            def _(pe):
                S.start(pe, "tensor")
                G.start(pe, "tensor")
                pe.wait_ge(ready, READY)

                def prepare(n, s, k):
                    if k == 6:
                        pe.wait_ge(G["w_staged"], G.now(n))
                        pe.wait_ge(G["wT_kept"], G.before(n))
                        for b in range(GB):
                            last = nc.tensor.transpose(bt[0:PARTS * NE, b * P:(b + 1) * P], wnow[s][:, b, :],
                                                       ident[:])
                        last.then_inc(G["w_turned"], 1)

                def product(out, parts, cols, s):
                    for j, (w, x) in enumerate(zip(parts, (x_hm[s], x_hm[s], x_hl[s]))):
                        last = nc.tensor.matmul(out[:], w[:, cols], x[:], start=(j == 0), stop=(j == 2))
                    return last

                def body(i, k, lo, hi):
                    q, u, n = i * PER + k, k % SLOTS, i * SLOTS + k // NCH
                    if lo <= k < hi:
                        c, s = k % NCH, k // NCH
                        cols = slice(c * P, (c + 1) * P)
                        if c == 0:
                            pe.wait_ge(G["low_made"], G.now(n))
                            pe.wait_ge(G["high2_kept"], G.now(n))
                            pe.wait_ge(G["wT_kept"], G.now(n))
                        pe.wait_ge(S["activated"], S.past(q))
                        product(b1[u], w1_parts, cols, s).then_inc(S["h1_made"], 1)
                        pe.wait_ge(S["multiplied"], S.past(q))
                        product(b3[u], w3_parts, cols, s).then_inc(S["h3_made"], 1)
                        pe.wait_ge(S["weighted"], S.past(q))
                        nc.tensor.matmul(bw[u][:], owner[:, cols], wT[s][:], start=True, stop=True)\
                            .then_inc(S["wb_made"], 1)
                    if lo <= k - LAG < hi:
                        c = (k - LAG) % NCH
                        if c == 0:
                            pe.wait_ge(G["h_made"], G.before(n))
                        pe.wait_ge(S["weighted"], S.ago(q, LAG))
                        for b in range(GB):
                            last = nc.tensor.matmul(bo[:, b * D:(b + 1) * D], hid[u][:, b * P:(b + 1) * P], w2[:, c, :],
                                                    start=(c == 0 and b == 0), stop=(c == NCH - 1 and b == GB - 1))
                        last.then_inc(S["summed"], 1)

                pipeline(pe, body, prepare)

            @block.scalar
            def _(act):
                S.start(act, "scalar")
                act.preload_act_table_set("natural_log_exp_and_others")
                G.start(act, "scalar")
                act.wait_ge(shifted, 1)
                nc.scalar.activation(ex[:], ex[:], ACT.Exp).then_inc(exped, 1)
                act.preload_act_table_set("silu_and_others")
                act.wait_ge(ready, READY)
                act.wait_ge(route, ROUTE)

                def prepare(n, s, k):
                    x = flatT[:, bass.ds(n * W, W)]
                    if k == 1:
                        if not isinstance(n, int) or n >= SLOTS:
                            act.wait_ge(S["wb_made"], S.now(n * NCH - NCH - 1))
                        nc.scalar.activation(x_hm[s][:], x, ACT.Copy).then_inc(G["high_kept"], 1)
                    if k == 2:
                        nc.scalar.activation(x_hl[s][0:D, :], flatT[0:D, bass.ds(n * W, W)], ACT.Copy)\
                            .then_inc(G["high2_kept"], 1)
                    if k == 3:
                        act.wait_ge(G["rest_made"], G.now(n))
                        nc.scalar.activation(x_hm[s][D:P, :], x_rest[D:P, :], ACT.Copy).then_inc(G["mid_kept"], 1)
                    if k == 4:
                        act.wait_ge(G["w_turned"], G.past(n))
                        nc.scalar.activation(wnow[s][:], wts[:, bass.ds(n * GB, GB)].rearrange("p b k e -> p b (k e)"),
                                             ACT.Copy).then_inc(G["w_staged"], 1)
                    if k == 7:
                        act.wait_ge(G["w_turned"], G.now(n))
                        nc.scalar.activation(wT[s][:], bt[0:PARTS * NE, :], ACT.Copy).then_inc(G["wT_kept"], 1)

                def body(i, k, lo, hi):
                    q, u = i * PER + k, k % SLOTS
                    if lo <= k < hi:
                        act.wait_ge(S["h1_made"], S.now(q))
                        act.wait_ge(S["multiplied"], S.past(q))
                        nc.scalar.activation(act1[u][:], b1[u][:], ACT.Silu).then_inc(S["activated"], 1)

                pipeline(act, body, prepare)

            @block.vector
            def _(dve):
                S.start(dve, "vector")
                G.start(dve, "vector")
                nc.vector.memset(wts[:, NB:NB + GB], 0.0).then_inc(ready, 1)
                dve.wait_ge(loaded, 16 * LOADS)
                made = [0]

                def cut(ins):
                    made[0] += 1
                    ins.then_inc(split, 1)
                    dve.wait_ge(split, made[0])

                for w, (hh, mm, lh) in ((w1, w1_parts), (w3, w3_parts)):
                    cut(nc.vector.tensor_scalar(w[:], w[:], ln2[:, 0:1], None, ALU.mult))
                    cut(nc.vector.tensor_copy(hh[:], w[:]))
                    cut(nc.vector.tensor_tensor(w[:], w[:], hh[:], ALU.subtract))
                    cut(nc.vector.tensor_copy(mm[:], w[:]))
                    nc.vector.tensor_tensor(lh[0:D, :], w[0:D, :], mm[0:D, :], ALU.subtract).then_inc(ready, 1)
                    nc.vector.tensor_copy(lh[D:P, :], hh[D:P, :]).then_inc(ready, 1)
                nc.vector.tensor_copy(owner[:], owner_f[:]).then_inc(ready, 1)
                steps = [0]

                def step(ins):
                    steps[0] += 1
                    ins.then_inc(route, 1)
                    dve.wait_ge(route, steps[0])

                ranks = rank[:, None, :].to_broadcast([P, NB, NE])
                step(nc.vector.tensor_reduce(top[:], logits[:], AX, ALU.max))
                nc.vector.tensor_tensor(ex[:], logits[:], over(top[:], NE), ALU.subtract).then_inc(shifted, 1)
                step(nc.vector.tensor_tensor(tie[:], logits[:], over(top[:], NE), ALU.is_equal))
                step(nc.vector.tensor_tensor(tie[:], tie[:], ranks, ALU.mult))
                step(nc.vector.tensor_reduce(top[:], tie[:], AX, ALU.max))
                step(nc.vector.tensor_tensor(both[:], tie[:], over(top[:], NE), ALU.is_equal))
                step(nc.vector.scalar_tensor_tensor(pick[:], both[:], -1e30, logits[:], ALU.mult, ALU.add))
                step(nc.vector.tensor_reduce(top[:], pick[:], AX, ALU.max))
                step(nc.vector.tensor_tensor(tie[:], pick[:], over(top[:], NE), ALU.is_equal))
                step(nc.vector.tensor_tensor(tie[:], tie[:], ranks, ALU.mult))
                step(nc.vector.tensor_reduce(top[:], tie[:], AX, ALU.max))
                step(nc.vector.tensor_tensor(pick[:], tie[:], over(top[:], NE), ALU.is_equal))
                step(nc.vector.tensor_tensor(both[:], both[:], pick[:], ALU.add))
                dve.wait_ge(exped, 1)
                step(nc.vector.tensor_reduce(total[:], ex[:], AX, ALU.add))
                step(nc.vector.tensor_tensor(ex[:], ex[:], both[:], ALU.mult))
                step(nc.vector.tensor_reduce(top[:], ex[:], AX, ALU.add))
                step(nc.vector.scalar_tensor_tensor(top[:], total[:], 1e-9, top[:], ALU.mult, ALU.add))
                step(nc.vector.reciprocal(top[:], top[:]))
                step(nc.vector.tensor_tensor(ex[:], ex[:], over(top[:], NE), ALU.mult))
                for k in range(PARTS):
                    step(nc.vector.tensor_copy(low[:], ex[:]))
                    if k < PARTS - 1:
                        step(nc.vector.tensor_tensor(ex[:], ex[:], low[:], ALU.subtract))
                    copied = nc.vector.tensor_copy(wts[:, 0:NB, k, :], low[:])
                    if k < PARTS - 1:
                        copied.then_inc(parted, 1)
                        dve.wait_ge(parted, 1 + k)
                    else:
                        step(copied)
                assert steps[0] == ROUTE

                def body(i, k, lo, hi):
                    q, u, n = i * PER + k, k % SLOTS, i * SLOTS + k // NCH
                    if k % NCH == LAG and lo <= k - LAG - 1 < hi:
                        dve.wait_ge(S["summed"], S.ago(q, LAG + 1))
                        hs = H[:, bass.ds(n * GB - GB, GB), :]
                        nc.vector.tensor_tensor(hs, grouped(bo[:, 0:GB * D], D), hs, ALU.add).then_inc(G["h_made"], 1)
                    if lo <= k < hi:
                        dve.wait_ge(S["h3_made"], S.now(q))
                        dve.wait_ge(S["activated"], S.now(q))
                        dve.wait_ge(S["weighted"], S.past(q))
                        nc.vector.tensor_tensor(prod[u][:], b3[u][:], act1[u][:], ALU.mult).then_inc(S["multiplied"], 1)
                    if lo <= k - 1 < hi:
                        v = (k - 1) % SLOTS
                        dve.wait_ge(S["wb_made"], S.before(q))
                        dve.wait_ge(S["multiplied"], S.before(q))
                        dve.wait_ge(S["summed"], S.ago(q, 1 + SLOTS))
                        nc.vector.tensor_tensor(hid[v][:], bw[v][:], prod[v][:], ALU.mult).then_inc(S["weighted"], 1)

                pipeline(dve, body, lambda n, s, k: None)
        m.clear_semaphores()


def phase_decay_attention(nc, dram, H, ident, NB):
    HD = 8
    NH = 8
    STRIP = 32
    QUAD = P // STRIP
    TAPS = dram["d_conv"].shape[1]
    PADT = TAPS - 1
    KX = D + 1
    GQ = NH
    NQ = NB // GB * GQ
    SLOTS = 4
    TURN = 2 * GQ
    AGAIN = (5,9,7,2,2,2,2,7)
    LAG_SCAN, LAG_DECAY, LAG_WEIGH, LAG_EXP2, LAG_TURN, LAG_PV, LAG_KEEP, LAG_Y = 1, 2, 3, 4, 5, 6, 7, 8
    with ExitStack() as ctx:
        m = Mem(nc, ctx)
        conv = m.sb("d_conv", [KX, TAPS, D])
        beta = m.sb("d_beta", [KX, D])
        keep = m.sb("d_keep", [KX, D])
        diag = m.sb("d_diag", [D, D])
        NW = 4 * P + D
        win = m.sb("d_win", [KX, NW])
        lnw = m.sb("d_lnw", [KX, 1])
        lnb = m.sb("d_lnb", [D, KX])
        wout = m.sb("d_wout", [KX, D])
        gam = m.sb("d_gam", [P, NH])
        gab = m.sb("d_gab", [P, NH])
        gsq = m.sb("d_gsq", [P, NH])
        pos = m.sb("d_pos", [P, W])
        cont = m.sb("d_cont", [P, W])
        hide_f = m.sb("d_hide_f", [P, P])
        hide = m.sb("d_hide", [P, P], BF16)
        ident_b = m.sb("d_ident_b", [P, P], BF16)
        notfirst = m.sb("d_notfirst", [P, 1])

        st, mv, rstd = m.sb("d_st", [P, GB, 6]), m.sb("d_mv", [P, GB, 2]), m.sb("d_rstd", [P, GB])
        st2, mv2, rstd2 = m.sb("d_st2", [P, GB, 6]), m.sb("d_mv2", [P, GB, 2]), m.sb("d_rstd2", [P, GB])
        xn, hn = m.sb("d_xn", [P, GB, D]), m.sb("d_hn", [P, GB, D])
        xT = m.sb("d_xT", [KX, GB, PADT + P])
        hT, hTr = m.sb("d_hT", [KX, W]), m.sb("d_hTr", [KX, W])
        qT = [m.sb(f"d_qT{s}", [P, 2, W]) for s in range(2)]
        kT = [m.sb(f"d_kT{s}", [P, 2, W]) for s in range(2)]
        v = [m.sb(f"d_v{s}", [P, GB, NH, STRIP]) for s in range(2)]
        attT = m.sb("d_attT", [P, W])
        y = [m.sb(f"d_y{s}", [P, GB, D]) for s in range(2)]
        yT = m.sb("d_yT", [KX, W])

        def slots(name, shape):
            return [m.sb(f"{name}{u}", shape) for u in range(SLOTS)]

        mx, mx2 = slots("d_mx", [P, GB]), slots("d_mx2", [P, GB])
        ex, later, decay = slots("d_ex", [P, W]), slots("d_later", [P, 1 + W]), slots("d_decay", [P, W])
        p2, pT = slots("d_p2", [P, W]), slots("d_pT", [P, W])
        rtot, inv = slots("d_rtot", [P, GB]), m.sb("d_inv", [P, GB, QUAD])
        bS = [m.ps(f"d_S{u}", [P, 512]) for u in range(SLOTS)]
        bT = m.ps("d_T", [P, 512])
        bO = m.ps("d_O", [P, 512])
        bX0, bX1 = m.ps("d_X0", [P, 512]), m.ps("d_X1", [P, 512])

        passed = m.sem("d_passed")
        loaded, ready, fold, folded = m.sem("d_loaded"), m.sem("d_ready"), m.sem("d_fold"), m.sem("d_folded")
        chain, gchain = m.sem("d_chain"), m.sem("d_gchain")
        S = Signals(m, "d", SLOTS, tensor="scored turned attended",
                    scalar="exped log_done root_done decay_made exped2 pT_kept",
                    vector="max_made shifted scanned inv_total rate_made weighed max2_made",
                    gpsimd="placed scaled shifted2")
        Q = Signals(m, "dq", 2, tensor="back", scalar="attT_kept", vector="inv_sum y_made")
        G = Signals(m, "dg", 3, tensor="x_turned filtered h_turned k_made*2 q_made*2 v_made y_turned out_made",
                    scalar="log_var rstd_made xT_kept log_var2 rstd2_made hT_kept q_kept*2 k_kept*2 v_kept yT_kept",
                    vector="stats moments centred stats2 moments2 centred2 h_made", gpsimd="hTr_kept")
        LOADS, READY = 12, 19
        TURNS = NQ // TURN
        assert NQ % TURN == 0

        def quad_of(i, k, lag):
            return i * (TURN // QUAD) + (k - lag - QUAD + 1) // QUAD

        def group_of(i, k, lag=0):
            return i * 2 + (k - lag) // GQ

        def on_back(k, lo, hi):
            return lo <= k - LAG_KEEP < hi and (k - LAG_KEEP) % QUAD == QUAD - 1

        class Beside:
            def norm(self, n, j): pass
            def filter(self, n, j): pass
            def project(self, n, s, j): pass
            def close(self, n, s, j): pass
            def finish(self, n, s, j): pass

        def beside(i, k, work):
            j, n, s = k % GQ, group_of(i, k), (k // GQ) % 2
            over_ = isinstance(i, int) and i == TURNS
            if not over_:
                work.norm(n + 3, j)
                work.filter(n + 2, j)
                work.project(n + 1, 1 - s, j)
            if not (over_ and k >= GQ):
                work.close(n, s, j)
            if not (isinstance(n, int) and n < 2):
                work.finish(n - 2, s, j)

        def pipeline(body, eng, work):
            for m_ in range(-3, 0):
                for j in range(GQ):
                    work.norm(m_ + 3, j)
                    if m_ >= -2:
                        work.filter(m_ + 2, j)
                    if m_ >= -1:
                        work.project(m_ + 1, 0, j)
            for k in range(TURN):
                body(0, k, 0, TURN)
            if TURNS > 1:
                with eng.Fori(1, TURNS) as i:
                    for k in range(TURN):
                        body(i, k, -TURN, TURN)
            for k in range(GQ + 3):
                body(TURNS, k, -TURN, 0)

        with nc.Block() as block:
            @block.sync
            def _(sp):
                for dst, name in ((conv, "d_conv"), (beta, "d_beta"), (win, "d_win"), (lnw, "d_lnw"), (lnb, "d_lnb"),
                                  (wout, "d_wout"), (gam, "d_gam"), (pos, "d_pos"), (cont, "d_cont"),
                                  (hide_f, "d_hide"), (notfirst, "d_notfirst"), (diag, "ident64")):
                    sp.dma_start(dst[:], dram[name]).then_inc(loaded, 16)

            @block.gpsimd
            def _(pool):
                S.start(pool, "gpsimd")
                G.start(pool, "gpsimd")
                pool.wait_ge(ready, READY)

                class Work(Beside):
                    def project(self, n, s, j):
                        if j == 2:
                            pool.wait_ge(G["hT_kept"], G.now(n))
                            pool.wait_ge(G["v_made"], G.before(n))
                            pool.sem_inc(passed, 1)
                            pool.tensor_copy(grouped(hTr[0:D, :], P), grouped(hT[0:D, :], P)[:, :, ::-1])\
                                .then_inc(G["hTr_kept"], 1)

                def body(i, k, lo, hi):
                    t = i * TURN + k

                    def unit(lag):
                        return lo <= k - lag < hi, t - lag, (k - lag) % SLOTS
                    on, q, u = unit(LAG_SCAN)
                    if on:
                        pool.wait_ge(S["scanned"], S.now(q))
                        pool.wait_ge(S["weighed"], S.past(q))
                        pool.tensor_tensor(decay[u][:], later[u][:, 0:W], pos[:], ALU.mult).then_inc(S["placed"], 1)
                        pool.wait_ge(S["rate_made"], S.now(q))
                        pool.wait_ge(S["placed"], S.now(q))
                        pool.tensor_tensor(grouped(decay[u][:], P), grouped(decay[u][:], P), over(rtot[u][:], P),
                                           ALU.mult).then_inc(S["scaled"], 1)
                    on, q, u = unit(LAG_WEIGH)
                    if on:
                        pool.wait_ge(S["max2_made"], S.now(q))
                        pool.tensor_tensor(grouped(p2[u][:], P), grouped(p2[u][:], P), over(mx2[u][:], P),
                                           ALU.subtract).then_inc(S["shifted2"], 1)
                    beside(i, k, work)

                work = Work()
                pipeline(body, pool, work)

            @block.tensor
            def _(pe):
                S.start(pe, "tensor")
                Q.start(pe, "tensor")
                G.start(pe, "tensor")
                pe.wait_ge(loaded, 16 * LOADS)
                nc.tensor.matmul(bX0[0:KX, :], lnb[:], win[0:D, 0:4 * P], start=True, stop=True)
                nc.tensor.matmul(bT[0:KX, 0:D], lnb[:], win[0:D, 4 * P:NW], start=True, stop=True).then_inc(fold, 1)
                pe.wait_ge(ready, READY)
                pe.wait_ge(folded, 3)

                class Work(Beside):
                    def filter(self, n, j):
                        if j == 2:
                            pe.wait_ge(G["centred"], G.now(n))
                            pe.wait_ge(G["hT_kept"], G.before(n))
                            pe.sem_inc(passed, 1)
                            for b in range(GB):
                                last = nc.tensor.transpose(bX1[0:D, b * P:(b + 1) * P], xn[:, b, :], ident[:])
                            last.then_inc(G["x_turned"], 1)
                        if 3 <= j < 3 + GB:
                            b = j - 3
                            if b == 0:
                                pe.wait_ge(G["xT_kept"], G.now(n))
                            for tap in range(TAPS):
                                rows = KX if tap == TAPS - 1 else D
                                last = nc.tensor.matmul(bX1[:, b * D:(b + 1) * D], xT[0:rows, b, tap:tap + P],
                                                        conv[0:rows, tap, :], start=(tap == 0), stop=(tap == TAPS - 1))
                            if b == GB - 1:
                                last.then_inc(G["filtered"], 1)

                    def project(self, n, s, j):
                        if j == 1:
                            pe.wait_ge(G["centred2"], G.now(n))
                            pe.sem_inc(passed, 1)
                            for b in range(GB):
                                last = nc.tensor.transpose(bX1[0:D, b * P:(b + 1) * P], hn[:, b, :], ident[:])
                            last.then_inc(G["h_turned"], 1)
                        if j in (3, 5):
                            c = (j - 3) // 2
                            if c == 0:
                                pe.wait_ge(G["h_made"], G.now(n - 3))
                                pe.wait_ge(G["hT_kept"], G.now(n))
                            else:
                                pe.wait_ge(G["k_kept"][0], G.now(n))
                            nc.tensor.matmul(bX0[:], win[:, c * P:(c + 1) * P], hT[:], start=True, stop=True)\
                                .then_inc(G["q_made"][c], 1)
                        if j in (4, 6):
                            c = (j - 4) // 2
                            pe.wait_ge(G["hTr_kept"], G.now(n))
                            pe.wait_ge(G["q_kept"][c], G.now(n))
                            nc.tensor.matmul(bX0[:], win[:, (2 + c) * P:(3 + c) * P], hTr[:], start=True, stop=True)\
                                .then_inc(G["k_made"][c], 1)
                        if j == 7:
                            pe.wait_ge(G["k_kept"][1], G.now(n))
                            for b in range(GB):
                                last = nc.tensor.matmul(bX0[:, b * D:(b + 1) * D], hTr[:, b * P:(b + 1) * P],
                                                        win[:, 4 * P:NW], start=True, stop=True)
                            last.then_inc(G["v_made"], 1)

                    def finish(self, n, s, j):
                        if j == 0:
                            pe.wait_ge(Q["y_made"], Q.now(n * (GQ // QUAD) + GQ // QUAD - 1))
                            if isinstance(n, int) and n == NQ // GQ - 1:
                                pe.wait_ge(G["h_made"], G.before(n))
                            else:
                                pe.wait_ge(G["v_kept"], G.now(n + 2))
                            pe.sem_inc(passed, 1)
                            for b in range(GB):
                                last = nc.tensor.transpose(bX0[0:D, b * P:(b + 1) * P], y[s][:, b, :], ident[:])
                            last.then_inc(G["y_turned"], 1)
                        if j == 1:
                            pe.wait_ge(G["yT_kept"], G.now(n))
                            for b in range(GB):
                                last = nc.tensor.matmul(bX0[:, b * D:(b + 1) * D], yT[:, b * P:(b + 1) * P], wout[:],
                                                        start=True, stop=True)
                            last.then_inc(G["out_made"], 1)

                def body(i, k, lo, hi):
                    t = i * TURN + k

                    def unit(lag):
                        return lo <= k - lag < hi, t - lag, (k - lag) % SLOTS
                    on, q, u = unit(0)
                    if on:
                        s, c = (k // GQ) % 2, (k % GQ) // 4
                        r = slice(32 * u, 32 * u + HD)
                        if k % 4 == 0:
                            pe.wait_ge(G["q_kept"][c], G.now(group_of(i, k)))
                            pe.wait_ge(G["k_kept"][c], G.now(group_of(i, k)))
                        pe.wait_ge(S["weighed"], S.past(q))
                        for _ in range(AGAIN[k % GQ]):
                            nc.tensor.matmul(bS[u][:], ident_b[:], hide[:, None, :].to_broadcast([P, GB, P]),
                                             start=True, stop=True)
                        nc.tensor.matmul(bS[u][:], ident_b[:], hide[:, None, :].to_broadcast([P, GB, P]),
                                         start=True, stop=False)
                        for b in range(GB):
                            cols = slice(b * P, (b + 1) * P)
                            last = nc.tensor.matmul(bS[u][:, cols], qT[s][r, c, cols], kT[s][r, c, cols],
                                                    start=False, stop=(b == GB - 1))
                        last.then_inc(S["scored"], 1)
                    on, q, u = unit(LAG_TURN)
                    if on:
                        pe.wait_ge(S["exped2"], S.now(q))
                        pe.wait_ge(S["pT_kept"], S.before(q))
                        if on_back(k - 1, lo, hi):
                            pe.wait_ge(Q["y_made"], Q.now(quad_of(i, k - 1, LAG_KEEP)))
                        for b in range(GB):
                            cols = slice(b * P, (b + 1) * P)
                            last = nc.tensor.transpose(bT[:, cols], p2[u][:, cols], ident[:])
                        last.then_inc(S["turned"], 1)
                    on, q, u = unit(LAG_PV)
                    if on:
                        j = k - LAG_PV
                        s, h = (j // GQ) % 2, j % GQ
                        if h == 0:
                            pe.wait_ge(G["v_kept"], G.now(group_of(i, k, LAG_PV)))
                        if h % QUAD == 0:
                            pe.wait_ge(Q["attT_kept"], Q.before(quad_of(i, k + QUAD - 1, LAG_PV)))
                        pe.wait_ge(S["pT_kept"], S.now(q))
                        r = slice(h % QUAD * STRIP, (h % QUAD + 1) * STRIP)
                        for b in range(GB):
                            last = nc.tensor.matmul(bO[r, b * P:(b + 1) * P], v[s][:, b, h, :],
                                                    pT[u][:, b * P:(b + 1) * P], start=True, stop=True)
                        last.then_inc(S["attended"], 1)
                    beside(i, k, work)
                    if on_back(k, lo, hi):
                        n = quad_of(i, k, LAG_KEEP)
                        pe.wait_ge(Q["attT_kept"], Q.now(n))
                        on, q, _ = unit(LAG_TURN)
                        if on:
                            pe.wait_ge(S["pT_kept"], S.now(q))
                        for b in range(GB):
                            cols = slice(b * P, (b + 1) * P)
                            last = nc.tensor.transpose(bT[:, cols], attT[:, cols], ident[:])
                        last.then_inc(Q["back"], 1)

                work = Work()
                pipeline(body, pe, work)

            @block.scalar
            def _(act):
                S.start(act, "scalar")
                Q.start(act, "scalar")
                act.preload_act_table_set("natural_log_exp_and_others")
                G.start(act, "scalar")
                act.wait_ge(loaded, 16 * LOADS)
                act.wait_ge(gchain, 2)
                nc.scalar.activation(gab[:], gab[:], ACT.Exp, scale=-1.0).then_inc(gchain, 1)
                act.wait_ge(gchain, 3)
                nc.scalar.activation(gab[:], gab[:], ACT.Ln, bias=1.0).then_inc(gchain, 1)
                act.wait_ge(ready, READY)
                act.wait_ge(folded, 2)
                nc.scalar.activation(win[:, 0:2 * P], win[:, 0:2 * P], ACT.Copy, scale=HD ** -0.5).then_inc(folded, 1)

                class Copies(Beside):
                    def filter(self, n, j):
                        if j == 3:
                            act.wait_ge(G["x_turned"], G.now(n))
                            act.wait_ge(G["filtered"], G.before(n))
                            nc.scalar.activation(xT[0:D, :, PADT:], grouped(bX1[0:D, :], P), ACT.Copy)\
                                .then_inc(G["xT_kept"], 1)

                    def project(self, n, s, j):
                        if j == 2:
                            act.wait_ge(G["h_turned"], G.now(n))
                            act.wait_ge(G["q_made"][1], G.before(n))
                            act.wait_ge(G["hTr_kept"], G.before(n))
                            nc.scalar.activation(hT[0:D, :], bX1[0:D, :], ACT.Copy).then_inc(G["hT_kept"], 1)
                        if j in (4, 6):
                            c = (j - 4) // 2
                            act.wait_ge(G["q_made"][c], G.now(n))
                            nc.scalar.activation(qT[s][:, c, :], bX0[:], ACT.Copy).then_inc(G["q_kept"][c], 1)
                        if j in (5, 7):
                            c = (j - 5) // 2
                            act.wait_ge(G["k_made"][c], G.now(n))
                            nc.scalar.activation(kT[s][:, c, :], bX0[:], ACT.Copy).then_inc(G["k_kept"][c], 1)

                    def close(self, n, s, j):
                        if j == 0:
                            act.wait_ge(G["v_made"], G.now(n))
                            nc.scalar.activation(v[s][:].rearrange("p b h e -> p (b h) e")[:, :, 0:HD],
                                                 grouped(bX0[:, 0:GB * D], HD), ACT.Copy).then_inc(G["v_kept"], 1)

                    def finish(self, n, s, j):
                        if j == 1:
                            act.wait_ge(G["y_turned"], G.now(n))
                            act.wait_ge(G["out_made"], G.before(n))
                            nc.scalar.activation(yT[0:D, :], bX0[0:D, :], ACT.Copy).then_inc(G["yT_kept"], 1)

                class Rates(Beside):
                    def norm(self, n, j):
                        if j == 4:
                            act.wait_ge(G["moments"], G.now(n))
                            act.wait_ge(G["centred"], G.before(n))
                            nc.scalar.activation(rstd[:], mv[:, :, 1], ACT.Ln, bias=1e-5).then_inc(G["log_var"], 1)
                            act.wait_ge(G["log_var"], G.now(n))
                            nc.scalar.activation(rstd[:], rstd[:], ACT.Exp, scale=-0.5).then_inc(G["rstd_made"], 1)

                    def filter(self, n, j):
                        if j == 7:
                            act.wait_ge(G["moments2"], G.now(n))
                            act.wait_ge(G["centred2"], G.before(n))
                            nc.scalar.activation(rstd2[:], mv2[:, :, 1], ACT.Ln, bias=1e-12).then_inc(G["log_var2"], 1)
                            act.wait_ge(G["log_var2"], G.now(n))
                            nc.scalar.activation(rstd2[:], rstd2[:], ACT.Exp, scale=-0.5).then_inc(G["rstd2_made"], 1)

                class Both(Beside):
                    def norm(self, n, j):
                        rates.norm(n, j)

                    def filter(self, n, j):
                        copies.filter(n, j)
                        rates.filter(n, j)

                    def project(self, n, s, j):
                        copies.project(n, s, j)

                def body(i, k, lo, hi):
                    t = i * TURN + k

                    def unit(lag):
                        return lo <= k - lag < hi, t - lag, (k - lag) % SLOTS
                    if on_back(k, lo, hi):
                        n = quad_of(i, k, LAG_KEEP)
                        act.wait_ge(S["attended"], S.now(i * TURN + k - LAG_KEEP))
                        act.wait_ge(Q["back"], Q.before(n))
                        nc.scalar.activation(attT[:], bO[:], ACT.Copy).then_inc(Q["attT_kept"], 1)
                    beside(i, k, copies)
                    on, q, u = unit(LAG_DECAY)
                    if on:
                        act.wait_ge(S["scaled"], S.now(q))
                        nc.scalar.activation(decay[u][:], decay[u][:], ACT.Ln, bias=1e-18).then_inc(S["log_done"], 1)
                    on2, q2, u2 = unit(LAG_EXP2)
                    if on2:
                        act.wait_ge(S["shifted2"], S.now(q2))
                        nc.scalar.activation(p2[u2][:], p2[u2][:], ACT.Exp).then_inc(S["exped2"], 1)
                    if on:
                        act.wait_ge(S["log_done"], S.now(q))
                        nc.scalar.activation(decay[u][:], decay[u][:], ACT.Exp, scale=0.5).then_inc(S["root_done"], 1)
                    on2, q2, u2 = unit(LAG_TURN)
                    if on2:
                        act.wait_ge(S["turned"], S.now(q2))
                        act.wait_ge(S["attended"], S.past(q2))
                        nc.scalar.activation(pT[u2][:], bT[:], ACT.Copy).then_inc(S["pT_kept"], 1)
                    if on:
                        act.wait_ge(S["root_done"], S.now(q))
                        nc.scalar.activation(decay[u][:], decay[u][:], ACT.Exp, scale=-1.0).then_inc(S["decay_made"], 1)
                    on, q, u = unit(0)
                    if on:
                        act.wait_ge(S["shifted"], S.now(q))
                        nc.scalar.activation(ex[u][:], ex[u][:], ACT.Exp).then_inc(S["exped"], 1)
                    beside(i, k, rates)

                copies, rates = Copies(), Rates()
                pipeline(body, act, Both())

            @block.vector
            def _(dve):
                S.start(dve, "vector")
                Q.start(dve, "vector")
                G.start(dve, "vector")
                dve.wait_ge(loaded, 16 * LOADS)
                steps = [0]

                def link(ins):
                    steps[0] += 1
                    ins.then_inc(chain, 1)
                    dve.wait_ge(chain, steps[0])

                nc.vector.tensor_scalar(gab[:], gam[:], -1.0, None, ALU.mult).then_inc(gchain, 1)
                dve.wait_ge(gchain, 1)
                nc.vector.tensor_tensor(gab[:], gab[:], gam[:], ALU.max).then_inc(gchain, 1)
                link(nc.vector.tensor_tensor(beta[:], beta[:], beta[:], ALU.mult))
                link(nc.vector.tensor_scalar(keep[:], beta[:], -1.0, 1.0, ALU.mult, ALU.add))
                link(nc.vector.tensor_tensor(conv[:], conv[:], keep[:, None, :].to_broadcast([KX, TAPS, D]), ALU.mult))
                link(nc.vector.tensor_scalar(beta[:], beta[:], 1.0, None, ALU.add))
                link(nc.vector.tensor_tensor(diag[:], diag[:], beta[0:D, :], ALU.mult))
                link(nc.vector.tensor_tensor(conv[0:D, TAPS - 1, :], conv[0:D, TAPS - 1, :], diag[:], ALU.add))
                dve.wait_ge(fold, 1)
                nc.vector.scalar_tensor_tensor(win[:, 0:4 * P], win[:, 0:4 * P], lnw[:, 0:1], bX0[0:KX, :],
                                               ALU.mult, ALU.add).then_inc(folded, 1)
                nc.vector.scalar_tensor_tensor(win[:, 4 * P:NW], win[:, 4 * P:NW], lnw[:, 0:1], bT[0:KX, 0:D],
                                               ALU.mult, ALU.add).then_inc(folded, 1)
                dve.wait_ge(gchain, 4)
                link(nc.vector.tensor_scalar(gam[:], gam[:], 0.0, None, ALU.max))
                link(nc.vector.tensor_tensor(gam[:], gam[:], gab[:], ALU.add))
                nc.vector.tensor_tensor(gsq[:], gam[:], gam[:], ALU.mult).then_inc(ready, 1)
                nc.vector.tensor_copy(hide[:], hide_f[:]).then_inc(ready, 1)
                nc.vector.tensor_copy(ident_b[:], ident[:]).then_inc(ready, 1)
                for u in range(SLOTS):
                    nc.vector.memset(later[u][:, 0:1], 0.0).then_inc(ready, 1)
                for s in range(2):
                    nc.vector.memset(v[s][:, :, :, HD:HD + 1], 1.0).then_inc(ready, 1)
                    nc.vector.memset(v[s][:, :, :, HD + 1:], 0.0).then_inc(ready, 1)
                nc.vector.memset(xT[0:D, :, 0:PADT], 0.0).then_inc(ready, 1)
                nc.vector.memset(xT[D:KX], 1.0).then_inc(ready, 1)
                for tile in (hT, hTr, yT):
                    nc.vector.memset(tile[D:KX, :], 1.0).then_inc(ready, 1)
                nc.vector.memset(H[:, NB:NB + 3 * GB, :], 0.0).then_inc(ready, 1)
                nc.vector.memset(rstd[:], 0.0).then_inc(ready, 1)
                nc.vector.memset(rstd2[:], 0.0).then_inc(ready, 1)
                dve.wait_ge(ready, READY)
                dve.wait_ge(folded, 3)

                class Work(Beside):
                    def norm(self, n, j):
                        if j == 3:
                            dve.wait_ge(G["centred"], G.before(n))
                            for b in range(GB):
                                last = nc.vector.bn_stats(
                                    st[:, b, :], H[:, bass.ds(n * GB + b, 1), :].rearrange("p b d -> p (b d)"))
                            last.then_inc(G["stats"], 1)
                            dve.wait_ge(G["stats"], G.now(n))
                            dve.sem_inc(passed, 1)
                            for b in range(GB):
                                last = nc.vector.bn_aggr(mv[:, b, :], st[:, b, :])
                            last.then_inc(G["moments"], 1)
                        if j == 5:
                            dve.wait_ge(G["rstd_made"], G.now(n))
                            dve.wait_ge(G["x_turned"], G.before(n))
                            for b in range(GB):
                                last = nc.vector.tensor_scalar(
                                    xn[:, b, :], H[:, bass.ds(n * GB + b, 1), :].rearrange("p b d -> p (b d)"),
                                    mv[:, b, 0:1], rstd[:, b:b + 1], ALU.subtract, ALU.mult)
                            last.then_inc(G["centred"], 1)

                    def filter(self, n, j):
                        if j == 7:
                            dve.wait_ge(G["filtered"], G.now(n))
                            dve.wait_ge(G["centred2"], G.before(n))
                            for b in range(GB):
                                last = nc.vector.bn_stats(st2[:, b, :], bX1[:, b * D:(b + 1) * D])
                            last.then_inc(G["stats2"], 1)
                            dve.wait_ge(G["stats2"], G.now(n))
                            dve.sem_inc(passed, 1)
                            for b in range(GB):
                                last = nc.vector.bn_aggr(mv2[:, b, :], st2[:, b, :])
                            last.then_inc(G["moments2"], 1)

                    def project(self, n, s, j):
                        if j == 0:
                            dve.wait_ge(G["rstd2_made"], G.now(n))
                            dve.wait_ge(G["h_turned"], G.before(n))
                            for b in range(GB):
                                last = nc.vector.tensor_scalar(hn[:, b, :], bX1[:, b * D:(b + 1) * D], mv2[:, b, 0:1],
                                                               rstd2[:, b:b + 1], ALU.subtract, ALU.mult)
                            last.then_inc(G["centred2"], 1)

                    def finish(self, n, s, j):
                        if j == 2:
                            dve.wait_ge(G["out_made"], G.now(n))
                            hs = H[:, bass.ds(n * GB, GB), :]
                            nc.vector.tensor_tensor(hs, grouped(bX0[:, 0:GB * D], D), hs, ALU.add)\
                                .then_inc(G["h_made"], 1)

                def body(i, k, lo, hi):
                    t = i * TURN + k

                    def unit(lag):
                        return lo <= k - lag < hi, t - lag, (k - lag) % SLOTS
                    on0, q0, u0 = unit(0)
                    on1, q1, u1 = unit(LAG_SCAN)
                    on3, q3, u3 = unit(LAG_WEIGH)
                    on_y = lo <= k - LAG_Y < hi and (k - LAG_Y) % QUAD == QUAD - 1
                    if on_y:
                        n, c, s = quad_of(i, k, LAG_Y), (k - LAG_Y) // QUAD % 2, (k - LAG_Y) // GQ % 2
                        sums = bT[:].rearrange("p (b h e) -> p b h e", h=QUAD, e=STRIP)
                        dve.wait_ge(Q["back"], Q.now(n))
                        nc.vector.reciprocal(inv[:], sums[:, :, :, HD]).then_inc(Q["inv_sum"], 1)
                        dve.wait_ge(Q["inv_sum"], Q.now(n))
                        if c == 0:
                            dve.wait_ge(G["y_turned"], G.ago(group_of(i, k, LAG_Y), 2))
                        half = y[s][:].rearrange("p b (c h e) -> p b c h e", c=2, h=QUAD)[:, :, c]
                        nc.vector.scalar_tensor_tensor(half, sums[:, :, :, 0:HD], notfirst[:, 0:1],
                                                       inv[:, :, :, None].to_broadcast([P, GB, QUAD, HD]),
                                                       ALU.mult, ALU.mult).then_inc(Q["y_made"], 1)
                    if on1:
                        dve.wait_ge(S["exped"], S.now(q1))
                        dve.wait_ge(S["placed"], S.past(q1))
                        nc.vector.tensor_tensor_scan(later[u1][:, 1:1 + W], cont[:], ex[u1][:], 0.0,
                                                     ALU.mult, ALU.add).then_inc(S["scanned"], 1)
                    if on1:
                        dve.wait_ge(S["scanned"], S.now(q1))
                        dve.wait_ge(S["scaled"], S.past(q1))
                        nc.vector.reciprocal(rtot[u1][:], grouped(later[u1][:, 1:1 + W], P)[:, :, P - 1])\
                            .then_inc(S["inv_total"], 1)
                    if on3:
                        dve.wait_ge(S["decay_made"], S.now(q3))
                        dve.wait_ge(S["turned"], S.past(q3))
                        nc.vector.scalar_tensor_tensor(p2[u3][:], decay[u3][:], 1e-5, bS[u3][:], ALU.max, ALU.mult)\
                            .then_inc(S["weighed"], 1)
                    if on1:
                        h = (k - LAG_SCAN) % GQ
                        dve.wait_ge(S["inv_total"], S.now(q1))
                        nc.vector.tensor_scalar(rtot[u1][:], rtot[u1][:], gsq[:, h:h + 1], None, ALU.mult)\
                            .then_inc(S["rate_made"], 1)
                    if on0:
                        dve.wait_ge(S["scored"], S.now(q0))
                        nc.vector.tensor_reduce(mx[u0][:], grouped(bS[u0][:], P), AX, ALU.max).then_inc(S["max_made"], 1)
                    if on3:
                        dve.wait_ge(S["weighed"], S.now(q3))
                        dve.wait_ge(S["shifted2"], S.past(q3))
                        nc.vector.tensor_reduce(mx2[u3][:], grouped(p2[u3][:], P), AX, ALU.max)\
                            .then_inc(S["max2_made"], 1)
                    if on0:
                        dve.wait_ge(S["max_made"], S.now(q0))
                        dve.wait_ge(S["scanned"], S.past(q0))
                        nc.vector.tensor_tensor(grouped(ex[u0][:], P), grouped(bS[u0][:], P), over(mx[u0][:], P),
                                                ALU.subtract).then_inc(S["shifted"], 1)
                    beside(i, k, work)

                work = Work()
                pipeline(body, dve, work)
        m.clear_semaphores()


def phase_selected_mlp(nc, dram, out, H, ident, NB):
    HID = dram["g_w1"].shape[1]
    NC = HID // P
    TOPK = P // 2 - 1
    NG = NB // GB
    SLOTS = 2
    with ExitStack() as ctx:
        m = Mem(nc, ctx)
        w1, b1 = m.sb("g_w1", [D, HID]), m.sb("g_b1", [P, NC])
        w2, b2 = m.sb("g_w2", [P, NC, D]), m.sb("g_b2", [P, D])
        wr, br = m.sb("g_wr", [D, 1]), m.sb("g_br", [P, 1])
        xTall = m.sb("xTall", [D, NB * P])
        weight = m.sb("weight", [P, NB])
        gain = m.sb("gain", [P, NB])
        rows, left = m.sb("g_rows", [NB, P]), m.sb("g_left", [NB, P])
        top8 = m.sb("g_top8", [NB, 8])
        above, equal = m.sb("g_above", [NB, P]), m.sb("g_equal", [NB, P])
        upto, ones = m.sb("g_upto", [NB, P]), m.sb("g_ones", [NB, P])
        count = m.sb("g_count", [NB, 1])

        def slots(name, shape):
            return [m.sb(f"{name}{u}", shape) for u in range(SLOTS)]

        st, mv, rstd = slots("g_st", [P, GB, 6]), slots("g_mv", [P, GB, 2]), slots("g_rstd", [P, GB])
        x, xT = slots("g_x", [P, GB, D]), slots("g_xT", [D, W])
        hid = slots("g_hid", [P, NC, W])
        biased, scaled, res = slots("g_biased", [P, GB, D]), slots("g_scaled", [P, GB, D]), slots("g_res", [P, GB, D])
        bA = [m.ps(f"g_A{u}", [P, 512]) for u in range(SLOTS)]
        bB = [m.ps(f"g_B{u}", [P, 512]) for u in range(SLOTS)]
        bH = [[m.ps(f"g_H{u}{c}", [P, 512]) for c in range(NC)] for u in range(SLOTS)]

        passed = m.sem("g_passed")
        loaded, ready = m.sem("g_loaded"), m.sem("g_ready")
        turned, turned_back, chosen, select = m.sem("g_turned"), m.sem("g_turned_back"), m.sem("g_chosen"), m.sem("g_select")
        stored = [m.sem(f"g_stored{u}") for u in range(SLOTS)]
        S = Signals(m, "g", SLOTS, tensor="x_turned weighed", scalar="log_var rstd_made xT_kept weight_kept",
                    vector="stats moments centred", gpsimd="h_made xT_stored")
        M = Signals(m, "gm", SLOTS, tensor="hid_made*2 out_made", scalar="activated*2",
                    vector="bias_added gained result_made")
        LOADS = 6
        assert NC == 2 and 8 < TOPK

        with nc.Block() as block:
            @block.sync
            def _(sp):
                for dst, name in ((w1, "g_w1"), (b1, "g_b1"), (b2, "g_b2"), (wr, "g_wr"), (br, "g_br")):
                    sp.dma_start(dst[:], dram[name]).then_inc(loaded, 16)
                sp.dma_start(w2[:], dram["g_w2"].rearrange("(c p) n -> p c n", p=P)).then_inc(loaded, 16)
                for u in range(SLOTS):
                    sp.sem_inc(stored[u], 16)
                with sp.Fori(0, NG // SLOTS) as i:
                    for u in range(SLOTS):
                        n = i * SLOTS + u
                        sp.wait_ge(M["result_made"], M.now(n))
                        sp.dma_start(out[bass.ds(n * GB, GB)].rearrange("b t d -> t b d"), res[u][:])\
                            .then_inc(stored[u], 16)
                for u in range(SLOTS):
                    sp.wait_ge(stored[u], 16 * (NG // SLOTS + 1))

            @block.gpsimd
            def _(pool):
                S.start(pool, "gpsimd")
                with pool.Fori(0, NG // SLOTS) as i:
                    for u in range(SLOTS):
                        n = i * SLOTS + u
                        pool.wait_ge(S["centred"], S.now(n))
                        hs = H[:, bass.ds(n * GB, GB), :]
                        pool.tensor_tensor(hs, hs, x[u][:], ALU.add).then_inc(S["h_made"], 1)
                    for u in range(SLOTS):
                        n = i * SLOTS + u
                        pool.wait_ge(S["xT_kept"], S.now(n))
                        pool.sem_inc(passed, 1)
                        pool.tensor_copy(xTall[:, bass.ds(n * W, W)], xT[u][:]).then_inc(S["xT_stored"], 1)

            @block.tensor
            def _(pe):
                S.start(pe, "tensor")
                M.start(pe, "tensor")
                pe.wait_ge(loaded, 16 * LOADS)
                with pe.Fori(0, NG // SLOTS) as i:
                    for u in range(SLOTS):
                        n = i * SLOTS + u
                        pe.wait_ge(S["centred"], S.now(n))
                        pe.wait_ge(S["xT_kept"], S.past(n))
                        pe.sem_inc(passed, 1)
                        for b in range(GB):
                            last = nc.tensor.transpose(bA[u][0:D, b * P:(b + 1) * P], x[u][:, b, :], ident[:])
                        last.then_inc(S["x_turned"], 1)
                    for u in range(SLOTS):
                        n = i * SLOTS + u
                        pe.wait_ge(S["xT_kept"], S.now(n))
                        pe.wait_ge(S["weight_kept"], S.past(n))
                        for b in range(GB):
                            last = nc.tensor.matmul(bB[u][:, b:b + 1], xT[u][:, b * P:(b + 1) * P], wr[:],
                                                    start=True, stop=True)
                        last.then_inc(S["weighed"], 1)
                pe.wait_ge(S["weight_kept"], S.now(NG - 1))
                nc.tensor.transpose(bA[0][0:NB, 0:P], weight[:], ident[:]).then_inc(turned, 1)
                pe.wait_ge(chosen, 1)
                nc.tensor.transpose(bA[1][:, 0:NB], above[:], ident[0:NB, 0:NB]).then_inc(turned_back, 1)
                pe.wait_ge(S["xT_stored"], S.now(NG - 1))
                with pe.Fori(0, NG // SLOTS) as i:
                    for u in range(SLOTS):
                        n = i * SLOTS + u
                        for c in range(NC):
                            pe.wait_ge(M["activated"][c], M.past(n))
                            pe.sem_inc(passed, 1)
                            nc.tensor.matmul(bH[u][c][:], w1[:, c * P:(c + 1) * P], xTall[:, bass.ds(n * W, W)],
                                             start=True, stop=True).then_inc(M["hid_made"][c], 1)
                    for u in range(SLOTS):
                        n = i * SLOTS + u
                        pe.wait_ge(M["activated"][0], M.now(n))
                        pe.wait_ge(M["activated"][1], M.now(n))
                        pe.wait_ge(M["bias_added"], M.past(n))
                        for b in range(GB):
                            for c in range(NC):
                                last = nc.tensor.matmul(bB[u][:, b * D:(b + 1) * D], hid[u][:, c, b * P:(b + 1) * P],
                                                        w2[:, c, :], start=(c == 0), stop=(c == NC - 1))
                        last.then_inc(M["out_made"], 1)

            @block.scalar
            def _(act):
                S.start(act, "scalar")
                M.start(act, "scalar")
                act.preload_act_table_set("natural_log_exp_and_others")
                act.wait_ge(loaded, 16 * LOADS)
                with act.Fori(0, NG // SLOTS) as i:
                    for u in range(SLOTS):
                        n = i * SLOTS + u
                        act.wait_ge(S["moments"], S.now(n))
                        act.wait_ge(S["centred"], S.past(n))
                        nc.scalar.activation(rstd[u][:], mv[u][:, :, 1], ACT.Ln, bias=1e-5).then_inc(S["log_var"], 1)
                    for u in range(SLOTS):
                        n = i * SLOTS + u
                        act.wait_ge(S["log_var"], S.now(n))
                        nc.scalar.activation(rstd[u][:], rstd[u][:], ACT.Exp, scale=-0.5).then_inc(S["rstd_made"], 1)
                    for u in range(SLOTS):
                        n = i * SLOTS + u
                        act.wait_ge(S["x_turned"], S.now(n))
                        act.wait_ge(S["weighed"], S.past(n))
                        act.wait_ge(S["xT_stored"], S.past(n))
                        nc.scalar.activation(xT[u][:], bA[u][0:D, :], ACT.Copy).then_inc(S["xT_kept"], 1)
                    for u in range(SLOTS):
                        n = i * SLOTS + u
                        act.wait_ge(S["weighed"], S.now(n))
                        nc.scalar.activation(weight[:, bass.ds(n * GB, GB)], bB[u][:, 0:GB], ACT.Identity,
                                             bias=br[:, 0:1]).then_inc(S["weight_kept"], 1)
                act.preload_act_table_set("gelu_apprx_tanh_and_others")
                with act.Fori(0, NG // SLOTS) as i:
                    for u in range(SLOTS):
                        n = i * SLOTS + u
                        for c in range(NC):
                            act.wait_ge(M["hid_made"][c], M.now(n))
                            act.wait_ge(M["out_made"], M.past(n))
                            nc.scalar.activation(hid[u][:, c, :], bH[u][c][:], ACT.Gelu_apprx_tanh, bias=b1[:, c:c + 1])\
                                .then_inc(M["activated"][c], 1)

            @block.vector
            def _(dve):
                S.start(dve, "vector")
                M.start(dve, "vector")
                nc.vector.memset(ones[:], 1.0).then_inc(ready, 1)
                with dve.Fori(0, NG // SLOTS) as i:
                    for u in range(SLOTS):
                        n = i * SLOTS + u
                        dve.wait_ge(S["moments"], S.past(n))
                        for b in range(GB):
                            last = nc.vector.bn_stats(
                                st[u][:, b, :], H[:, bass.ds(n * GB + b, 1), :].rearrange("p b d -> p (b d)"))
                        last.then_inc(S["stats"], 1)
                    for u in range(SLOTS):
                        n = i * SLOTS + u
                        dve.wait_ge(S["stats"], S.now(n))
                        dve.wait_ge(S["centred"], S.past(n))
                        dve.sem_inc(passed, 1)
                        for b in range(GB):
                            last = nc.vector.bn_aggr(mv[u][:, b, :], st[u][:, b, :])
                        last.then_inc(S["moments"], 1)
                    for u in range(SLOTS):
                        n = i * SLOTS + u
                        dve.wait_ge(S["rstd_made"], S.now(n))
                        dve.wait_ge(S["x_turned"], S.past(n))
                        dve.wait_ge(S["h_made"], S.past(n))
                        for b in range(GB):
                            last = nc.vector.tensor_scalar(
                                x[u][:, b, :], H[:, bass.ds(n * GB + b, 1), :].rearrange("p b d -> p (b d)"),
                                mv[u][:, b, 0:1], rstd[u][:, b:b + 1], ALU.subtract, ALU.mult)
                        last.then_inc(S["centred"], 1)
                steps = [0]

                def step(ins):
                    steps[0] += 1
                    ins.then_inc(select, 1)
                    dve.wait_ge(select, steps[0])

                dve.wait_ge(ready, 1)
                dve.wait_ge(turned, 1)
                step(nc.vector.tensor_copy(rows[:], bA[0][0:NB, 0:P]))
                step(nc.vector.tensor_copy(left[:], rows[:]))
                for r in range((TOPK - 1) // 8):
                    step(nc.vector.max(top8[:], left[:]))
                    step(nc.vector.match_replace(left[:], top8[:], left[:], -3e38))
                step(nc.vector.max(top8[:], left[:]))
                nth = top8[:, (TOPK - 1) % 8:(TOPK - 1) % 8 + 1]
                step(nc.vector.tensor_scalar(above[:], rows[:], nth, None, ALU.is_gt))
                step(nc.vector.tensor_scalar(equal[:], rows[:], nth, None, ALU.is_equal))
                step(nc.vector.tensor_reduce(count[:], above[:], AX, ALU.add))
                step(nc.vector.tensor_scalar(count[:], count[:], -1.0, float(TOPK), ALU.mult, ALU.add))
                step(nc.vector.tensor_tensor_scan(upto[:], ones[:], equal[:], 0.0, ALU.mult, ALU.add))
                step(nc.vector.scalar_tensor_tensor(equal[:], upto[:], count[:, 0:1], equal[:], ALU.is_le, ALU.mult))
                step(nc.vector.tensor_tensor(above[:], above[:], equal[:], ALU.add))
                nc.vector.tensor_tensor(above[:], above[:], rows[:], ALU.mult).then_inc(chosen, 1)
                dve.wait_ge(turned_back, 1)
                step(nc.vector.tensor_copy(gain[:], bA[1][:, 0:NB]))
                dve.wait_ge(S["h_made"], S.now(NG - 1))
                with dve.Fori(0, NG // SLOTS) as i:
                    for u in range(SLOTS):
                        n = i * SLOTS + u
                        dve.wait_ge(M["out_made"], M.now(n))
                        dve.wait_ge(M["gained"], M.past(n))
                        nc.vector.tensor_tensor(biased[u][:], grouped(bB[u][:, 0:GB * D], D),
                                                b2[:, None, :].to_broadcast([P, GB, D]), ALU.add)\
                            .then_inc(M["bias_added"], 1)
                    for u in range(SLOTS):
                        n = i * SLOTS + u
                        dve.wait_ge(M["bias_added"], M.now(n))
                        dve.wait_ge(M["result_made"], M.past(n))
                        nc.vector.tensor_tensor(scaled[u][:], biased[u][:], over(gain[:, bass.ds(n * GB, GB)], D),
                                                ALU.mult).then_inc(M["gained"], 1)
                    for u in range(SLOTS):
                        n = i * SLOTS + u
                        dve.wait_ge(M["gained"], M.now(n))
                        dve.wait_ge(stored[u], (i + 1) * 16)
                        nc.vector.tensor_tensor(res[u][:], scaled[u][:], H[:, bass.ds(n * GB, GB), :], ALU.add)\
                            .then_inc(M["result_made"], 1)
        m.clear_semaphores()


def tower(nc, dram, out, NB):
    NE = dram["router"].shape[1]
    with ExitStack() as ctx:
        m = Mem(nc, ctx)
        H = m.sb("H", [P, NB + 3 * GB, D])
        ident = m.sb("ident", [P, P])
        const_loaded = m.sem("const_loaded")
        with nc.Block() as block:
            @block.sync
            def _(sp):
                sp.dma_start(ident[:], dram["ident"]).then_inc(const_loaded, 16)
                sp.wait_ge(const_loaded, 16)
        gathered = [m.sem(f"gathered{u}") for u in range(2)]
        phase_embed_attend(nc, dram, H, ident, gathered, NB)
        with ExitStack() as moe:
            m2 = Mem(nc, moe)
            flatT = m2.sb("flatT", [P, NB * P + W])
            logits = m2.sb("logits", [P, NB, NE])
            phase_block_attention(nc, dram, H, flatT, logits, ident, NB)
            phase_experts(nc, dram, H, flatT, logits, ident, NB)
        phase_decay_attention(nc, dram, H, ident, NB)
        phase_selected_mlp(nc, dram, out, H, ident, NB)


def lay_out(inputs):
    g = {k: np.asarray(v) for k, v in inputs.items()}
    a = {}
    col = lambda v: v[:, None]
    a["tokens"] = g["x"].T
    a["table"] = g["L0_tok_embed_table"]
    ws = [np.concatenate([g[f"L0_tok_W{k}"], g[f"L0_tok_b{k}"][None]], 0) for k in (1, 2)]
    a["tok_w"] = np.stack(ws)
    a["tok_wT"] = np.stack([w.T for w in ws])
    a["tok_wa"] = g["L0_tok_Wa"]
    a["tok_ba"] = np.tile(g["L0_tok_ba"][None], (P, 1))
    for c in "qkv":
        a[f"a0_{c}"] = np.concatenate([g[f"L0_attn_W{c}"], col(g[f"L0_attn_b{c}"])], 1)
    a["a0_woT"] = g["L0_attn_Wo"].T
    a["a0_bo"] = np.tile(g["L0_attn_bo"][None], (P, 1))
    a["a0_first"] = np.stack([a["a0_q"][0], a["a0_k"][0]], 1)
    a["ident"] = np.eye(P, dtype=np.float32)
    HD = 16
    turned = (np.arange(HD) + HD // 2) % HD
    wq = g["L0_ffn_wq"].reshape(4, HD, D)
    wk = g["L0_ffn_wk"].reshape(2, HD, D)[[0, 0, 1, 1]]
    a["f_wq"] = np.concatenate([wq, wq[:, turned]], 1).reshape(P, D).T
    a["f_wk"] = np.concatenate([wk, wk], 1).reshape(P, D).T
    a["f_wkp"] = np.concatenate([wk[:, turned]] * 2, 1).reshape(P, D).T
    a["f_wv"] = g["L0_ffn_wv"].T
    a["f_wo"] = g["L0_ffn_wo"].T
    a["f_ln1"] = col(g["L0_ffn_ln1_w"])
    a["f_ln2"] = col(g["L0_ffn_ln2_w"])
    a["router"] = g["L0_ffn_router_w"].T
    inv_freq = 1.0 / 10000.0 ** (np.arange(0, HD, 2, dtype=np.float32) / HD)
    ang = np.outer(np.arange(P, dtype=np.float32), inv_freq)
    ang = np.concatenate([ang, ang], -1)
    cos = np.cos(ang).T.astype(np.float32)
    sin = np.sin(ang).T.astype(np.float32) * np.where(np.arange(HD) < HD // 2, -1, 1)[:, None].astype(np.float32)
    a["rope_q"] = np.tile(np.concatenate([cos, sin]) * np.float32(HD ** -0.5), (4, 1))
    a["cos_k"] = np.tile(cos, (8, 1))
    a["sin_k"] = np.tile(sin, (8, 1))
    a["hide"] = np.where(np.tril(np.ones((P, P), bool)), 0.0, -1e30).astype(np.float32)
    NE, HID = g["L0_ffn_w1"].shape[:2]
    pad = -NE * HID % P
    for k in (1, 3):
        w = np.pad(g[f"L0_ffn_w{k}"].reshape(NE * HID, D), ((0, pad), (0, 0))).T
        a[f"e_w{k}"] = np.concatenate([w, w])
    a["e_ln2"] = np.concatenate([a["f_ln2"]] * 2)
    a["e_w2"] = np.pad(g["L0_ffn_w2"].transpose(0, 2, 1).reshape(NE * HID, D), ((0, pad), (0, 0)))
    owner = np.pad(np.repeat(np.eye(NE), HID, 1), ((0, 0), (0, pad)))
    a["owner"] = np.tile(owner, (3, 1)).astype(np.float32)
    a["rank"] = np.tile(np.arange(NE, 0, -1), (P, 1)).astype(np.float32)
    taps = g["L1_attn_conv_w"].transpose(1, 2, 0)
    bias = np.zeros((1,) + taps.shape[1:], np.float32)
    bias[0, -1] = g["L1_attn_conv_b"]
    a["d_conv"] = np.concatenate([taps, bias])
    a["d_beta"] = np.tile(g["L1_attn_sqrt_beta"].reshape(1, D), (D + 1, 1))

    def strips(w):
        w = w.reshape(w.shape[0], 8, 8)
        return np.pad(w, ((0, 0), (0, 0), (0, 24))).reshape(w.shape[0], 256)

    wqkv = [np.concatenate([g[f"L1_attn_{c}_w"].T, g[f"L1_attn_{c}_b"][None]]) for c in "qkv"]
    a["d_win"] = np.concatenate([strips(wqkv[0]), strips(wqkv[1]), wqkv[2]], 1)
    a["d_lnw"] = np.concatenate([g["L1_attn_ln_w"], np.ones(1, np.float32)])[:, None]
    a["d_lnb"] = np.concatenate([np.zeros((D, D), np.float32), col(g["L1_attn_ln_b"])], 1)
    a["d_wout"] = np.concatenate([g["L1_attn_out_w"].T, g["L1_attn_out_b"][None]])
    a["d_gam"] = np.tile(g["L1_attn_gammas"].reshape(1, 8), (P, 1))
    i, j = np.arange(P)[:, None], P - 1 - np.arange(P)[None]
    a["d_pos"] = np.tile(np.maximum(i - j, 0), (1, 4)).astype(np.float32)
    a["d_cont"] = np.tile((np.arange(W) % P != 0), (P, 1)).astype(np.float32)
    a["d_hide"] = np.where(j > i, -1e32, 0.0).astype(np.float32)
    a["d_notfirst"] = (i > 0).astype(np.float32)
    a["ident64"] = np.eye(D, dtype=np.float32)
    a["g_w1"] = g["L1_ffn_w1"]
    a["g_b1"] = g["L1_ffn_b1"].reshape(-1, P).T
    a["g_w2"] = g["L1_ffn_w2"]
    a["g_b2"] = np.tile(g["L1_ffn_b2"][None], (P, 1))
    a["g_wr"] = g["L1_ffn_wr"]
    a["g_br"] = np.tile(g["L1_ffn_br"][None], (P, 1))
    return {k: np.ascontiguousarray(v) for k, v in a.items()}


def kernel(**inputs):
    import concourse.bacc as _bacc
    from concourse.bass_utils import run_bass_kernel_spmd as _run

    nc = _bacc.Bacc("TRN2", target_bir_lowering=False, num_devices=1)
    laid = lay_out(inputs)
    NB = laid["tokens"].shape[1]
    arrays, dram = {}, {}
    for name, a in laid.items():
        arrays[f"in_{name}"] = a
        dram[name] = nc.dram_tensor(f"in_{name}", a.shape, mybir.dt.from_np(a.dtype), kind="ExternalInput").ap()
    out = nc.dram_tensor("out_h", (NB, P, D), F32, kind="ExternalOutput").ap()
    tower(nc, dram, out, NB)
    r = _run(nc, [arrays], core_ids=[0])
    return r.results[0]["out_h"]
```

```python
from contextlib import ExitStack

import concourse.bass as bass
import numpy as np
from concourse import mybir

ALU = mybir.AluOpType
ACT = mybir.ActivationFunctionType
AX = mybir.AxisListType.X
F32 = mybir.dt.float32
BF16 = mybir.dt.bfloat16
I32 = mybir.dt.int32

P = 128
D = 64
GB = 4
W = GB * P


class Signals:

    def __init__(self, mem, phase, slots, **owned):
        self.slots, self.sems = slots, {}
        self.names = {engine: text.split() for engine, text in owned.items()}
        for listed in self.names.values():
            for name in listed:
                name, _, count = name.partition("*")
                made = [mem.sem(f"{phase}_{name}{k}") for k in range(int(count or 1))]
                self.sems[name] = made if count else made[0]

    def __getitem__(self, name):
        return self.sems[name]

    def start(self, eng, engine):
        for name in self.names[engine]:
            made = self.sems[name.partition("*")[0]]
            for sem in made if "*" in name else [made]:
                eng.sem_inc(sem, self.slots)

    def now(self, n):
        return n + (self.slots + 1)

    def ago(self, n, k):
        return n + (self.slots + 1 - k)

    def before(self, n):
        return n + self.slots

    def past(self, n):
        return n + 1


def grouped(ap, width):
    return ap.rearrange("p (g w) -> p g w", w=width)


def over(ap, width):
    return ap[:, :, None].to_broadcast([ap.shape[0], ap.shape[1], width])


class Mem:

    def __init__(self, nc, ctx):
        self.nc, self.ctx, self.sems = nc, ctx, []

    def sb(self, name, shape, dt=F32):
        return self.ctx.enter_context(self.nc.sbuf_tensor(name, shape, dt))

    def ps(self, name, shape, dt=F32):
        return self.ctx.enter_context(self.nc.psum_tensor(name, shape, dt))

    def sem(self, name):
        self.sems.append(self.ctx.enter_context(self.nc.semaphore(name)))
        return self.sems[-1]

    def clear_semaphores(self):
        numbers = sorted(s.num for s in self.sems)
        with self.nc.Block() as block:
            @block.gpsimd
            def _(pool):
                first = last = numbers[0]
                for n in numbers[1:] + [None]:
                    if n is None or n != last + 1:
                        pool.sem_clear(range(first, last + 1))
                        first = n
                    last = n




def phase_embed_attend(nc, dram, H, ident, gathered, NB):
    E_DIM = dram["table"].shape[1] // 2
    KE = E_DIM + 1
    KX = D + 1
    NG = NB // GB
    SLOTS = 4
    TURNS = NG // SLOTS
    ROWS, PROJECT, CENTRE, TURN_X, VALUES, SCORE, MAX, EXP, FINISH = 1, 2, 3, 4, 5, 6, 7, 8, 9
    PEEL = -(-FINISH // SLOTS)
    assert NG % SLOTS == 0
    with ExitStack() as ctx:
        m = Mem(nc, ctx)
        tok = m.sb("tok", [P, NB], I32)
        idx = [m.sb(f"idx{u}", [P, GB], I32) for u in range(SLOTS)]
        nothing = m.sb("nothing", [P, 2], I32)
        rows = [m.sb(f"rows{u}", [P, GB, 2 * E_DIM]) for u in range(SLOTS)]
        rowsT = [m.sb(f"rowsT{u}", [P, 2, W]) for u in range(SLOTS)]
        tokw = m.sb("tokw", [KE, 2, KX])
        tokwT = m.sb("tokwT", [D, 2, KE])
        wa = m.sb("wa", [D, 1])
        nba = m.sb("nba", [P, 1])
        qa = m.sb("qa", [D, KX])
        ka = m.sb("ka", [D, KX])
        va = m.sb("va", [D, KX])
        woT = m.sb("woT", [D, D])
        bo = m.sb("bo", [P, D])
        qk = m.sb("qk", [KX, KX])
        vo = m.sb("vo", [KX, D + 3])
        gate = [m.sb(f"gate{u}", [P, 2, GB]) for u in range(SLOTS)]
        part = [m.sb(f"part{u}", [P, 2, GB, D]) for u in range(SLOTS)]
        h0 = [m.sb(f"h0{u}", [P, GB, D]) for u in range(SLOTS)]
        st = [m.sb(f"st{u}", [P, GB, 6]) for u in range(SLOTS)]
        mv = [m.sb(f"mv{u}", [P, GB, 2]) for u in range(SLOTS)]
        rstd = [m.sb(f"rstd{u}", [P, GB]) for u in range(SLOTS)]
        xn = [m.sb(f"xn{u}", [P, GB, D]) for u in range(SLOTS)]
        xT = [m.sb(f"xT{u}", [KX, W]) for u in range(SLOTS)]
        yT = [m.sb(f"yT{u}", [KX, W]) for u in range(SLOTS)]
        v = [m.sb(f"v{u}", [P, GB, D + 3]) for u in range(SLOTS)]
        mx = [m.sb(f"mx{u}", [P, GB]) for u in range(SLOTS)]
        pr = [m.sb(f"pr{u}", [P, W]) for u in range(SLOTS)]
        pT = [m.sb(f"pT{u}", [P, W]) for u in range(SLOTS)]
        live = [m.sb(f"live{u}", [P, GB, 2]) for u in range(SLOTS)]
        rs = [m.sb(f"rs{u}", [P, GB]) for u in range(SLOTS)]
        att = [m.sb(f"att{u}", [P, GB, D]) for u in range(SLOTS)]
        b_rows, b_x, b_y, b_v, b_s, b_out = [m.ps(f"a_{name}", [P, 512])
                                             for name in ("rows_T", "x_T", "y", "v", "scores", "attended")]
        b_part = [m.ps(f"a_part{k}", [P, 512]) for k in range(2)]

        passed = m.sem("a_passed")
        loaded = m.sem("a_loaded")
        assert len(gathered) == SLOTS
        preset = m.sem("a_preset")
        folded = m.sem("a_folded")
        folded_sb = m.sem("a_folded_sb")
        S = Signals(m, "a", SLOTS,
                    gpsimd="idx_staged settled bias_added",
                    tensor="rows0_turned rows1_turned projected x_turned y_made v_made scored p_turned attended",
                    scalar="rows0_kept gate_exp0 gate_exp log_var rstd_made xT_kept v_kept p_exp pT_kept",
                    vector="rows1_kept gate_plus gated part0 part1 h0_made stats moments centred yT_kept "
                           "max_made shifted live_made live_row inv_sum inv_live att_made h_made")
        LOADS = 11

        def pipeline(eng, body):
            def step(i, k):
                def unit(lag):
                    n = i * SLOTS + k - lag
                    return not isinstance(n, int) or 0 <= n < NG, n, (k - lag) % SLOTS
                body(unit)
            for t in range(min(PEEL, TURNS) * SLOTS):
                step(t // SLOTS, t % SLOTS)
            if TURNS > PEEL:
                with eng.Fori(PEEL, TURNS) as i:
                    for k in range(SLOTS):
                        step(i, k)
            for k in range(FINISH):
                step(TURNS, k)

        with nc.Block() as block:
            @block.sync
            def _(sp):
                sp.dma_start(tok[:], dram["tokens"]).then_inc(loaded, 16)
                sp.dma_start(tokw[:, :, 0:D], dram["tok_w"].rearrange("v k n -> k v n")).then_inc(loaded, 16)
                sp.dma_start(tokwT[:], dram["tok_wT"].rearrange("v k n -> k v n")).then_inc(loaded, 16)
                sp.dma_start(wa[:], dram["tok_wa"]).then_inc(loaded, 16)
                sp.dma_start(nba[:], dram["tok_ba"]).then_inc(loaded, 16)
                sp.dma_start(qa[:], dram["a0_q"]).then_inc(loaded, 16)
                sp.dma_start(ka[:], dram["a0_k"]).then_inc(loaded, 16)
                sp.dma_start(va[:], dram["a0_v"]).then_inc(loaded, 16)
                sp.dma_start(woT[:], dram["a0_woT"]).then_inc(loaded, 16)
                sp.dma_start(bo[:], dram["a0_bo"]).then_inc(loaded, 16)
                sp.dma_start(vo[:, D + 1:D + 3], dram["a0_first"]).then_inc(loaded, 16)

            @block.gpsimd
            def _(pool):
                S.start(pool, "gpsimd")
                pool.wait_ge(loaded, 16 * LOADS)
                pool.wait_ge(preset, 2 * SLOTS + 3)

                def body(unit):
                    on, n, u = unit(0)
                    if on:
                        pool.wait_ge(S["rows1_turned"], S.past(n))
                        pool.tensor_tensor(idx[u][:], tok[:, bass.ds(n * GB, GB)],
                                           nothing[:, 0:1].to_broadcast([P, GB]), ALU.add).then_inc(S["idx_staged"], 1)
                        pool.wait_ge(S["idx_staged"], S.now(n))
                        pool.tensor_tensor(nothing[:, 1:2], nothing[:, 0:1], nothing[:, 0:1], ALU.add)\
                            .then_inc(S["settled"], 1)
                        for b in range(GB):
                            pool.indirect_dma_start(rows[u][:, b, :], None, dram["table"],
                                                    bass.IndirectOffsetOnAxis(ap=idx[u][:, b:b + 1], axis=0))\
                                .then_inc(gathered[u], 16)
                    on, n, u = unit(TURN_X)
                    if on:
                        pool.wait_ge(S["centred"], S.now(n))
                        pool.tensor_tensor(H[:, bass.ds(n * GB, GB), :], h0[u][:],
                                           bo[:, None, :].to_broadcast([P, GB, D]), ALU.add)\
                            .then_inc(S["bias_added"], 1)

                pipeline(pool, body)

            @block.tensor
            def _(pe):
                S.start(pe, "tensor")
                pe.wait_ge(loaded, 16 * LOADS)
                for k in range(2):
                    nc.tensor.matmul(b_rows[0:KE, k:k + 1], tokwT[:, k, :], wa[:], start=True, stop=True)
                nc.tensor.matmul(b_x[0:KX, 0:KX], qa[:], ka[:], start=True, stop=True)
                nc.tensor.matmul(b_y[0:KX, 0:D], va[:], woT[:], start=True, stop=True).then_inc(folded, 1)
                pe.wait_ge(folded_sb, 4)
                pe.wait_ge(preset, 2 * SLOTS + 3)

                def turn_rows(n, u, k):
                    for b in range(GB):
                        done = nc.tensor.transpose(b_rows[0:E_DIM, b * P:(b + 1) * P],
                                                   rows[u][:, b, k * E_DIM:(k + 1) * E_DIM], ident[:])
                    done.then_inc(S["rows1_turned" if k else "rows0_turned"], 1)

                def body(unit):
                    on, n, u = unit(ROWS)
                    if on:
                        pe.wait_ge(gathered[u], (n - u) * (16 * GB // SLOTS) + 16 * GB)
                        pe.wait_ge(S["rows1_kept"], S.before(n))
                        turn_rows(n, u, 0)
                    on, n, u = unit(PROJECT)
                    if on:
                        pe.wait_ge(S["rows0_kept"], S.now(n))
                        pe.wait_ge(S["rows1_kept"], S.now(n))
                        pe.wait_ge(S["part1"], S.before(n))
                        for k in range(2):
                            for b in range(GB):
                                done = nc.tensor.matmul(b_part[k][:, b * KX:(b + 1) * KX],
                                                        rowsT[u][0:KE, k, b * P:(b + 1) * P], tokw[:, k, :],
                                                        start=True, stop=True)
                        done.then_inc(S["projected"], 1)
                    on, n, u = unit(EXP)
                    if on:
                        pe.wait_ge(S["p_exp"], S.now(n))
                        pe.wait_ge(S["att_made"], S.before(n))
                        for b in range(GB):
                            done = nc.tensor.transpose(b_out[:, b * P:(b + 1) * P], pr[u][:, b * P:(b + 1) * P],
                                                       ident[:])
                        done.then_inc(S["p_turned"], 1)
                    on, n, u = unit(TURN_X)
                    if on:
                        pe.wait_ge(S["centred"], S.now(n))
                        pe.wait_ge(S["xT_kept"], S.before(n))
                        pe.sem_inc(passed, 1)
                        for b in range(GB):
                            done = nc.tensor.transpose(b_x[0:D, b * P:(b + 1) * P], xn[u][:, b, :], ident[:])
                        done.then_inc(S["x_turned"], 1)
                    on, n, u = unit(ROWS)
                    if on:
                        pe.wait_ge(S["rows0_kept"], S.now(n))
                        turn_rows(n, u, 1)
                    on, n, u = unit(VALUES)
                    if on:
                        pe.wait_ge(S["xT_kept"], S.now(n))
                        pe.wait_ge(S["yT_kept"], S.before(n))
                        nc.tensor.matmul(b_y[0:KX, :], qk[:], xT[u][:], start=True, stop=True)\
                            .then_inc(S["y_made"], 1)
                        pe.wait_ge(S["v_kept"], S.before(n))
                        for b in range(GB):
                            done = nc.tensor.matmul(b_v[:, b * (D + 3):(b + 1) * (D + 3)],
                                                    xT[u][:, b * P:(b + 1) * P], vo[:], start=True, stop=True)
                        done.then_inc(S["v_made"], 1)
                    on, n, u = unit(SCORE)
                    if on:
                        pe.wait_ge(S["yT_kept"], S.now(n))
                        pe.wait_ge(S["shifted"], S.before(n))
                        for b in range(GB):
                            done = nc.tensor.matmul(b_s[:, b * P:(b + 1) * P], yT[u][:, b * P:(b + 1) * P],
                                                    xT[u][:, b * P:(b + 1) * P], start=True, stop=True)
                        done.then_inc(S["scored"], 1)
                    on, n, u = unit(EXP)
                    if on:
                        pe.wait_ge(S["pT_kept"], S.now(n))
                        pe.wait_ge(S["v_kept"], S.now(n))
                        for b in range(GB):
                            done = nc.tensor.matmul(b_out[:, b * KX:(b + 1) * KX], pT[u][:, b * P:(b + 1) * P],
                                                    v[u][:, b, 0:KX], start=True, stop=True)
                        done.then_inc(S["attended"], 1)

                pipeline(pe, body)

            @block.scalar
            def _(act):
                S.start(act, "scalar")
                act.preload_act_table_set("natural_log_exp_and_others")
                act.wait_ge(loaded, 16 * LOADS)
                act.wait_ge(folded, 1)
                nc.scalar.activation(tokw[:, :, D], b_rows[0:KE, 0:2], ACT.Copy).then_inc(folded_sb, 1)
                nc.scalar.activation(qk[:], b_x[0:KX, 0:KX], ACT.Copy, scale=D ** -0.5)\
                    .then_inc(folded_sb, 1)
                nc.scalar.activation(vo[:, 0:D], b_y[0:KX, 0:D], ACT.Copy).then_inc(folded_sb, 1)
                nc.scalar.activation(nba[:], nba[:], ACT.Copy, scale=-1.0).then_inc(folded_sb, 1)
                act.wait_ge(folded_sb, 4)
                act.wait_ge(preset, 2 * SLOTS + 3)

                def body(unit):
                    on, n, u = unit(EXP)
                    if on:
                        act.wait_ge(S["shifted"], S.now(n))
                        nc.scalar.activation(pr[u][:], pr[u][:], ACT.Exp).then_inc(S["p_exp"], 1)
                    on, n, u = unit(CENTRE)
                    if on:
                        act.wait_ge(S["moments"], S.now(n))
                        act.wait_ge(S["centred"], S.past(n))
                        nc.scalar.activation(rstd[u][:], mv[u][:, :, 1], ACT.Ln, bias=1e-5).then_inc(S["log_var"], 1)
                        act.wait_ge(S["log_var"], S.now(n))
                        nc.scalar.activation(rstd[u][:], rstd[u][:], ACT.Exp, scale=-0.5).then_inc(S["rstd_made"], 1)
                    on, n, u = unit(SCORE)
                    if on:
                        act.wait_ge(S["v_made"], S.now(n))
                        act.wait_ge(S["attended"], S.past(n))
                        act.wait_ge(S["live_made"], S.past(n))
                        nc.scalar.activation(v[u][:], grouped(b_v[:, 0:GB * (D + 3)], D + 3), ACT.Copy)\
                            .then_inc(S["v_kept"], 1)
                    on, n, u = unit(ROWS)
                    if on:
                        act.wait_ge(S["rows0_turned"], S.now(n))
                        act.wait_ge(S["projected"], S.past(n))
                        nc.scalar.activation(rowsT[u][0:E_DIM, 0, :], b_rows[0:E_DIM, :], ACT.Copy)\
                            .then_inc(S["rows0_kept"], 1)
                    on, n, u = unit(PROJECT)
                    if on:
                        act.wait_ge(S["projected"], S.now(n))
                        act.wait_ge(S["part1"], S.past(n))
                        for k in range(2):
                            logit = grouped(b_part[k][:, 0:GB * KX], KX)[:, :, D]
                            nc.scalar.activation(gate[u][:, k, :], logit, ACT.Exp, bias=nba[:, 0:1], scale=-1.0)\
                                .then_inc(S["gate_exp"] if k else S["gate_exp0"], 1)
                    on, n, u = unit(EXP)
                    if on:
                        act.wait_ge(S["p_turned"], S.now(n))
                        act.wait_ge(S["attended"], S.past(n))
                        nc.scalar.activation(pT[u][:], b_out[:], ACT.Copy).then_inc(S["pT_kept"], 1)
                    on, n, u = unit(TURN_X)
                    if on:
                        act.wait_ge(S["x_turned"], S.now(n))
                        act.wait_ge(S["scored"], S.past(n))
                        nc.scalar.activation(xT[u][0:D, :], b_x[0:D, :], ACT.Copy).then_inc(S["xT_kept"], 1)

                pipeline(act, body)

            @block.vector
            def _(dve):
                S.start(dve, "vector")
                nc.vector.memset(nothing[:], 0).then_inc(preset, 1)
                for u in range(SLOTS):
                    nc.vector.memset(rowsT[u][64:P, :, :], 1.0).then_inc(preset, 1)
                    nc.vector.memset(xT[u][D:KX, :], 1.0).then_inc(preset, 1)
                nc.vector.memset(vo[0:D, D:D + 1], 0.0).then_inc(preset, 1)
                nc.vector.memset(vo[D:KX, D:D + 1], 1.0).then_inc(preset, 1)
                dve.wait_ge(preset, 2 * SLOTS + 3)

                def body(unit):
                    on9, n9, u9 = unit(FINISH)
                    on7, n7, u7 = unit(MAX)
                    if on9:
                        dve.wait_ge(S["attended"], S.now(n9))
                        nc.vector.reciprocal(rs[u9][:], grouped(b_out[:, 0:GB * KX], KX)[:, :, D])\
                            .then_inc(S["inv_sum"], 1)
                        dve.wait_ge(S["v_kept"], S.now(n9))
                        nc.vector.tensor_scalar(live[u9][:], v[u9][:, :, D + 1:D + 3], 0.0, None, ALU.not_equal)\
                            .then_inc(S["live_made"], 1)
                    on, n, u = unit(SCORE)
                    if on:
                        dve.wait_ge(S["y_made"], S.now(n))
                        dve.wait_ge(S["scored"], S.past(n))
                        nc.vector.tensor_copy(yT[u][:], b_y[0:KX, :]).then_inc(S["yT_kept"], 1)
                    if on9:
                        dve.wait_ge(S["inv_sum"], S.now(n9))
                        dve.wait_ge(S["live_made"], S.now(n9))
                        nc.vector.tensor_tensor(rs[u9][:], rs[u9][:], live[u9][:, :, 0], ALU.mult)\
                            .then_inc(S["live_row"], 1)
                    if on7:
                        dve.wait_ge(S["scored"], S.now(n7))
                        nc.vector.tensor_reduce(mx[u7][:], grouped(b_s[:], P), AX, ALU.max).then_inc(S["max_made"], 1)
                    if on9:
                        dve.wait_ge(S["live_row"], S.now(n9))
                        nc.vector.tensor_tensor(rs[u9][:], rs[u9][:], live[u9][:, :, 1], ALU.mult)\
                            .then_inc(S["inv_live"], 1)
                        dve.wait_ge(S["inv_live"], S.now(n9))
                        nc.vector.tensor_tensor(att[u9][:], grouped(b_out[:, 0:GB * KX], KX)[:, :, 0:D],
                                                over(rs[u9][:], D), ALU.mult).then_inc(S["att_made"], 1)
                    if on7:
                        dve.wait_ge(S["max_made"], S.now(n7))
                        dve.wait_ge(S["p_turned"], S.past(n7))
                        nc.vector.tensor_tensor(grouped(pr[u7][:], P), grouped(b_s[:], P), over(mx[u7][:], P),
                                                ALU.subtract).then_inc(S["shifted"], 1)
                    if on9:
                        dve.wait_ge(S["att_made"], S.now(n9))
                        dve.wait_ge(S["bias_added"], S.now(n9))
                        hs = H[:, bass.ds(n9 * GB, GB), :]
                        nc.vector.tensor_tensor(hs, hs, att[u9][:], ALU.add).then_inc(S["h_made"], 1)
                    on, n, u = unit(CENTRE)
                    if on:
                        dve.wait_ge(S["rstd_made"], S.now(n))
                        dve.wait_ge(S["x_turned"], S.past(n))
                        for b in range(GB):
                            done = nc.vector.tensor_scalar(xn[u][:, b, :], h0[u][:, b, :], mv[u][:, b, 0:1],
                                                           rstd[u][:, b:b + 1], ALU.subtract, ALU.mult)
                        done.then_inc(S["centred"], 1)
                    on, n, u = unit(ROWS)
                    if on:
                        dve.wait_ge(S["rows1_turned"], S.now(n))
                        dve.wait_ge(S["projected"], S.past(n))
                        nc.vector.tensor_copy(rowsT[u][0:E_DIM, 1, :], b_rows[0:E_DIM, :]).then_inc(S["rows1_kept"], 1)
                    on, n, u = unit(PROJECT)
                    if on:
                        dve.wait_ge(S["gate_exp"], S.now(n))
                        nc.vector.tensor_scalar(gate[u][:], gate[u][:], 1.0, None, ALU.add).then_inc(S["gate_plus"], 1)
                        dve.wait_ge(S["gate_plus"], S.now(n))
                        nc.vector.reciprocal(gate[u][:], gate[u][:]).then_inc(S["gated"], 1)
                        dve.wait_ge(S["gated"], S.now(n))
                        for k in range(2):
                            nc.vector.tensor_tensor(part[u][:, k], grouped(b_part[k][:, 0:GB * KX], KX)[:, :, 0:D],
                                                    over(gate[u][:, k, :], D), ALU.mult)\
                                .then_inc(S["part1"] if k else S["part0"], 1)
                        dve.wait_ge(S["part1"], S.now(n))
                        dve.wait_ge(S["bias_added"], S.past(n))
                        nc.vector.tensor_tensor(h0[u][:], part[u][:, 0], part[u][:, 1], ALU.add)\
                            .then_inc(S["h0_made"], 1)
                        dve.wait_ge(S["h0_made"], S.now(n))
                        for b in range(GB):
                            done = nc.vector.bn_stats(st[u][:, b, :], h0[u][:, b, :])
                        done.then_inc(S["stats"], 1)
                        dve.wait_ge(S["stats"], S.now(n))
                        dve.wait_ge(S["rstd_made"], S.past(n))
                        dve.sem_inc(passed, 1)
                        for b in range(GB):
                            done = nc.vector.bn_aggr(mv[u][:, b, :], st[u][:, b, :])
                        done.then_inc(S["moments"], 1)

                pipeline(dve, body)
        m.clear_semaphores()


def phase_block_attention(nc, dram, H, flatT, logits, ident, NB):
    NH, HD, NKV = 4, 16, 2
    NE = dram["router"].shape[1]
    STRIP = P // NH
    NG = NB // GB
    GQ = NH
    NQ = NG * GQ
    SLOTS = 4
    TURN = 2 * GQ
    TURNS = NQ // TURN
    AHEAD = 3
    LAG_EXP, LAG_TURN, LAG_PV, LAG_KEEP, LAG_Y = 1, 2, 3, 4, 5
    assert NQ % TURN == 0 and TURNS >= 2
    with ExitStack() as ctx:
        m = Mem(nc, ctx)
        wq = m.sb("f_wq", [D, P])
        wk = m.sb("f_wk", [D, P])
        wkp = m.sb("f_wkp", [D, P])
        wv = m.sb("f_wv", [D, NKV * HD])
        wo = m.sb("f_wo", [D, D])
        ln1 = m.sb("f_ln1", [D, 1])
        ln2 = m.sb("f_ln2", [D, 1])
        router = m.sb("f_router", [D, NE])
        rope_q = m.sb("rope_q", [P, P])
        cos_k = m.sb("cos_k", [P, P])
        sin_k = m.sb("sin_k", [P, P])
        hide_f = m.sb("hide_f", [P, P])
        hide = m.sb("hide", [P, P], BF16)
        ident_b = m.sb("ident_b", [P, P], BF16)

        x = m.sb("b_x", [P, NB + AHEAD * GB, D])
        st, mv, rstd = m.sb("b_st", [P, GB, 6]), m.sb("b_mv", [P, GB, 2]), m.sb("b_rstd", [P, GB])
        msq, rms = m.sb("b_msq", [P, GB]), m.sb("b_rms", [P, GB])
        xn, xT = m.sb("b_xn", [P, GB, D]), m.sb("b_xT", [D, W])
        q = [m.sb(f"b_q{s}", [P, W]) for s in range(2)]
        k0 = [m.sb(f"b_k0{s}", [P, W]) for s in range(2)]
        k1 = m.sb("b_k1", [P, W])
        v = [m.sb(f"b_v{s}", [P, GB, NKV, STRIP]) for s in range(2)]
        mx = [m.sb(f"b_mx{u}", [P, GB]) for u in range(SLOTS)]
        pr = [m.sb(f"b_pr{u}", [P, W]) for u in range(SLOTS)]
        pT = [m.sb(f"b_pT{u}", [P, W]) for u in range(SLOTS)]
        attT = m.sb("b_attT", [P, W])
        inv = m.sb("b_inv", [P, GB, NH])
        y, yT = m.sb("b_y", [P, GB, D]), m.sb("b_yT", [D, W])
        x2, sq, ss = m.sb("b_x2", [P, GB, D]), m.sb("b_sq", [P, GB, D]), m.sb("b_ss", [P, GB])
        fl, flT = m.sb("b_fl", [P, GB, 2, D]), m.sb("b_flT", [P, W])
        bS = [m.ps(f"b_S{u}", [P, 512]) for u in range(2)]
        bT = m.ps("b_T", [P, 512])
        bO = m.ps("b_O", [P, 512])
        bX = [m.ps(f"b_X{u}", [P, 512]) for u in range(4)]

        passed = m.sem("b_passed")
        loaded = m.sem("b_loaded")
        ready = m.sem("b_ready")
        S = Signals(m, "b", SLOTS, tensor="scored turned attended", scalar="exped pT_kept",
                    vector="max_made shifted")
        G = Signals(m, "bg", 4,
                    gpsimd="xn_made k_made h_made flat_made flatT_kept",
                    tensor="x_turned q_made k0_made k1_made v_made back y_turned out_made flat_turned routed",
                    scalar="log_var rstd_made log_msq rms_made xT_kept v_kept attT_kept yT_kept "
                           "log_ss rms2_made flT_kept logits_kept",
                    vector="stats moments rstd_sq msq_made centred q_kept k0_kept k1_kept inv_sum y_made "
                           "x2_made squared summed")
        LOADS, READY = 12, 14

        def group_of(i, k, lag=0):
            return i * (TURN // GQ) + (k - lag) // GQ

        def on_back(k, lo, hi):
            return lo <= k - LAG_KEEP < hi and (k - LAG_KEEP) % GQ == GQ - 1

        def known(n, least):
            return not (isinstance(n, int) and n < least)

        class Beside:
            def norm(self, n, j): pass
            def turn(self, n, j): pass
            def project(self, n, s, j): pass
            def output(self, n, j): pass
            def route(self, n, j): pass

        def beside(i, k, work):
            j, n, s = k % GQ, group_of(i, k), (k // GQ) % 2
            if not (isinstance(i, int) and i == TURNS):
                work.norm(n + 3, j)
                work.turn(n + 2, j)
                work.project(n + 1, 1 - s, j)
            if known(n, 2) and not (isinstance(n, int) and n - 2 >= NG):
                work.output(n - 2, j)
            if known(n, 3):
                work.route(n - 3, j)

        def pipeline(body, eng, work):
            for n in range(-3, 0):
                for j in range(GQ):
                    work.norm(n + 3, j)
                    if n >= -2:
                        work.turn(n + 2, j)
                    if n >= -1:
                        work.project(n + 1, 0, j)
            for k in range(TURN):
                body(0, k, 0, TURN)
            for k in range(TURN):
                body(1, k, -TURN, TURN)
            if TURNS > 2:
                with eng.Fori(2, TURNS) as i:
                    for k in range(TURN):
                        body(i, k, -TURN, TURN)
            for k in range(3 * GQ):
                body(TURNS, k, -TURN, 0)

        def last(n):
            return min(n, NG) if isinstance(n, int) else n

        with nc.Block() as block:
            @block.sync
            def _(sp):
                for dst, name in ((wq, "f_wq"), (wk, "f_wk"), (wkp, "f_wkp"), (wv, "f_wv"), (wo, "f_wo"),
                                  (ln1, "f_ln1"), (ln2, "f_ln2"), (router, "router"), (rope_q, "rope_q"),
                                  (cos_k, "cos_k"), (sin_k, "sin_k"), (hide_f, "hide")):
                    sp.dma_start(dst[:], dram[name]).then_inc(loaded, 16)

            @block.gpsimd
            def _(pool):
                G.start(pool, "gpsimd")
                pool.wait_ge(ready, READY)

                class Work(Beside):
                    def turn(self, n, j):
                        if j == 1:
                            pool.wait_ge(G["rms_made"], G.now(n))
                            pool.wait_ge(G["centred"], G.now(n))
                            pool.wait_ge(G["x_turned"], G.before(n))
                            pool.tensor_tensor(xn[:], x[:, bass.ds(n * GB, GB), :], over(rms[:], D), ALU.mult)\
                                .then_inc(G["xn_made"], 1)

                    def project(self, n, s, j):
                        if j == 2:
                            pool.wait_ge(G["k0_kept"], G.now(n))
                            pool.wait_ge(G["k1_kept"], G.now(n))
                            pool.tensor_tensor(k0[s][:], k0[s][:], k1[:], ALU.add).then_inc(G["k_made"], 1)

                    def output(self, n, j):
                        if j == 2:
                            pool.wait_ge(G["x2_made"], G.now(n))
                            hs = H[:, bass.ds(n * GB, GB), :]
                            pool.tensor_tensor(hs, hs, x2[:], ALU.add).then_inc(G["h_made"], 1)

                    def route(self, n, j):
                        if j == 0:
                            pool.wait_ge(G["rms2_made"], G.now(n))
                            pool.wait_ge(G["flat_turned"], G.before(n))
                            for half in range(2):
                                done = pool.tensor_tensor(fl[:, :, half, :], x2[:], over(ss[:], D), ALU.mult)
                            done.then_inc(G["flat_made"], 1)
                        if j == 3:
                            pool.wait_ge(G["flT_kept"], G.now(n))
                            pool.sem_inc(passed, 1)
                            pool.tensor_copy(flatT[:, bass.ds(n * W, W)], flT[:]).then_inc(G["flatT_kept"], 1)

                work = Work()
                pipeline(lambda i, k, lo, hi: beside(i, k, work), pool, work)

            @block.tensor
            def _(pe):
                S.start(pe, "tensor")
                G.start(pe, "tensor")
                pe.wait_ge(ready, READY)

                class Work(Beside):
                    def turn(self, n, j):
                        if j == 2:
                            pe.wait_ge(G["xn_made"], G.now(n))
                            pe.wait_ge(G["k0_kept"], G.before(n))
                            pe.sem_inc(passed, 1)
                            for b in range(GB):
                                done = nc.tensor.transpose(bX[0][0:D, b * P:(b + 1) * P], xn[:, b, :], ident[:])
                            done.then_inc(G["x_turned"], 1)
                        if j == 3:
                            pe.wait_ge(G["xT_kept"], G.now(n))
                            pe.wait_ge(G["q_kept"], G.before(n))
                            if known(n, 4):
                                pe.wait_ge(G["x2_made"], G.now(n - 4))
                            nc.tensor.matmul(bX[1][:], wq[:], xT[:], start=True, stop=True).then_inc(G["q_made"], 1)

                    def project(self, n, s, j):
                        if j == 0:
                            nc.tensor.matmul(bX[0][:], wk[:], xT[:], start=True, stop=True).then_inc(G["k0_made"], 1)
                            pe.wait_ge(G["k1_kept"], G.before(n))
                            if known(n, 5):
                                pe.wait_ge(G["logits_kept"], G.now(n - 5))
                            nc.tensor.matmul(bX[3][:], wkp[:], xT[:], start=True, stop=True).then_inc(G["k1_made"], 1)
                        if j == 1:
                            pe.wait_ge(G["v_kept"], G.before(n))
                            if known(n, 3):
                                pe.wait_ge(G["yT_kept"], G.now(n - 3))
                            for b in range(GB):
                                done = nc.tensor.matmul(bX[2][:, b * NKV * HD:(b + 1) * NKV * HD],
                                                        xT[:, b * P:(b + 1) * P], wv[:], start=True, stop=True)
                            done.then_inc(G["v_made"], 1)

                    def output(self, n, j):
                        if j == 0:
                            pe.wait_ge(G["y_made"], G.now(n))
                            pe.wait_ge(G["v_kept"], G.now(last(n + 2)))
                            pe.wait_ge(G["yT_kept"], G.before(n))
                            pe.sem_inc(passed, 1)
                            for b in range(GB):
                                done = nc.tensor.transpose(bX[2][0:D, b * P:(b + 1) * P], y[:, b, :], ident[:])
                            done.then_inc(G["y_turned"], 1)
                        if j == 1:
                            pe.wait_ge(G["yT_kept"], G.now(n))
                            pe.wait_ge(G["q_kept"], G.now(last(n + 3)))
                            pe.wait_ge(G["x2_made"], G.before(n))
                            for b in range(GB):
                                done = nc.tensor.matmul(bX[1][:, b * D:(b + 1) * D], yT[:, b * P:(b + 1) * P], wo[:],
                                                        start=True, stop=True)
                            done.then_inc(G["out_made"], 1)

                    def route(self, n, j):
                        if j == 1:
                            pe.wait_ge(G["flat_made"], G.now(n))
                            pe.wait_ge(G["k1_kept"], G.now(last(n + 4)))
                            pe.wait_ge(G["logits_kept"], G.before(n))
                            for b in range(GB):
                                done = nc.tensor.transpose(bX[3][:, b * P:(b + 1) * P],
                                                           fl[:, b].rearrange("p k d -> p (k d)"), ident[:])
                            done.then_inc(G["flat_turned"], 1)
                        if j == 2:
                            pe.wait_ge(G["flT_kept"], G.now(n))
                            for b in range(GB):
                                done = nc.tensor.matmul(bX[3][:, b * NE:(b + 1) * NE], flT[0:D, b * P:(b + 1) * P],
                                                        router[:], start=True, stop=True)
                            done.then_inc(G["routed"], 1)

                def body(i, k, lo, hi):
                    t = i * TURN + k

                    def unit(lag):
                        return lo <= k - lag < hi, t - lag, (k - lag) % SLOTS
                    on, n, u = unit(0)
                    if on:
                        s, h = (k // GQ) % 2, k % GQ
                        if h == 0:
                            pe.wait_ge(G["q_kept"], G.now(group_of(i, k)))
                            pe.wait_ge(G["k_made"], G.now(group_of(i, k)))
                        pe.wait_ge(S["shifted"], S.ago(n, 2))
                        nc.tensor.matmul(bS[u % 2][:], ident_b[:], hide[:, None, :].to_broadcast([P, GB, P]),
                                         start=True, stop=False)
                        r = slice(STRIP * h, STRIP * (h + 1))
                        for b in range(GB):
                            c = slice(b * P, (b + 1) * P)
                            done = nc.tensor.matmul(bS[u % 2][:, c], q[s][r, c], k0[s][r, c], start=False,
                                                    stop=(b == GB - 1))
                        done.then_inc(S["scored"], 1)
                    on, n, u = unit(LAG_TURN)
                    if on:
                        pe.wait_ge(S["exped"], S.now(n))
                        pe.wait_ge(S["pT_kept"], S.before(n))
                        if on_back(k - 1, lo, hi):
                            pe.wait_ge(G["y_made"], G.now(group_of(i, k - 1, LAG_KEEP)))
                        for b in range(GB):
                            c = slice(b * P, (b + 1) * P)
                            done = nc.tensor.transpose(bT[:, c], pr[u][:, c], ident[:])
                        done.then_inc(S["turned"], 1)
                    on, n, u = unit(LAG_PV)
                    if on:
                        j = k - LAG_PV
                        s, h = (j // GQ) % 2, j % GQ
                        if h == 0:
                            pe.wait_ge(G["v_kept"], G.now(group_of(i, k, LAG_PV)))
                            pe.wait_ge(G["attT_kept"], G.before(group_of(i, k, LAG_PV)))
                        pe.wait_ge(S["pT_kept"], S.now(n))
                        for b in range(GB):
                            c = slice(b * P, (b + 1) * P)
                            done = nc.tensor.matmul(bO[STRIP * h:STRIP * (h + 1), c], v[s][:, b, h * NKV // NH, :],
                                                    pT[u][:, c], start=True, stop=True)
                        done.then_inc(S["attended"], 1)
                    beside(i, k, work)
                    if on_back(k, lo, hi):
                        pe.wait_ge(G["attT_kept"], G.now(group_of(i, k, LAG_KEEP)))
                        on, n, _ = unit(LAG_TURN)
                        if on:
                            pe.wait_ge(S["pT_kept"], S.now(n))
                        for b in range(GB):
                            c = slice(b * P, (b + 1) * P)
                            done = nc.tensor.transpose(bT[:, c], attT[:, c], ident[:])
                        done.then_inc(G["back"], 1)

                work = Work()
                pipeline(body, pe, work)

            @block.scalar
            def _(act):
                S.start(act, "scalar")
                G.start(act, "scalar")
                act.preload_act_table_set("natural_log_exp_and_others")
                act.wait_ge(ready, READY)

                class Copies(Beside):
                    def turn(self, n, j):
                        if j == 3:
                            act.wait_ge(G["x_turned"], G.now(n))
                            act.wait_ge(G["v_made"], G.before(n))
                            nc.scalar.activation(xT[:], bX[0][0:D, :], ACT.Copy).then_inc(G["xT_kept"], 1)

                    def project(self, n, s, j):
                        if j == 3:
                            act.wait_ge(G["v_made"], G.now(n))
                            if known(n, 2):
                                act.wait_ge(S["attended"], S.now(n * GQ - GQ - 1))
                            nc.scalar.activation(v[s][:].rearrange("p b k e -> p (b k) e")[:, :, 0:HD],
                                                 grouped(bX[2][:, 0:GB * NKV * HD], HD), ACT.Copy)\
                                .then_inc(G["v_kept"], 1)

                    def output(self, n, j):
                        if j == 1:
                            act.wait_ge(G["y_turned"], G.now(n))
                            act.wait_ge(G["out_made"], G.before(n))
                            nc.scalar.activation(yT[:], bX[2][0:D, :], ACT.Copy).then_inc(G["yT_kept"], 1)

                    def route(self, n, j):
                        if j == 2:
                            act.wait_ge(G["flat_turned"], G.now(n))
                            act.wait_ge(G["routed"], G.before(n))
                            act.wait_ge(G["flatT_kept"], G.before(n))
                            nc.scalar.activation(flT[:], bX[3][:], ACT.Copy).then_inc(G["flT_kept"], 1)
                        if j == 3:
                            act.wait_ge(G["routed"], G.now(n))
                            nc.scalar.activation(logits[:, bass.ds(n * GB, GB), :],
                                                 grouped(bX[3][:, 0:GB * NE], NE), ACT.Copy)\
                                .then_inc(G["logits_kept"], 1)

                class Rates(Beside):
                    def norm(self, n, j):
                        if j == 3:
                            act.wait_ge(G["moments"], G.now(n))
                            act.wait_ge(G["centred"], G.before(n))
                            nc.scalar.activation(rstd[:], mv[:, :, 1], ACT.Ln, bias=1e-5).then_inc(G["log_var"], 1)
                            act.wait_ge(G["log_var"], G.now(n))
                            nc.scalar.activation(rstd[:], rstd[:], ACT.Exp, scale=-0.5).then_inc(G["rstd_made"], 1)

                    def turn(self, n, j):
                        if j == 0:
                            act.wait_ge(G["msq_made"], G.now(n))
                            act.wait_ge(G["xn_made"], G.before(n))
                            nc.scalar.activation(rms[:], msq[:], ACT.Ln, bias=1e-6).then_inc(G["log_msq"], 1)
                            act.wait_ge(G["log_msq"], G.now(n))
                            nc.scalar.activation(rms[:], rms[:], ACT.Exp, scale=-0.5).then_inc(G["rms_made"], 1)

                    def output(self, n, j):
                        if j == 3:
                            act.wait_ge(G["summed"], G.now(n))
                            nc.scalar.activation(ss[:], ss[:], ACT.Ln, scale=1.0 / D, bias=1e-6)\
                                .then_inc(G["log_ss"], 1)
                            act.wait_ge(G["log_ss"], G.now(n))
                            nc.scalar.activation(ss[:], ss[:], ACT.Exp, scale=-0.5).then_inc(G["rms2_made"], 1)

                class Both(Beside):
                    def norm(self, n, j):
                        rates.norm(n, j)

                    def turn(self, n, j):
                        copies.turn(n, j)
                        rates.turn(n, j)

                    def project(self, n, s, j):
                        copies.project(n, s, j)

                def body(i, k, lo, hi):
                    t = i * TURN + k

                    def unit(lag):
                        return lo <= k - lag < hi, t - lag, (k - lag) % SLOTS
                    if on_back(k, lo, hi):
                        n = group_of(i, k, LAG_KEEP)
                        act.wait_ge(S["attended"], S.now(t - LAG_KEEP))
                        act.wait_ge(G["back"], G.before(n))
                        nc.scalar.activation(attT[:], bO[:], ACT.Copy).then_inc(G["attT_kept"], 1)
                    on, n, u = unit(LAG_EXP)
                    if on:
                        act.wait_ge(S["shifted"], S.now(n))
                        nc.scalar.activation(pr[u][:], pr[u][:], ACT.Exp).then_inc(S["exped"], 1)
                    beside(i, k, copies)
                    on, n, u = unit(LAG_TURN)
                    if on:
                        act.wait_ge(S["turned"], S.now(n))
                        act.wait_ge(S["attended"], S.past(n))
                        nc.scalar.activation(pT[u][:], bT[:], ACT.Copy).then_inc(S["pT_kept"], 1)
                    beside(i, k, rates)

                copies, rates = Copies(), Rates()
                pipeline(body, act, Both())

            @block.vector
            def _(dve):
                S.start(dve, "vector")
                G.start(dve, "vector")
                dve.wait_ge(loaded, 16 * LOADS)
                for w, g in ((wq, ln1), (wk, ln1), (wkp, ln1), (wv, ln1), (router, ln2)):
                    nc.vector.tensor_scalar(w[:], w[:], g[:, 0:1], None, ALU.mult).then_inc(ready, 1)
                nc.vector.tensor_copy(hide[:], hide_f[:]).then_inc(ready, 1)
                nc.vector.tensor_copy(ident_b[:], ident[:]).then_inc(ready, 1)
                for s in range(2):
                    nc.vector.memset(v[s][:, :, :, HD:HD + 1], 1.0).then_inc(ready, 1)
                    nc.vector.memset(v[s][:, :, :, HD + 1:], 0.0).then_inc(ready, 1)
                nc.vector.memset(ss[:], 0.0).then_inc(ready, 1)
                nc.vector.memset(rstd[:], 0.0).then_inc(ready, 1)
                nc.vector.memset(H[:, NB:NB + AHEAD * GB, :], 0.0).then_inc(ready, 1)
                dve.wait_ge(ready, READY)

                class Work(Beside):
                    def norm(self, n, j):
                        if j == 3:
                            dve.wait_ge(G["centred"], G.before(n))
                            for b in range(GB):
                                done = nc.vector.bn_stats(
                                    st[:, b, :], H[:, bass.ds(n * GB + b, 1), :].rearrange("p b d -> p (b d)"))
                            done.then_inc(G["stats"], 1)
                            dve.wait_ge(G["stats"], G.now(n))
                            dve.sem_inc(passed, 1)
                            for b in range(GB):
                                done = nc.vector.bn_aggr(mv[:, b, :], st[:, b, :])
                            done.then_inc(G["moments"], 1)

                    def turn(self, n, j):
                        if j == 0:
                            dve.wait_ge(G["rstd_made"], G.now(n))
                            dve.wait_ge(G["rms_made"], G.before(n))
                            nc.vector.tensor_tensor(msq[:], rstd[:], rstd[:], ALU.mult).then_inc(G["rstd_sq"], 1)
                            for b in range(GB):
                                xs, hs = [a[:, bass.ds(n * GB + b, 1), :].rearrange("p b d -> p (b d)") for a in (x, H)]
                                done = nc.vector.tensor_scalar(xs, hs, mv[:, b, 0:1], rstd[:, b:b + 1],
                                                               ALU.subtract, ALU.mult)
                            done.then_inc(G["centred"], 1)
                            dve.wait_ge(G["rstd_sq"], G.now(n))
                            nc.vector.tensor_tensor(msq[:], msq[:], mv[:, :, 1], ALU.mult).then_inc(G["msq_made"], 1)

                    def rope(self, n, dst, src, table, made, kept):
                        dve.wait_ge(G[made], G.now(n))
                        nc.vector.tensor_tensor(grouped(dst[:], P), grouped(bX[src][:], P),
                                                table[:, None, :].to_broadcast([P, GB, P]), ALU.mult)\
                            .then_inc(G[kept], 1)

                    def project(self, n, s, j):
                        if j == 0:
                            if known(n, 2):
                                dve.wait_ge(S["scored"], S.now(n * GQ - GQ - 1))
                            self.rope(n, q[s], 1, rope_q, "q_made", "q_kept")
                        if j == 1:
                            dve.wait_ge(G["k_made"], G.before(n))
                            self.rope(n, k0[s], 0, cos_k, "k0_made", "k0_kept")
                            self.rope(n, k1, 3, sin_k, "k1_made", "k1_kept")

                    def output(self, n, j):
                        if j == 2:
                            dve.wait_ge(G["out_made"], G.now(n))
                            dve.wait_ge(G["h_made"], G.before(n))
                            dve.wait_ge(G["flat_made"], G.before(n))
                            nc.vector.tensor_tensor(x2[:], grouped(bX[1][:, 0:GB * D], D),
                                                    x[:, bass.ds(n * GB, GB), :], ALU.add).then_inc(G["x2_made"], 1)
                            dve.wait_ge(G["x2_made"], G.now(n))
                            nc.vector.tensor_tensor(sq[:], x2[:], x2[:], ALU.mult).then_inc(G["squared"], 1)
                        if j == 3:
                            dve.wait_ge(G["squared"], G.now(n))
                            nc.vector.tensor_reduce(ss[:], sq[:], AX, ALU.add).then_inc(G["summed"], 1)

                def body(i, k, lo, hi):
                    t = i * TURN + k
                    on, u = lo <= k < hi, k % SLOTS
                    if lo <= k - LAG_Y < hi and (k - LAG_Y) % GQ == GQ - 1:
                        n = group_of(i, k, LAG_Y)
                        sums = bT[:].rearrange("p (b h e) -> p b h e", h=NH, e=STRIP)
                        dve.wait_ge(G["back"], G.now(n))
                        nc.vector.reciprocal(inv[:], sums[:, :, :, HD]).then_inc(G["inv_sum"], 1)
                        dve.wait_ge(G["inv_sum"], G.now(n))
                        dve.wait_ge(G["y_turned"], G.before(n))
                        nc.vector.tensor_tensor(y[:].rearrange("p b (h e) -> p b h e", h=NH), sums[:, :, :, 0:HD],
                                                inv[:, :, :, None].to_broadcast([P, GB, NH, HD]), ALU.mult)\
                            .then_inc(G["y_made"], 1)
                    if on:
                        dve.wait_ge(S["scored"], S.now(t))
                        nc.vector.tensor_reduce(mx[u][:], grouped(bS[u % 2][:], P), AX, ALU.max)\
                            .then_inc(S["max_made"], 1)
                        dve.wait_ge(S["max_made"], S.now(t))
                        dve.wait_ge(S["turned"], S.past(t))
                        nc.vector.tensor_tensor(grouped(pr[u][:], P), grouped(bS[u % 2][:], P), over(mx[u][:], P),
                                                ALU.subtract).then_inc(S["shifted"], 1)
                    beside(i, k, work)

                work = Work()
                pipeline(body, dve, work)
        m.clear_semaphores()


def phase_experts(nc, dram, H, flatT, logits, ident, NB):
    NE = dram["router"].shape[1]
    NCH = dram["e_w1"].shape[1] // P
    PARTS = 3
    NG = NB // GB
    SLOTS = 2
    PER = SLOTS * NCH
    with ExitStack() as ctx:
        m = Mem(nc, ctx)
        w1 = m.sb("e_w1", [P, NCH * P])
        w3 = m.sb("e_w3", [P, NCH * P])
        w1_parts = [m.sb(f"e_w1_{name}", [P, NCH * P], BF16) for name in ("hh", "mm", "lh")]
        w3_parts = [m.sb(f"e_w3_{name}", [P, NCH * P], BF16) for name in ("hh", "mm", "lh")]
        x_hm = [m.sb(f"x_hm{u}", [P, W], BF16) for u in range(SLOTS)]
        x_hl = [m.sb(f"x_hl{u}", [P, W], BF16) for u in range(SLOTS)]
        x_rest = m.sb("x_rest", [P, W])
        w2 = m.sb("e_w2", [P, NCH, D])
        ln2 = m.sb("e_ln2", [P, 1])
        owner_f = m.sb("owner_f", [PARTS * NE, NCH * P])
        owner = m.sb("owner", [PARTS * NE, NCH * P], BF16)
        rank = m.sb("rank", [P, NE])
        wts = m.sb("wts", [P, NB + GB, PARTS, NE])
        ex = m.sb("ex", [P, NB, NE])
        tie = m.sb("tie", [P, NB, NE])
        pick = m.sb("pick", [P, NB, NE])
        both = m.sb("both", [P, NB, NE])
        low = m.sb("low", [P, NB, NE], BF16)
        top = m.sb("top", [P, NB])
        total = m.sb("total", [P, NB])
        wnow = [m.sb(f"wnow{u}", [P, GB, PARTS * NE]) for u in range(SLOTS)]
        wT = [m.sb(f"wT{u}", [PARTS * NE, W], BF16) for u in range(SLOTS)]
        act1 = [m.sb(f"act1{u}", [P, W]) for u in range(SLOTS)]
        prod = [m.sb(f"prod{u}", [P, W]) for u in range(SLOTS)]
        hid = [m.sb(f"hid{u}", [P, W]) for u in range(SLOTS)]
        b1 = [m.ps(f"c_h1{u}", [P, 512]) for u in range(SLOTS)]
        b3 = [m.ps(f"c_h3{u}", [P, 512]) for u in range(SLOTS)]
        bw = [m.ps(f"c_wb{u}", [P, 512]) for u in range(SLOTS)]
        bo = m.ps("c_out", [P, 512])
        bt = m.ps("c_turn", [P, 512])

        passed = m.sem("c_passed")
        loaded = m.sem("c_loaded")
        ready = m.sem("c_ready")
        shifted = m.sem("c_shifted")
        exped = m.sem("c_exped")
        route = m.sem("c_route")
        w_scaled, w_high, w_rest, w_mid = [m.sem(f"c_w_{name}") for name in ("scaled", "high", "rest", "mid")]
        parted = m.sem("c_parted")
        S = Signals(m, "c", SLOTS, tensor="h1_made h3_made wb_made summed", scalar="activated",
                    vector="multiplied weighted")
        G = Signals(m, "cg", SLOTS, tensor="w_turned", scalar="w_staged wT_kept high_kept mid_kept high2_kept",
                    vector="h_made", gpsimd="rest_made low_made")
        LOADS = 6
        READY = 7
        LAG = 2
        TURNS = NG // SLOTS
        assert NG % SLOTS == 0 and TURNS > 1
        ROUTE = 18 + 2 * PARTS

        with nc.Block() as block:
            @block.sync
            def _(sp):
                for dst, name in ((w1, "e_w1"), (w3, "e_w3"), (ln2, "e_ln2"), (owner_f, "owner"), (rank, "rank")):
                    sp.dma_start(dst[:], dram[name]).then_inc(loaded, 16)
                sp.dma_start(w2[:], dram["e_w2"].rearrange("(c p) n -> p c n", p=P)).then_inc(loaded, 16)

            def pipeline(eng, body, prepare):
                for k in range(NCH):
                    prepare(0, 0, k)
                for k in range(PER):
                    body(0, k, 0, PER)
                    prepare(k // NCH + 1, (k // NCH + 1) % SLOTS, k % NCH)
                with eng.Fori(1, TURNS) as i:
                    for k in range(PER):
                        body(i, k, -PER, PER)
                        prepare(i * SLOTS + k // NCH + 1, (k // NCH + 1) % SLOTS, k % NCH)
                for k in range(LAG + 1):
                    body(TURNS, k, -PER, 0)

            @block.gpsimd
            def _(pool):
                G.start(pool, "gpsimd")
                nc.gpsimd.memset(flatT[:, NB * P:NB * P + W], 0.0).then_inc(ready, 1)
                both_weights = ((w1, w1_parts), (w3, w3_parts))
                for j, (w, (hh, mm, lh)) in enumerate(both_weights):
                    pool.wait_ge(w_high, j + 1)
                    pool.tensor_tensor(w[:], w[:], hh[:], ALU.subtract).then_inc(w_rest, 1)
                for j, (w, (hh, mm, lh)) in enumerate(both_weights):
                    pool.wait_ge(w_mid, j + 1)
                    pool.wait_ge(w_rest, j + 1)
                    pool.tensor_tensor(lh[0:D, :], w[0:D, :], mm[0:D, :], ALU.subtract).then_inc(ready, 1)
                pool.wait_ge(ready, READY)

                def prepare(n, s, k):
                    if k == 1:
                        pool.wait_ge(G["high_kept"], G.now(n))
                        pool.wait_ge(G["low_made"], G.before(n))
                        pool.tensor_tensor(x_rest[D:P, :], flatT[D:P, bass.ds(n * W, W)], x_hm[s][D:P, :],
                                           ALU.subtract).then_inc(G["rest_made"], 1)
                    if k == 3:
                        pool.wait_ge(G["mid_kept"], G.now(n))
                        pool.tensor_tensor(x_hl[s][D:P, :], x_rest[D:P, :], x_hm[s][D:P, :], ALU.subtract)\
                            .then_inc(G["low_made"], 1)

                pipeline(pool, lambda i, k, lo, hi: None, prepare)

            @block.tensor
            def _(pe):
                S.start(pe, "tensor")
                G.start(pe, "tensor")
                pe.wait_ge(ready, READY)

                def prepare(n, s, k):
                    if k == 6:
                        pe.wait_ge(G["w_staged"], G.now(n))
                        pe.wait_ge(G["wT_kept"], G.before(n))
                        for b in range(GB):
                            last = nc.tensor.transpose(bt[0:PARTS * NE, b * P:(b + 1) * P], wnow[s][:, b, :],
                                                       ident[:])
                        last.then_inc(G["w_turned"], 1)

                def product(out, parts, cols, s):
                    for j, (w, x) in enumerate(zip(parts, (x_hm[s], x_hm[s], x_hl[s]))):
                        last = nc.tensor.matmul(out[:], w[:, cols], x[:], start=(j == 0), stop=(j == 2))
                    return last

                def body(i, k, lo, hi):
                    q, u, n = i * PER + k, k % SLOTS, i * SLOTS + k // NCH
                    if lo <= k < hi:
                        c, s = k % NCH, k // NCH
                        cols = slice(c * P, (c + 1) * P)
                        if c == 0:
                            pe.wait_ge(G["low_made"], G.now(n))
                            pe.wait_ge(G["high2_kept"], G.now(n))
                            pe.wait_ge(G["wT_kept"], G.now(n))
                        pe.wait_ge(S["activated"], S.past(q))
                        product(b1[u], w1_parts, cols, s).then_inc(S["h1_made"], 1)
                        pe.wait_ge(S["multiplied"], S.past(q))
                        product(b3[u], w3_parts, cols, s).then_inc(S["h3_made"], 1)
                        pe.wait_ge(S["weighted"], S.past(q))
                        nc.tensor.matmul(bw[u][:], owner[:, cols], wT[s][:], start=True, stop=True)\
                            .then_inc(S["wb_made"], 1)
                    if lo <= k - LAG < hi:
                        c = (k - LAG) % NCH
                        if c == 0:
                            pe.wait_ge(G["h_made"], G.before(n))
                        pe.wait_ge(S["weighted"], S.ago(q, LAG))
                        for b in range(GB):
                            last = nc.tensor.matmul(bo[:, b * D:(b + 1) * D], hid[u][:, b * P:(b + 1) * P], w2[:, c, :],
                                                    start=(c == 0 and b == 0), stop=(c == NCH - 1 and b == GB - 1))
                        last.then_inc(S["summed"], 1)

                pipeline(pe, body, prepare)

            @block.scalar
            def _(act):
                S.start(act, "scalar")
                act.preload_act_table_set("natural_log_exp_and_others")
                G.start(act, "scalar")
                both_weights = ((w1, w1_parts), (w3, w3_parts))
                for j, (w, (hh, mm, lh)) in enumerate(both_weights):
                    act.wait_ge(w_scaled, j + 1)
                    nc.scalar.activation(hh[:], w[:], ACT.Copy).then_inc(w_high, 1)
                for j, (w, (hh, mm, lh)) in enumerate(both_weights):
                    act.wait_ge(w_rest, j + 1)
                    nc.scalar.activation(mm[:], w[:], ACT.Copy).then_inc(w_mid, 1)
                    act.wait_ge(w_high, j + 1)
                    nc.scalar.activation(lh[D:P, :], hh[D:P, :], ACT.Copy).then_inc(ready, 1)
                act.wait_ge(shifted, 1)
                nc.scalar.activation(ex[:], ex[:], ACT.Exp).then_inc(exped, 1)
                act.preload_act_table_set("silu_and_others")
                act.wait_ge(ready, READY)
                act.wait_ge(route, ROUTE)

                def prepare(n, s, k):
                    x = flatT[:, bass.ds(n * W, W)]
                    if k == 1:
                        if not isinstance(n, int) or n >= SLOTS:
                            act.wait_ge(S["wb_made"], S.now(n * NCH - NCH - 1))
                        nc.scalar.activation(x_hm[s][:], x, ACT.Copy).then_inc(G["high_kept"], 1)
                    if k == 2:
                        nc.scalar.activation(x_hl[s][0:D, :], flatT[0:D, bass.ds(n * W, W)], ACT.Copy)\
                            .then_inc(G["high2_kept"], 1)
                    if k == 3:
                        act.wait_ge(G["rest_made"], G.now(n))
                        nc.scalar.activation(x_hm[s][D:P, :], x_rest[D:P, :], ACT.Copy).then_inc(G["mid_kept"], 1)
                    if k == 4:
                        act.wait_ge(G["w_turned"], G.past(n))
                        nc.scalar.activation(wnow[s][:], wts[:, bass.ds(n * GB, GB)].rearrange("p b k e -> p b (k e)"),
                                             ACT.Copy).then_inc(G["w_staged"], 1)
                    if k == 7:
                        act.wait_ge(G["w_turned"], G.now(n))
                        nc.scalar.activation(wT[s][:], bt[0:PARTS * NE, :], ACT.Copy).then_inc(G["wT_kept"], 1)

                def body(i, k, lo, hi):
                    q, u = i * PER + k, k % SLOTS
                    if lo <= k < hi:
                        act.wait_ge(S["h1_made"], S.now(q))
                        act.wait_ge(S["multiplied"], S.past(q))
                        nc.scalar.activation(act1[u][:], b1[u][:], ACT.Silu).then_inc(S["activated"], 1)

                pipeline(act, body, prepare)

            @block.vector
            def _(dve):
                S.start(dve, "vector")
                G.start(dve, "vector")
                nc.vector.memset(wts[:, NB:NB + GB], 0.0).then_inc(ready, 1)
                dve.wait_ge(loaded, 16 * LOADS)
                for w in (w1, w3):
                    nc.vector.tensor_scalar(w[:], w[:], ln2[:, 0:1], None, ALU.mult).then_inc(w_scaled, 1)
                nc.vector.tensor_copy(owner[:], owner_f[:]).then_inc(ready, 1)
                steps = [0]

                def step(ins):
                    steps[0] += 1
                    ins.then_inc(route, 1)
                    dve.wait_ge(route, steps[0])

                ranks = rank[:, None, :].to_broadcast([P, NB, NE])
                step(nc.vector.tensor_reduce(top[:], logits[:], AX, ALU.max))
                nc.vector.tensor_tensor(ex[:], logits[:], over(top[:], NE), ALU.subtract).then_inc(shifted, 1)
                step(nc.vector.tensor_tensor(tie[:], logits[:], over(top[:], NE), ALU.is_equal))
                step(nc.vector.tensor_tensor(tie[:], tie[:], ranks, ALU.mult))
                step(nc.vector.tensor_reduce(top[:], tie[:], AX, ALU.max))
                step(nc.vector.tensor_tensor(both[:], tie[:], over(top[:], NE), ALU.is_equal))
                step(nc.vector.scalar_tensor_tensor(pick[:], both[:], -1e30, logits[:], ALU.mult, ALU.add))
                step(nc.vector.tensor_reduce(top[:], pick[:], AX, ALU.max))
                step(nc.vector.tensor_tensor(tie[:], pick[:], over(top[:], NE), ALU.is_equal))
                step(nc.vector.tensor_tensor(tie[:], tie[:], ranks, ALU.mult))
                step(nc.vector.tensor_reduce(top[:], tie[:], AX, ALU.max))
                step(nc.vector.tensor_tensor(pick[:], tie[:], over(top[:], NE), ALU.is_equal))
                step(nc.vector.tensor_tensor(both[:], both[:], pick[:], ALU.add))
                dve.wait_ge(exped, 1)
                step(nc.vector.tensor_reduce(total[:], ex[:], AX, ALU.add))
                step(nc.vector.tensor_tensor(ex[:], ex[:], both[:], ALU.mult))
                step(nc.vector.tensor_reduce(top[:], ex[:], AX, ALU.add))
                step(nc.vector.scalar_tensor_tensor(top[:], total[:], 1e-9, top[:], ALU.mult, ALU.add))
                step(nc.vector.reciprocal(top[:], top[:]))
                step(nc.vector.tensor_tensor(ex[:], ex[:], over(top[:], NE), ALU.mult))
                for k in range(PARTS):
                    step(nc.vector.tensor_copy(low[:], ex[:]))
                    if k < PARTS - 1:
                        step(nc.vector.tensor_tensor(ex[:], ex[:], low[:], ALU.subtract))
                    copied = nc.vector.tensor_copy(wts[:, 0:NB, k, :], low[:])
                    if k < PARTS - 1:
                        copied.then_inc(parted, 1)
                        dve.wait_ge(parted, 1 + k)
                    else:
                        step(copied)
                assert steps[0] == ROUTE

                def body(i, k, lo, hi):
                    q, u, n = i * PER + k, k % SLOTS, i * SLOTS + k // NCH
                    if k % NCH == LAG and lo <= k - LAG - 1 < hi:
                        dve.wait_ge(S["summed"], S.ago(q, LAG + 1))
                        hs = H[:, bass.ds(n * GB - GB, GB), :]
                        nc.vector.tensor_tensor(hs, grouped(bo[:, 0:GB * D], D), hs, ALU.add).then_inc(G["h_made"], 1)
                    if lo <= k < hi:
                        dve.wait_ge(S["h3_made"], S.now(q))
                        dve.wait_ge(S["activated"], S.now(q))
                        dve.wait_ge(S["weighted"], S.past(q))
                        nc.vector.tensor_tensor(prod[u][:], b3[u][:], act1[u][:], ALU.mult).then_inc(S["multiplied"], 1)
                    if lo <= k - 1 < hi:
                        v = (k - 1) % SLOTS
                        dve.wait_ge(S["wb_made"], S.before(q))
                        dve.wait_ge(S["multiplied"], S.before(q))
                        dve.wait_ge(S["summed"], S.ago(q, 1 + SLOTS))
                        nc.vector.tensor_tensor(hid[v][:], bw[v][:], prod[v][:], ALU.mult).then_inc(S["weighted"], 1)

                pipeline(dve, body, lambda n, s, k: None)
        m.clear_semaphores()


def phase_decay_attention(nc, dram, H, ident, NB):
    HD = 8
    NH = 8
    STRIP = 32
    QUAD = P // STRIP
    TAPS = dram["d_conv"].shape[1]
    PADT = TAPS - 1
    KX = D + 1
    GQ = NH
    NQ = NB // GB * GQ
    SLOTS = 4
    TURN = 2 * GQ
    AGAIN = (4, 6, 6, 3, 3, 3, 3, 6)
    LAG_SCAN, LAG_DECAY, LAG_WEIGH, LAG_EXP2, LAG_TURN, LAG_PV, LAG_KEEP, LAG_Y = 1, 2, 3, 4, 5, 6, 7, 8
    with ExitStack() as ctx:
        m = Mem(nc, ctx)
        conv = m.sb("d_conv", [KX, TAPS, D])
        beta = m.sb("d_beta", [KX, D])
        keep = m.sb("d_keep", [KX, D])
        diag = m.sb("d_diag", [D, D])
        NW = 4 * P + D
        win = m.sb("d_win", [KX, NW])
        lnw = m.sb("d_lnw", [KX, 1])
        lnb = m.sb("d_lnb", [D, KX])
        wout = m.sb("d_wout", [KX, D])
        gam = m.sb("d_gam", [P, NH])
        gab = m.sb("d_gab", [P, NH])
        minus_g = m.sb("d_minus_g", [P, NH])
        pos = m.sb("d_pos", [P, W])
        cont = m.sb("d_cont", [P, W])
        hide_f = m.sb("d_hide_f", [P, P])
        hide = m.sb("d_hide", [P, P], BF16)
        ident_b = m.sb("d_ident_b", [P, P], BF16)
        notfirst = m.sb("d_notfirst", [P, 1])

        st, mv, rstd = m.sb("d_st", [P, GB, 6]), m.sb("d_mv", [P, GB, 2]), m.sb("d_rstd", [P, GB])
        st2, mv2, rstd2 = m.sb("d_st2", [P, GB, 6]), m.sb("d_mv2", [P, GB, 2]), m.sb("d_rstd2", [P, GB])
        xn, hn = m.sb("d_xn", [P, GB, D]), m.sb("d_hn", [P, GB, D])
        xT = m.sb("d_xT", [KX, GB, PADT + P])
        hT, hTr = m.sb("d_hT", [KX, W]), m.sb("d_hTr", [KX, W])
        qT = [m.sb(f"d_qT{s}", [P, 2, W]) for s in range(2)]
        kT = [m.sb(f"d_kT{s}", [P, 2, W]) for s in range(2)]
        v = [m.sb(f"d_v{s}", [P, GB, NH, STRIP]) for s in range(2)]
        attT = m.sb("d_attT", [P, W])
        y = [m.sb(f"d_y{s}", [P, GB, D]) for s in range(2)]
        yT = m.sb("d_yT", [KX, W])

        def slots(name, shape):
            return [m.sb(f"{name}{u}", shape) for u in range(SLOTS)]

        mx, mx2 = slots("d_mx", [P, GB]), slots("d_mx2", [P, GB])
        ex, later, decay = slots("d_ex", [P, W]), slots("d_later", [P, 1 + W]), slots("d_decay", [P, W])
        p2, pT = slots("d_p2", [P, W]), slots("d_pT", [P, W])
        rtot, inv = slots("d_rtot", [P, GB]), m.sb("d_inv", [P, GB, QUAD])
        bS = [m.ps(f"d_S{u}", [P, 512]) for u in range(SLOTS)]
        bT = m.ps("d_T", [P, 512])
        bO = m.ps("d_O", [P, 512])
        bX0, bX1 = m.ps("d_X0", [P, 512]), m.ps("d_X1", [P, 512])

        passed = m.sem("d_passed")
        loaded, ready, fold, folded = m.sem("d_loaded"), m.sem("d_ready"), m.sem("d_fold"), m.sem("d_folded")
        chain, gchain = m.sem("d_chain"), m.sem("d_gchain")
        S = Signals(m, "d", SLOTS, tensor="scored turned attended",
                    scalar="exped log_done root_done decay_made exped2 pT_kept",
                    vector="max_made shifted scanned inv_total weighed max2_made",
                    gpsimd="placed scaled shifted2")
        Q = Signals(m, "dq", 2, tensor="back", scalar="attT_kept", vector="inv_sum y_made")
        G = Signals(m, "dg", 3, tensor="x_turned filtered h_turned k_made*2 q_made*2 v_made y_turned out_made",
                    scalar="log_var rstd_made xT_kept log_var2 rstd2_made hT_kept q_kept*2 k_kept*2 v_kept yT_kept",
                    vector="stats moments centred stats2 moments2 centred2 h_made", gpsimd="hTr_kept")
        LOADS, READY = 12, 19
        TURNS = NQ // TURN
        assert NQ % TURN == 0

        def quad_of(i, k, lag):
            return i * (TURN // QUAD) + (k - lag - QUAD + 1) // QUAD

        def group_of(i, k, lag=0):
            return i * 2 + (k - lag) // GQ

        def on_back(k, lo, hi):
            return lo <= k - LAG_KEEP < hi and (k - LAG_KEEP) % QUAD == QUAD - 1

        class Beside:
            def norm(self, n, j): pass
            def filter(self, n, j): pass
            def project(self, n, s, j): pass
            def close(self, n, s, j): pass
            def finish(self, n, s, j): pass

        def beside(i, k, work):
            j, n, s = k % GQ, group_of(i, k), (k // GQ) % 2
            over_ = isinstance(i, int) and i == TURNS
            if not over_:
                work.norm(n + 3, j)
                work.filter(n + 2, j)
                work.project(n + 1, 1 - s, j)
            if not (over_ and k >= GQ):
                work.close(n, s, j)
            if not (isinstance(n, int) and n < 2):
                work.finish(n - 2, s, j)

        def pipeline(body, eng, work):
            for m_ in range(-3, 0):
                for j in range(GQ):
                    work.norm(m_ + 3, j)
                    if m_ >= -2:
                        work.filter(m_ + 2, j)
                    if m_ >= -1:
                        work.project(m_ + 1, 0, j)
            for k in range(TURN):
                body(0, k, 0, TURN)
            if TURNS > 1:
                with eng.Fori(1, TURNS) as i:
                    for k in range(TURN):
                        body(i, k, -TURN, TURN)
            for k in range(GQ + 3):
                body(TURNS, k, -TURN, 0)

        with nc.Block() as block:
            @block.sync
            def _(sp):
                for dst, name in ((conv, "d_conv"), (beta, "d_beta"), (win, "d_win"), (lnw, "d_lnw"), (lnb, "d_lnb"),
                                  (wout, "d_wout"), (gam, "d_gam"), (pos, "d_pos"), (cont, "d_cont"),
                                  (hide_f, "d_hide"), (notfirst, "d_notfirst"), (diag, "ident64")):
                    sp.dma_start(dst[:], dram[name]).then_inc(loaded, 16)

            @block.gpsimd
            def _(pool):
                S.start(pool, "gpsimd")
                G.start(pool, "gpsimd")
                pool.wait_ge(ready, READY)

                class Work(Beside):
                    def project(self, n, s, j):
                        if j == 2:
                            pool.wait_ge(G["hT_kept"], G.now(n))
                            pool.wait_ge(G["v_made"], G.before(n))
                            pool.sem_inc(passed, 1)
                            pool.tensor_copy(grouped(hTr[0:D, :], P), grouped(hT[0:D, :], P)[:, :, ::-1])\
                                .then_inc(G["hTr_kept"], 1)

                def body(i, k, lo, hi):
                    t = i * TURN + k

                    def unit(lag):
                        return lo <= k - lag < hi, t - lag, (k - lag) % SLOTS
                    on, q, u = unit(LAG_SCAN)
                    if on:
                        pool.wait_ge(S["scanned"], S.now(q))
                        pool.wait_ge(S["weighed"], S.past(q))
                        pool.tensor_tensor(decay[u][:], later[u][:, 0:W], pos[:], ALU.mult).then_inc(S["placed"], 1)
                        pool.wait_ge(S["inv_total"], S.now(q))
                        pool.wait_ge(S["placed"], S.now(q))
                        pool.tensor_tensor(grouped(decay[u][:], P), grouped(decay[u][:], P), over(rtot[u][:], P),
                                           ALU.mult).then_inc(S["scaled"], 1)
                    on, q, u = unit(LAG_WEIGH)
                    if on:
                        pool.wait_ge(S["max2_made"], S.now(q))
                        pool.tensor_tensor(grouped(p2[u][:], P), grouped(p2[u][:], P), over(mx2[u][:], P),
                                           ALU.subtract).then_inc(S["shifted2"], 1)
                    beside(i, k, work)

                work = Work()
                pipeline(body, pool, work)

            @block.tensor
            def _(pe):
                S.start(pe, "tensor")
                Q.start(pe, "tensor")
                G.start(pe, "tensor")
                pe.wait_ge(loaded, 16 * LOADS)
                nc.tensor.matmul(bX0[0:KX, :], lnb[:], win[0:D, 0:4 * P], start=True, stop=True)
                nc.tensor.matmul(bT[0:KX, 0:D], lnb[:], win[0:D, 4 * P:NW], start=True, stop=True).then_inc(fold, 1)
                pe.wait_ge(ready, READY)
                pe.wait_ge(folded, 3)

                class Work(Beside):
                    def filter(self, n, j):
                        if j == 2:
                            pe.wait_ge(G["centred"], G.now(n))
                            pe.wait_ge(G["hT_kept"], G.before(n))
                            pe.sem_inc(passed, 1)
                            for b in range(GB):
                                last = nc.tensor.transpose(bX1[0:D, b * P:(b + 1) * P], xn[:, b, :], ident[:])
                            last.then_inc(G["x_turned"], 1)
                        if 3 <= j < 3 + GB:
                            b = j - 3
                            if b == 0:
                                pe.wait_ge(G["xT_kept"], G.now(n))
                            for tap in range(TAPS):
                                rows = KX if tap == TAPS - 1 else D
                                last = nc.tensor.matmul(bX1[:, b * D:(b + 1) * D], xT[0:rows, b, tap:tap + P],
                                                        conv[0:rows, tap, :], start=(tap == 0), stop=(tap == TAPS - 1))
                            if b == GB - 1:
                                last.then_inc(G["filtered"], 1)

                    def project(self, n, s, j):
                        if j == 1:
                            pe.wait_ge(G["centred2"], G.now(n))
                            pe.sem_inc(passed, 1)
                            for b in range(GB):
                                last = nc.tensor.transpose(bX1[0:D, b * P:(b + 1) * P], hn[:, b, :], ident[:])
                            last.then_inc(G["h_turned"], 1)
                        if j in (3, 5):
                            c = (j - 3) // 2
                            if c == 0:
                                pe.wait_ge(G["h_made"], G.now(n - 3))
                                pe.wait_ge(G["hT_kept"], G.now(n))
                            else:
                                pe.wait_ge(G["k_kept"][0], G.now(n))
                            nc.tensor.matmul(bX0[:], win[:, c * P:(c + 1) * P], hT[:], start=True, stop=True)\
                                .then_inc(G["q_made"][c], 1)
                        if j in (4, 6):
                            c = (j - 4) // 2
                            pe.wait_ge(G["hTr_kept"], G.now(n))
                            pe.wait_ge(G["q_kept"][c], G.now(n))
                            nc.tensor.matmul(bX0[:], win[:, (2 + c) * P:(3 + c) * P], hTr[:], start=True, stop=True)\
                                .then_inc(G["k_made"][c], 1)
                        if j == 7:
                            pe.wait_ge(G["k_kept"][1], G.now(n))
                            for b in range(GB):
                                last = nc.tensor.matmul(bX0[:, b * D:(b + 1) * D], hTr[:, b * P:(b + 1) * P],
                                                        win[:, 4 * P:NW], start=True, stop=True)
                            last.then_inc(G["v_made"], 1)

                    def finish(self, n, s, j):
                        if j == 0:
                            pe.wait_ge(Q["y_made"], Q.now(n * (GQ // QUAD) + GQ // QUAD - 1))
                            if isinstance(n, int) and n == NQ // GQ - 1:
                                pe.wait_ge(G["h_made"], G.before(n))
                            else:
                                pe.wait_ge(G["v_kept"], G.now(n + 2))
                            pe.sem_inc(passed, 1)
                            for b in range(GB):
                                last = nc.tensor.transpose(bX0[0:D, b * P:(b + 1) * P], y[s][:, b, :], ident[:])
                            last.then_inc(G["y_turned"], 1)
                        if j == 1:
                            pe.wait_ge(G["yT_kept"], G.now(n))
                            for b in range(GB):
                                last = nc.tensor.matmul(bX0[:, b * D:(b + 1) * D], yT[:, b * P:(b + 1) * P], wout[:],
                                                        start=True, stop=True)
                            last.then_inc(G["out_made"], 1)

                def body(i, k, lo, hi):
                    t = i * TURN + k

                    def unit(lag):
                        return lo <= k - lag < hi, t - lag, (k - lag) % SLOTS
                    on, q, u = unit(0)
                    if on:
                        s, c = (k // GQ) % 2, (k % GQ) // 4
                        r = slice(32 * u, 32 * u + HD)
                        if k % 4 == 0:
                            pe.wait_ge(G["q_kept"][c], G.now(group_of(i, k)))
                            pe.wait_ge(G["k_kept"][c], G.now(group_of(i, k)))
                        pe.wait_ge(S["weighed"], S.past(q))
                        for _ in range(AGAIN[k % GQ]):
                            nc.tensor.matmul(bS[u][:], ident_b[:], hide[:, None, :].to_broadcast([P, GB, P]),
                                             start=True, stop=True)
                        nc.tensor.matmul(bS[u][:], ident_b[:], hide[:, None, :].to_broadcast([P, GB, P]),
                                         start=True, stop=False)
                        for b in range(GB):
                            cols = slice(b * P, (b + 1) * P)
                            last = nc.tensor.matmul(bS[u][:, cols], qT[s][r, c, cols], kT[s][r, c, cols],
                                                    start=False, stop=(b == GB - 1))
                        last.then_inc(S["scored"], 1)
                    on, q, u = unit(LAG_TURN)
                    if on:
                        pe.wait_ge(S["exped2"], S.now(q))
                        pe.wait_ge(S["pT_kept"], S.before(q))
                        if on_back(k - 1, lo, hi):
                            pe.wait_ge(Q["y_made"], Q.now(quad_of(i, k - 1, LAG_KEEP)))
                        for b in range(GB):
                            cols = slice(b * P, (b + 1) * P)
                            last = nc.tensor.transpose(bT[:, cols], p2[u][:, cols], ident[:])
                        last.then_inc(S["turned"], 1)
                    on, q, u = unit(LAG_PV)
                    if on:
                        j = k - LAG_PV
                        s, h = (j // GQ) % 2, j % GQ
                        if h == 0:
                            pe.wait_ge(G["v_kept"], G.now(group_of(i, k, LAG_PV)))
                        if h % QUAD == 0:
                            pe.wait_ge(Q["attT_kept"], Q.before(quad_of(i, k + QUAD - 1, LAG_PV)))
                        pe.wait_ge(S["pT_kept"], S.now(q))
                        r = slice(h % QUAD * STRIP, (h % QUAD + 1) * STRIP)
                        for b in range(GB):
                            last = nc.tensor.matmul(bO[r, b * P:(b + 1) * P], v[s][:, b, h, :],
                                                    pT[u][:, b * P:(b + 1) * P], start=True, stop=True)
                        last.then_inc(S["attended"], 1)
                    beside(i, k, work)
                    if on_back(k, lo, hi):
                        n = quad_of(i, k, LAG_KEEP)
                        pe.wait_ge(Q["attT_kept"], Q.now(n))
                        on, q, _ = unit(LAG_TURN)
                        if on:
                            pe.wait_ge(S["pT_kept"], S.now(q))
                        for b in range(GB):
                            cols = slice(b * P, (b + 1) * P)
                            last = nc.tensor.transpose(bT[:, cols], attT[:, cols], ident[:])
                        last.then_inc(Q["back"], 1)

                work = Work()
                pipeline(body, pe, work)

            @block.scalar
            def _(act):
                S.start(act, "scalar")
                Q.start(act, "scalar")
                act.preload_act_table_set("natural_log_exp_and_others")
                G.start(act, "scalar")
                act.wait_ge(loaded, 16 * LOADS)
                act.wait_ge(gchain, 2)
                nc.scalar.activation(gab[:], gab[:], ACT.Exp, scale=-1.0).then_inc(gchain, 1)
                act.wait_ge(gchain, 3)
                nc.scalar.activation(gab[:], gab[:], ACT.Ln, bias=1.0).then_inc(gchain, 1)
                act.wait_ge(ready, READY)
                act.wait_ge(folded, 2)
                nc.scalar.activation(win[:, 0:2 * P], win[:, 0:2 * P], ACT.Copy, scale=HD ** -0.5).then_inc(folded, 1)

                class Copies(Beside):
                    def filter(self, n, j):
                        if j == 3:
                            act.wait_ge(G["x_turned"], G.now(n))
                            act.wait_ge(G["filtered"], G.before(n))
                            nc.scalar.activation(xT[0:D, :, PADT:], grouped(bX1[0:D, :], P), ACT.Copy)\
                                .then_inc(G["xT_kept"], 1)

                    def project(self, n, s, j):
                        if j == 2:
                            act.wait_ge(G["h_turned"], G.now(n))
                            act.wait_ge(G["q_made"][1], G.before(n))
                            act.wait_ge(G["hTr_kept"], G.before(n))
                            nc.scalar.activation(hT[0:D, :], bX1[0:D, :], ACT.Copy).then_inc(G["hT_kept"], 1)
                        if j in (4, 6):
                            c = (j - 4) // 2
                            act.wait_ge(G["q_made"][c], G.now(n))
                            nc.scalar.activation(qT[s][:, c, :], bX0[:], ACT.Copy).then_inc(G["q_kept"][c], 1)
                        if j in (5, 7):
                            c = (j - 5) // 2
                            act.wait_ge(G["k_made"][c], G.now(n))
                            nc.scalar.activation(kT[s][:, c, :], bX0[:], ACT.Copy).then_inc(G["k_kept"][c], 1)

                    def close(self, n, s, j):
                        if j == 0:
                            act.wait_ge(G["v_made"], G.now(n))
                            nc.scalar.activation(v[s][:].rearrange("p b h e -> p (b h) e")[:, :, 0:HD],
                                                 grouped(bX0[:, 0:GB * D], HD), ACT.Copy).then_inc(G["v_kept"], 1)

                    def finish(self, n, s, j):
                        if j == 1:
                            act.wait_ge(G["y_turned"], G.now(n))
                            act.wait_ge(G["out_made"], G.before(n))
                            nc.scalar.activation(yT[0:D, :], bX0[0:D, :], ACT.Copy).then_inc(G["yT_kept"], 1)

                class Rates(Beside):
                    def norm(self, n, j):
                        if j == 4:
                            act.wait_ge(G["moments"], G.now(n))
                            act.wait_ge(G["centred"], G.before(n))
                            nc.scalar.activation(rstd[:], mv[:, :, 1], ACT.Ln, bias=1e-5).then_inc(G["log_var"], 1)
                            act.wait_ge(G["log_var"], G.now(n))
                            nc.scalar.activation(rstd[:], rstd[:], ACT.Exp, scale=-0.5).then_inc(G["rstd_made"], 1)

                    def filter(self, n, j):
                        if j == 7:
                            act.wait_ge(G["moments2"], G.now(n))
                            act.wait_ge(G["centred2"], G.before(n))
                            nc.scalar.activation(rstd2[:], mv2[:, :, 1], ACT.Ln, bias=1e-12).then_inc(G["log_var2"], 1)
                            act.wait_ge(G["log_var2"], G.now(n))
                            nc.scalar.activation(rstd2[:], rstd2[:], ACT.Exp, scale=-0.5).then_inc(G["rstd2_made"], 1)

                class Both(Beside):
                    def norm(self, n, j):
                        rates.norm(n, j)

                    def filter(self, n, j):
                        copies.filter(n, j)
                        rates.filter(n, j)

                    def project(self, n, s, j):
                        copies.project(n, s, j)

                def body(i, k, lo, hi):
                    t = i * TURN + k

                    def unit(lag):
                        return lo <= k - lag < hi, t - lag, (k - lag) % SLOTS
                    if on_back(k, lo, hi):
                        n = quad_of(i, k, LAG_KEEP)
                        act.wait_ge(S["attended"], S.now(i * TURN + k - LAG_KEEP))
                        act.wait_ge(Q["back"], Q.before(n))
                        nc.scalar.activation(attT[:], bO[:], ACT.Copy).then_inc(Q["attT_kept"], 1)
                    beside(i, k, copies)
                    on, q, u = unit(LAG_DECAY)
                    if on:
                        act.wait_ge(S["scaled"], S.now(q))
                        nc.scalar.activation(decay[u][:], decay[u][:], ACT.Ln, bias=1e-18).then_inc(S["log_done"], 1)
                    on2, q2, u2 = unit(LAG_EXP2)
                    if on2:
                        act.wait_ge(S["shifted2"], S.now(q2))
                        nc.scalar.activation(p2[u2][:], p2[u2][:], ACT.Exp).then_inc(S["exped2"], 1)
                    if on:
                        act.wait_ge(S["log_done"], S.now(q))
                        nc.scalar.activation(decay[u][:], decay[u][:], ACT.Exp, scale=0.5).then_inc(S["root_done"], 1)
                    on2, q2, u2 = unit(LAG_TURN)
                    if on2:
                        act.wait_ge(S["turned"], S.now(q2))
                        act.wait_ge(S["attended"], S.past(q2))
                        nc.scalar.activation(pT[u2][:], bT[:], ACT.Copy).then_inc(S["pT_kept"], 1)
                    if on:
                        h = (k - LAG_DECAY) % GQ
                        act.wait_ge(S["root_done"], S.now(q))
                        nc.scalar.activation(decay[u][:], decay[u][:], ACT.Exp, scale=minus_g[:, h:h + 1])\
                            .then_inc(S["decay_made"], 1)
                    on, q, u = unit(0)
                    if on:
                        act.wait_ge(S["shifted"], S.now(q))
                        nc.scalar.activation(ex[u][:], ex[u][:], ACT.Exp).then_inc(S["exped"], 1)
                    beside(i, k, rates)

                copies, rates = Copies(), Rates()
                pipeline(body, act, Both())

            @block.vector
            def _(dve):
                S.start(dve, "vector")
                Q.start(dve, "vector")
                G.start(dve, "vector")
                dve.wait_ge(loaded, 16 * LOADS)
                steps = [0]

                def link(ins):
                    steps[0] += 1
                    ins.then_inc(chain, 1)
                    dve.wait_ge(chain, steps[0])

                nc.vector.tensor_scalar(gab[:], gam[:], -1.0, None, ALU.mult).then_inc(gchain, 1)
                dve.wait_ge(gchain, 1)
                nc.vector.tensor_tensor(gab[:], gab[:], gam[:], ALU.max).then_inc(gchain, 1)
                link(nc.vector.tensor_tensor(beta[:], beta[:], beta[:], ALU.mult))
                link(nc.vector.tensor_scalar(keep[:], beta[:], -1.0, 1.0, ALU.mult, ALU.add))
                link(nc.vector.tensor_tensor(conv[:], conv[:], keep[:, None, :].to_broadcast([KX, TAPS, D]), ALU.mult))
                link(nc.vector.tensor_scalar(beta[:], beta[:], 1.0, None, ALU.add))
                link(nc.vector.tensor_tensor(diag[:], diag[:], beta[0:D, :], ALU.mult))
                link(nc.vector.tensor_tensor(conv[0:D, TAPS - 1, :], conv[0:D, TAPS - 1, :], diag[:], ALU.add))
                dve.wait_ge(fold, 1)
                nc.vector.scalar_tensor_tensor(win[:, 0:4 * P], win[:, 0:4 * P], lnw[:, 0:1], bX0[0:KX, :],
                                               ALU.mult, ALU.add).then_inc(folded, 1)
                nc.vector.scalar_tensor_tensor(win[:, 4 * P:NW], win[:, 4 * P:NW], lnw[:, 0:1], bT[0:KX, 0:D],
                                               ALU.mult, ALU.add).then_inc(folded, 1)
                dve.wait_ge(gchain, 4)
                link(nc.vector.tensor_scalar(gam[:], gam[:], 0.0, None, ALU.max))
                link(nc.vector.tensor_tensor(gam[:], gam[:], gab[:], ALU.add))
                nc.vector.tensor_scalar(minus_g[:], gam[:], -1.0, None, ALU.mult).then_inc(ready, 1)
                nc.vector.tensor_copy(hide[:], hide_f[:]).then_inc(ready, 1)
                nc.vector.tensor_copy(ident_b[:], ident[:]).then_inc(ready, 1)
                for u in range(SLOTS):
                    nc.vector.memset(later[u][:, 0:1], 0.0).then_inc(ready, 1)
                for s in range(2):
                    nc.vector.memset(v[s][:, :, :, HD:HD + 1], 1.0).then_inc(ready, 1)
                    nc.vector.memset(v[s][:, :, :, HD + 1:], 0.0).then_inc(ready, 1)
                nc.vector.memset(xT[0:D, :, 0:PADT], 0.0).then_inc(ready, 1)
                nc.vector.memset(xT[D:KX], 1.0).then_inc(ready, 1)
                for tile in (hT, hTr, yT):
                    nc.vector.memset(tile[D:KX, :], 1.0).then_inc(ready, 1)
                nc.vector.memset(H[:, NB:NB + 3 * GB, :], 0.0).then_inc(ready, 1)
                nc.vector.memset(rstd[:], 0.0).then_inc(ready, 1)
                nc.vector.memset(rstd2[:], 0.0).then_inc(ready, 1)
                dve.wait_ge(ready, READY)
                dve.wait_ge(folded, 3)

                class Work(Beside):
                    def norm(self, n, j):
                        if j == 3:
                            dve.wait_ge(G["centred"], G.before(n))
                            for b in range(GB):
                                last = nc.vector.bn_stats(
                                    st[:, b, :], H[:, bass.ds(n * GB + b, 1), :].rearrange("p b d -> p (b d)"))
                            last.then_inc(G["stats"], 1)
                            dve.wait_ge(G["stats"], G.now(n))
                            dve.sem_inc(passed, 1)
                            for b in range(GB):
                                last = nc.vector.bn_aggr(mv[:, b, :], st[:, b, :])
                            last.then_inc(G["moments"], 1)
                        if j == 5:
                            dve.wait_ge(G["rstd_made"], G.now(n))
                            dve.wait_ge(G["x_turned"], G.before(n))
                            for b in range(GB):
                                last = nc.vector.tensor_scalar(
                                    xn[:, b, :], H[:, bass.ds(n * GB + b, 1), :].rearrange("p b d -> p (b d)"),
                                    mv[:, b, 0:1], rstd[:, b:b + 1], ALU.subtract, ALU.mult)
                            last.then_inc(G["centred"], 1)

                    def filter(self, n, j):
                        if j == 7:
                            dve.wait_ge(G["filtered"], G.now(n))
                            dve.wait_ge(G["centred2"], G.before(n))
                            for b in range(GB):
                                last = nc.vector.bn_stats(st2[:, b, :], bX1[:, b * D:(b + 1) * D])
                            last.then_inc(G["stats2"], 1)
                            dve.wait_ge(G["stats2"], G.now(n))
                            dve.sem_inc(passed, 1)
                            for b in range(GB):
                                last = nc.vector.bn_aggr(mv2[:, b, :], st2[:, b, :])
                            last.then_inc(G["moments2"], 1)

                    def project(self, n, s, j):
                        if j == 0:
                            dve.wait_ge(G["rstd2_made"], G.now(n))
                            dve.wait_ge(G["h_turned"], G.before(n))
                            for b in range(GB):
                                last = nc.vector.tensor_scalar(hn[:, b, :], bX1[:, b * D:(b + 1) * D], mv2[:, b, 0:1],
                                                               rstd2[:, b:b + 1], ALU.subtract, ALU.mult)
                            last.then_inc(G["centred2"], 1)

                    def finish(self, n, s, j):
                        if j == 2:
                            dve.wait_ge(G["out_made"], G.now(n))
                            hs = H[:, bass.ds(n * GB, GB), :]
                            nc.vector.tensor_tensor(hs, grouped(bX0[:, 0:GB * D], D), hs, ALU.add)\
                                .then_inc(G["h_made"], 1)

                def body(i, k, lo, hi):
                    t = i * TURN + k

                    def unit(lag):
                        return lo <= k - lag < hi, t - lag, (k - lag) % SLOTS
                    on0, q0, u0 = unit(0)
                    on1, q1, u1 = unit(LAG_SCAN)
                    on3, q3, u3 = unit(LAG_WEIGH)
                    on_y = lo <= k - LAG_Y < hi and (k - LAG_Y) % QUAD == QUAD - 1
                    if on_y:
                        n, c, s = quad_of(i, k, LAG_Y), (k - LAG_Y) // QUAD % 2, (k - LAG_Y) // GQ % 2
                        sums = bT[:].rearrange("p (b h e) -> p b h e", h=QUAD, e=STRIP)
                        dve.wait_ge(Q["back"], Q.now(n))
                        nc.vector.reciprocal(inv[:], sums[:, :, :, HD]).then_inc(Q["inv_sum"], 1)
                        dve.wait_ge(Q["inv_sum"], Q.now(n))
                        if c == 0:
                            dve.wait_ge(G["y_turned"], G.ago(group_of(i, k, LAG_Y), 2))
                        half = y[s][:].rearrange("p b (c h e) -> p b c h e", c=2, h=QUAD)[:, :, c]
                        nc.vector.scalar_tensor_tensor(half, sums[:, :, :, 0:HD], notfirst[:, 0:1],
                                                       inv[:, :, :, None].to_broadcast([P, GB, QUAD, HD]),
                                                       ALU.mult, ALU.mult).then_inc(Q["y_made"], 1)
                    if on1:
                        dve.wait_ge(S["exped"], S.now(q1))
                        dve.wait_ge(S["placed"], S.past(q1))
                        nc.vector.tensor_tensor_scan(later[u1][:, 1:1 + W], cont[:], ex[u1][:], 0.0,
                                                     ALU.mult, ALU.add).then_inc(S["scanned"], 1)
                    if on1:
                        dve.wait_ge(S["scanned"], S.now(q1))
                        dve.wait_ge(S["scaled"], S.past(q1))
                        nc.vector.reciprocal(rtot[u1][:], grouped(later[u1][:, 1:1 + W], P)[:, :, P - 1])\
                            .then_inc(S["inv_total"], 1)
                    if on3:
                        dve.wait_ge(S["decay_made"], S.now(q3))
                        dve.wait_ge(S["turned"], S.past(q3))
                        nc.vector.scalar_tensor_tensor(p2[u3][:], decay[u3][:], 1e-5, bS[u3][:], ALU.max, ALU.mult)\
                            .then_inc(S["weighed"], 1)
                    if on0:
                        dve.wait_ge(S["scored"], S.now(q0))
                        nc.vector.tensor_reduce(mx[u0][:], grouped(bS[u0][:], P), AX, ALU.max).then_inc(S["max_made"], 1)
                    if on3:
                        dve.wait_ge(S["weighed"], S.now(q3))
                        dve.wait_ge(S["shifted2"], S.past(q3))
                        nc.vector.tensor_reduce(mx2[u3][:], grouped(p2[u3][:], P), AX, ALU.max)\
                            .then_inc(S["max2_made"], 1)
                    if on0:
                        dve.wait_ge(S["max_made"], S.now(q0))
                        dve.wait_ge(S["scanned"], S.past(q0))
                        nc.vector.tensor_tensor(grouped(ex[u0][:], P), grouped(bS[u0][:], P), over(mx[u0][:], P),
                                                ALU.subtract).then_inc(S["shifted"], 1)
                    beside(i, k, work)

                work = Work()
                pipeline(body, dve, work)
        m.clear_semaphores()


def phase_selected_mlp(nc, dram, out, H, ident, NB):
    HID = dram["g_w1"].shape[1]
    NC = HID // P
    TOPK = P // 2 - 1
    NG = NB // GB
    SLOTS = 2
    with ExitStack() as ctx:
        m = Mem(nc, ctx)
        w1, b1 = m.sb("g_w1", [D, HID]), m.sb("g_b1", [P, NC])
        w2, b2 = m.sb("g_w2", [P, NC, D]), m.sb("g_b2", [P, D])
        wr, br = m.sb("g_wr", [D, 1]), m.sb("g_br", [P, 1])
        xTall = m.sb("xTall", [D, NB * P])
        weight = m.sb("weight", [P, NB])
        gain = m.sb("gain", [P, NB])
        rows, left = m.sb("g_rows", [NB, P]), m.sb("g_left", [NB, P])
        top8 = m.sb("g_top8", [NB, 8])
        above, equal = m.sb("g_above", [NB, P]), m.sb("g_equal", [NB, P])
        upto, ones = m.sb("g_upto", [NB, P]), m.sb("g_ones", [NB, P])
        count = m.sb("g_count", [NB, 1])

        def slots(name, shape):
            return [m.sb(f"{name}{u}", shape) for u in range(SLOTS)]

        st, mv, rstd = slots("g_st", [P, GB, 6]), slots("g_mv", [P, GB, 2]), slots("g_rstd", [P, GB])
        x, xT = slots("g_x", [P, GB, D]), slots("g_xT", [D, W])
        hid = slots("g_hid", [P, NC, W])
        biased, scaled, res = slots("g_biased", [P, GB, D]), slots("g_scaled", [P, GB, D]), slots("g_res", [P, GB, D])
        bA = [m.ps(f"g_A{u}", [P, 512]) for u in range(SLOTS)]
        bB = [m.ps(f"g_B{u}", [P, 512]) for u in range(SLOTS)]
        bH = [[m.ps(f"g_H{u}{c}", [P, 512]) for c in range(NC)] for u in range(SLOTS)]

        passed = m.sem("g_passed")
        loaded, ready = m.sem("g_loaded"), m.sem("g_ready")
        turned, turned_back, chosen, select = m.sem("g_turned"), m.sem("g_turned_back"), m.sem("g_chosen"), m.sem("g_select")
        stored = [m.sem(f"g_stored{u}") for u in range(SLOTS)]
        S = Signals(m, "g", SLOTS, tensor="x_turned weighed", scalar="log_var rstd_made xT_kept weight_kept",
                    vector="stats moments centred", gpsimd="h_made xT_stored")
        M = Signals(m, "gm", SLOTS, tensor="hid_made*2 out_made", scalar="activated*2",
                    vector="bias_added gained result_made")
        LOADS = 6
        assert NC == 2 and 8 < TOPK

        with nc.Block() as block:
            @block.sync
            def _(sp):
                for dst, name in ((w1, "g_w1"), (b1, "g_b1"), (b2, "g_b2"), (wr, "g_wr"), (br, "g_br")):
                    sp.dma_start(dst[:], dram[name]).then_inc(loaded, 16)
                sp.dma_start(w2[:], dram["g_w2"].rearrange("(c p) n -> p c n", p=P)).then_inc(loaded, 16)
                for u in range(SLOTS):
                    sp.sem_inc(stored[u], 16)
                with sp.Fori(0, NG // SLOTS) as i:
                    for u in range(SLOTS):
                        n = i * SLOTS + u
                        sp.wait_ge(M["result_made"], M.now(n))
                        sp.dma_start(out[bass.ds(n * GB, GB)].rearrange("b t d -> t b d"), res[u][:])\
                            .then_inc(stored[u], 16)
                for u in range(SLOTS):
                    sp.wait_ge(stored[u], 16 * (NG // SLOTS + 1))

            @block.gpsimd
            def _(pool):
                S.start(pool, "gpsimd")
                with pool.Fori(0, NG // SLOTS) as i:
                    for u in range(SLOTS):
                        n = i * SLOTS + u
                        pool.wait_ge(S["centred"], S.now(n))
                        hs = H[:, bass.ds(n * GB, GB), :]
                        pool.tensor_tensor(hs, hs, x[u][:], ALU.add).then_inc(S["h_made"], 1)
                    for u in range(SLOTS):
                        n = i * SLOTS + u
                        pool.wait_ge(S["xT_kept"], S.now(n))
                        pool.sem_inc(passed, 1)
                        pool.tensor_copy(xTall[:, bass.ds(n * W, W)], xT[u][:]).then_inc(S["xT_stored"], 1)

            @block.tensor
            def _(pe):
                S.start(pe, "tensor")
                M.start(pe, "tensor")
                pe.wait_ge(loaded, 16 * LOADS)
                with pe.Fori(0, NG // SLOTS) as i:
                    for u in range(SLOTS):
                        n = i * SLOTS + u
                        pe.wait_ge(S["centred"], S.now(n))
                        pe.wait_ge(S["xT_kept"], S.past(n))
                        pe.sem_inc(passed, 1)
                        for b in range(GB):
                            last = nc.tensor.transpose(bA[u][0:D, b * P:(b + 1) * P], x[u][:, b, :], ident[:])
                        last.then_inc(S["x_turned"], 1)
                    for u in range(SLOTS):
                        n = i * SLOTS + u
                        pe.wait_ge(S["xT_kept"], S.now(n))
                        pe.wait_ge(S["weight_kept"], S.past(n))
                        for b in range(GB):
                            last = nc.tensor.matmul(bB[u][:, b:b + 1], xT[u][:, b * P:(b + 1) * P], wr[:],
                                                    start=True, stop=True)
                        last.then_inc(S["weighed"], 1)
                pe.wait_ge(S["weight_kept"], S.now(NG - 1))
                nc.tensor.transpose(bA[0][0:NB, 0:P], weight[:], ident[:]).then_inc(turned, 1)
                pe.wait_ge(chosen, 1)
                nc.tensor.transpose(bA[1][:, 0:NB], above[:], ident[0:NB, 0:NB]).then_inc(turned_back, 1)
                pe.wait_ge(S["xT_stored"], S.now(NG - 1))
                with pe.Fori(0, NG // SLOTS) as i:
                    for u in range(SLOTS):
                        n = i * SLOTS + u
                        for c in range(NC):
                            pe.wait_ge(M["activated"][c], M.past(n))
                            pe.sem_inc(passed, 1)
                            nc.tensor.matmul(bH[u][c][:], w1[:, c * P:(c + 1) * P], xTall[:, bass.ds(n * W, W)],
                                             start=True, stop=True).then_inc(M["hid_made"][c], 1)
                    for u in range(SLOTS):
                        n = i * SLOTS + u
                        pe.wait_ge(M["activated"][0], M.now(n))
                        pe.wait_ge(M["activated"][1], M.now(n))
                        pe.wait_ge(M["bias_added"], M.past(n))
                        for b in range(GB):
                            for c in range(NC):
                                last = nc.tensor.matmul(bB[u][:, b * D:(b + 1) * D], hid[u][:, c, b * P:(b + 1) * P],
                                                        w2[:, c, :], start=(c == 0), stop=(c == NC - 1))
                        last.then_inc(M["out_made"], 1)

            @block.scalar
            def _(act):
                S.start(act, "scalar")
                M.start(act, "scalar")
                act.preload_act_table_set("natural_log_exp_and_others")
                act.wait_ge(loaded, 16 * LOADS)
                with act.Fori(0, NG // SLOTS) as i:
                    for u in range(SLOTS):
                        n = i * SLOTS + u
                        act.wait_ge(S["moments"], S.now(n))
                        act.wait_ge(S["centred"], S.past(n))
                        nc.scalar.activation(rstd[u][:], mv[u][:, :, 1], ACT.Ln, bias=1e-5).then_inc(S["log_var"], 1)
                    for u in range(SLOTS):
                        n = i * SLOTS + u
                        act.wait_ge(S["log_var"], S.now(n))
                        nc.scalar.activation(rstd[u][:], rstd[u][:], ACT.Exp, scale=-0.5).then_inc(S["rstd_made"], 1)
                    for u in range(SLOTS):
                        n = i * SLOTS + u
                        act.wait_ge(S["x_turned"], S.now(n))
                        act.wait_ge(S["weighed"], S.past(n))
                        act.wait_ge(S["xT_stored"], S.past(n))
                        nc.scalar.activation(xT[u][:], bA[u][0:D, :], ACT.Copy).then_inc(S["xT_kept"], 1)
                    for u in range(SLOTS):
                        n = i * SLOTS + u
                        act.wait_ge(S["weighed"], S.now(n))
                        nc.scalar.activation(weight[:, bass.ds(n * GB, GB)], bB[u][:, 0:GB], ACT.Identity,
                                             bias=br[:, 0:1]).then_inc(S["weight_kept"], 1)
                act.preload_act_table_set("gelu_apprx_tanh_and_others")
                with act.Fori(0, NG // SLOTS) as i:
                    for u in range(SLOTS):
                        n = i * SLOTS + u
                        for c in range(NC):
                            act.wait_ge(M["hid_made"][c], M.now(n))
                            act.wait_ge(M["out_made"], M.past(n))
                            nc.scalar.activation(hid[u][:, c, :], bH[u][c][:], ACT.Gelu_apprx_tanh, bias=b1[:, c:c + 1])\
                                .then_inc(M["activated"][c], 1)

            @block.vector
            def _(dve):
                S.start(dve, "vector")
                M.start(dve, "vector")
                nc.vector.memset(ones[:], 1.0).then_inc(ready, 1)
                with dve.Fori(0, NG // SLOTS) as i:
                    for u in range(SLOTS):
                        n = i * SLOTS + u
                        dve.wait_ge(S["moments"], S.past(n))
                        for b in range(GB):
                            last = nc.vector.bn_stats(
                                st[u][:, b, :], H[:, bass.ds(n * GB + b, 1), :].rearrange("p b d -> p (b d)"))
                        last.then_inc(S["stats"], 1)
                    for u in range(SLOTS):
                        n = i * SLOTS + u
                        dve.wait_ge(S["stats"], S.now(n))
                        dve.wait_ge(S["centred"], S.past(n))
                        dve.sem_inc(passed, 1)
                        for b in range(GB):
                            last = nc.vector.bn_aggr(mv[u][:, b, :], st[u][:, b, :])
                        last.then_inc(S["moments"], 1)
                    for u in range(SLOTS):
                        n = i * SLOTS + u
                        dve.wait_ge(S["rstd_made"], S.now(n))
                        dve.wait_ge(S["x_turned"], S.past(n))
                        dve.wait_ge(S["h_made"], S.past(n))
                        for b in range(GB):
                            last = nc.vector.tensor_scalar(
                                x[u][:, b, :], H[:, bass.ds(n * GB + b, 1), :].rearrange("p b d -> p (b d)"),
                                mv[u][:, b, 0:1], rstd[u][:, b:b + 1], ALU.subtract, ALU.mult)
                        last.then_inc(S["centred"], 1)
                steps = [0]

                def step(ins):
                    steps[0] += 1
                    ins.then_inc(select, 1)
                    dve.wait_ge(select, steps[0])

                dve.wait_ge(ready, 1)
                dve.wait_ge(turned, 1)
                step(nc.vector.tensor_copy(rows[:], bA[0][0:NB, 0:P]))
                step(nc.vector.tensor_copy(left[:], rows[:]))
                for r in range((TOPK - 1) // 8):
                    step(nc.vector.max(top8[:], left[:]))
                    step(nc.vector.match_replace(left[:], top8[:], left[:], -3e38))
                step(nc.vector.max(top8[:], left[:]))
                nth = top8[:, (TOPK - 1) % 8:(TOPK - 1) % 8 + 1]
                step(nc.vector.tensor_scalar(above[:], rows[:], nth, None, ALU.is_gt))
                step(nc.vector.tensor_scalar(equal[:], rows[:], nth, None, ALU.is_equal))
                step(nc.vector.tensor_reduce(count[:], above[:], AX, ALU.add))
                step(nc.vector.tensor_scalar(count[:], count[:], -1.0, float(TOPK), ALU.mult, ALU.add))
                step(nc.vector.tensor_tensor_scan(upto[:], ones[:], equal[:], 0.0, ALU.mult, ALU.add))
                step(nc.vector.scalar_tensor_tensor(equal[:], upto[:], count[:, 0:1], equal[:], ALU.is_le, ALU.mult))
                step(nc.vector.tensor_tensor(above[:], above[:], equal[:], ALU.add))
                nc.vector.tensor_tensor(above[:], above[:], rows[:], ALU.mult).then_inc(chosen, 1)
                dve.wait_ge(turned_back, 1)
                step(nc.vector.tensor_copy(gain[:], bA[1][:, 0:NB]))
                dve.wait_ge(S["h_made"], S.now(NG - 1))
                with dve.Fori(0, NG // SLOTS) as i:
                    for u in range(SLOTS):
                        n = i * SLOTS + u
                        dve.wait_ge(M["out_made"], M.now(n))
                        dve.wait_ge(M["gained"], M.past(n))
                        nc.vector.tensor_tensor(biased[u][:], grouped(bB[u][:, 0:GB * D], D),
                                                b2[:, None, :].to_broadcast([P, GB, D]), ALU.add)\
                            .then_inc(M["bias_added"], 1)
                    for u in range(SLOTS):
                        n = i * SLOTS + u
                        dve.wait_ge(M["bias_added"], M.now(n))
                        dve.wait_ge(M["result_made"], M.past(n))
                        nc.vector.tensor_tensor(scaled[u][:], biased[u][:], over(gain[:, bass.ds(n * GB, GB)], D),
                                                ALU.mult).then_inc(M["gained"], 1)
                    for u in range(SLOTS):
                        n = i * SLOTS + u
                        dve.wait_ge(M["gained"], M.now(n))
                        dve.wait_ge(stored[u], (i + 1) * 16)
                        nc.vector.tensor_tensor(res[u][:], scaled[u][:], H[:, bass.ds(n * GB, GB), :], ALU.add)\
                            .then_inc(M["result_made"], 1)
        m.clear_semaphores()


def tower(nc, dram, out, NB):
    NE = dram["router"].shape[1]
    with ExitStack() as ctx:
        m = Mem(nc, ctx)
        H = m.sb("H", [P, NB + 3 * GB, D])
        ident = m.sb("ident", [P, P])
        const_loaded = m.sem("const_loaded")
        with nc.Block() as block:
            @block.sync
            def _(sp):
                sp.dma_start(ident[:], dram["ident"]).then_inc(const_loaded, 16)
                sp.wait_ge(const_loaded, 16)
        gathered = [m.sem(f"gathered{u}") for u in range(4)]
        phase_embed_attend(nc, dram, H, ident, gathered, NB)
        with ExitStack() as moe:
            m2 = Mem(nc, moe)
            flatT = m2.sb("flatT", [P, NB * P + W])
            logits = m2.sb("logits", [P, NB, NE])
            phase_block_attention(nc, dram, H, flatT, logits, ident, NB)
            phase_experts(nc, dram, H, flatT, logits, ident, NB)
        phase_decay_attention(nc, dram, H, ident, NB)
        phase_selected_mlp(nc, dram, out, H, ident, NB)


def lay_out(inputs):
    g = {k: np.asarray(v) for k, v in inputs.items()}
    a = {}
    col = lambda v: v[:, None]
    a["tokens"] = g["x"].T
    a["table"] = g["L0_tok_embed_table"]
    ws = [np.concatenate([g[f"L0_tok_W{k}"], g[f"L0_tok_b{k}"][None]], 0) for k in (1, 2)]
    a["tok_w"] = np.stack(ws)
    a["tok_wT"] = np.stack([w.T for w in ws])
    a["tok_wa"] = g["L0_tok_Wa"]
    a["tok_ba"] = np.tile(g["L0_tok_ba"][None], (P, 1))
    for c in "qkv":
        a[f"a0_{c}"] = np.concatenate([g[f"L0_attn_W{c}"], col(g[f"L0_attn_b{c}"])], 1)
    a["a0_woT"] = g["L0_attn_Wo"].T
    a["a0_bo"] = np.tile(g["L0_attn_bo"][None], (P, 1))
    a["a0_first"] = np.stack([a["a0_q"][0], a["a0_k"][0]], 1)
    a["ident"] = np.eye(P, dtype=np.float32)
    HD = 16
    turned = (np.arange(HD) + HD // 2) % HD
    wq = g["L0_ffn_wq"].reshape(4, HD, D)
    wk = g["L0_ffn_wk"].reshape(2, HD, D)[[0, 0, 1, 1]]
    a["f_wq"] = np.concatenate([wq, wq[:, turned]], 1).reshape(P, D).T
    a["f_wk"] = np.concatenate([wk, wk], 1).reshape(P, D).T
    a["f_wkp"] = np.concatenate([wk[:, turned]] * 2, 1).reshape(P, D).T
    a["f_wv"] = g["L0_ffn_wv"].T
    a["f_wo"] = g["L0_ffn_wo"].T
    a["f_ln1"] = col(g["L0_ffn_ln1_w"])
    a["f_ln2"] = col(g["L0_ffn_ln2_w"])
    a["router"] = g["L0_ffn_router_w"].T
    inv_freq = 1.0 / 10000.0 ** (np.arange(0, HD, 2, dtype=np.float32) / HD)
    ang = np.outer(np.arange(P, dtype=np.float32), inv_freq)
    ang = np.concatenate([ang, ang], -1)
    cos = np.cos(ang).T.astype(np.float32)
    sin = np.sin(ang).T.astype(np.float32) * np.where(np.arange(HD) < HD // 2, -1, 1)[:, None].astype(np.float32)
    a["rope_q"] = np.tile(np.concatenate([cos, sin]) * np.float32(HD ** -0.5), (4, 1))
    a["cos_k"] = np.tile(cos, (8, 1))
    a["sin_k"] = np.tile(sin, (8, 1))
    a["hide"] = np.where(np.tril(np.ones((P, P), bool)), 0.0, -1e30).astype(np.float32)
    NE, HID = g["L0_ffn_w1"].shape[:2]
    pad = -NE * HID % P
    for k in (1, 3):
        w = np.pad(g[f"L0_ffn_w{k}"].reshape(NE * HID, D), ((0, pad), (0, 0))).T
        a[f"e_w{k}"] = np.concatenate([w, w])
    a["e_ln2"] = np.concatenate([a["f_ln2"]] * 2)
    a["e_w2"] = np.pad(g["L0_ffn_w2"].transpose(0, 2, 1).reshape(NE * HID, D), ((0, pad), (0, 0)))
    owner = np.pad(np.repeat(np.eye(NE), HID, 1), ((0, 0), (0, pad)))
    a["owner"] = np.tile(owner, (3, 1)).astype(np.float32)
    a["rank"] = np.tile(np.arange(NE, 0, -1), (P, 1)).astype(np.float32)
    taps = g["L1_attn_conv_w"].transpose(1, 2, 0)
    bias = np.zeros((1,) + taps.shape[1:], np.float32)
    bias[0, -1] = g["L1_attn_conv_b"]
    a["d_conv"] = np.concatenate([taps, bias])
    a["d_beta"] = np.tile(g["L1_attn_sqrt_beta"].reshape(1, D), (D + 1, 1))

    def strips(w):
        w = w.reshape(w.shape[0], 8, 8)
        return np.pad(w, ((0, 0), (0, 0), (0, 24))).reshape(w.shape[0], 256)

    wqkv = [np.concatenate([g[f"L1_attn_{c}_w"].T, g[f"L1_attn_{c}_b"][None]]) for c in "qkv"]
    a["d_win"] = np.concatenate([strips(wqkv[0]), strips(wqkv[1]), wqkv[2]], 1)
    a["d_lnw"] = np.concatenate([g["L1_attn_ln_w"], np.ones(1, np.float32)])[:, None]
    a["d_lnb"] = np.concatenate([np.zeros((D, D), np.float32), col(g["L1_attn_ln_b"])], 1)
    a["d_wout"] = np.concatenate([g["L1_attn_out_w"].T, g["L1_attn_out_b"][None]])
    a["d_gam"] = np.tile(g["L1_attn_gammas"].reshape(1, 8), (P, 1))
    i, j = np.arange(P)[:, None], P - 1 - np.arange(P)[None]
    a["d_pos"] = np.tile(np.maximum(i - j, 0), (1, 4)).astype(np.float32)
    a["d_cont"] = np.tile((np.arange(W) % P != 0), (P, 1)).astype(np.float32)
    a["d_hide"] = np.where(j > i, -1e32, 0.0).astype(np.float32)
    a["d_notfirst"] = (i > 0).astype(np.float32)
    a["ident64"] = np.eye(D, dtype=np.float32)
    a["g_w1"] = g["L1_ffn_w1"]
    a["g_b1"] = g["L1_ffn_b1"].reshape(-1, P).T
    a["g_w2"] = g["L1_ffn_w2"]
    a["g_b2"] = np.tile(g["L1_ffn_b2"][None], (P, 1))
    a["g_wr"] = g["L1_ffn_wr"]
    a["g_br"] = np.tile(g["L1_ffn_br"][None], (P, 1))
    return {k: np.ascontiguousarray(v) for k, v in a.items()}


def kernel(**inputs):
    import concourse.bacc as _bacc
    from concourse.bass_utils import run_bass_kernel_spmd as _run

    nc = _bacc.Bacc("TRN2", target_bir_lowering=False, num_devices=1)
    laid = lay_out(inputs)
    NB = laid["tokens"].shape[1]
    arrays, dram = {}, {}
    for name, a in laid.items():
        arrays[f"in_{name}"] = a
        dram[name] = nc.dram_tensor(f"in_{name}", a.shape, mybir.dt.from_np(a.dtype), kind="ExternalInput").ap()
    out = nc.dram_tensor("out_h", (NB, P, D), F32, kind="ExternalOutput").ap()
    tower(nc, dram, out, NB)
    r = _run(nc, [arrays], core_ids=[0])
    return r.results[0]["out_h"]
```
